# Optimizing a Trainium2 kernel written in Bass

```python
import numpy as np
import jax
import jax.numpy as jnp

def _softmax(x, axis=-1):
    return jax.nn.softmax(x, axis=axis)

def _gelu(x):
    return jax.nn.gelu(x, approximate=True)

def _silu(x):
    return jax.nn.silu(x)

def _sigmoid(x):
    return jax.nn.sigmoid(x)

def _layernorm(x, axis=-1, eps=1e-05):
    m = jnp.mean(x, axis=axis, keepdims=True)
    v = jnp.var(x, axis=axis, keepdims=True)
    return (x - m) / jnp.sqrt(v + eps)

def _scatter_add(tgt, idx, src, axis=0):
    return tgt.at[idx].add(src)

def _segment_sum(src, seg, n):
    return jax.ops.segment_sum(src, seg, n)
kernel_name = 'mk_xattn_ffn_d2_seqx_r4_2d5f15'

def setup_inputs(seed: int=0):
    np.random.seed(seed)
    _w = jnp.asarray

    def _rec_inputs():
        import jax
        import jax.numpy as jnp
        _rk = jax.random.key(seed)
        x = -7.109e-05 + 0.9999 * jax.random.normal(jax.random.fold_in(_rk, 1), (8, 112, 1024), jnp.float32)
        _lenS = 112 - jax.random.randint(jax.random.fold_in(_rk, 7), (8,), 0, max(1, 112 // 4) + 1, jnp.int32)
        _lenS2 = 375 - jax.random.randint(jax.random.fold_in(_rk, 8), (8,), 0, max(1, 375 // 4) + 1, jnp.int32)
        _ctx_4096P = jax.random.normal(jax.random.fold_in(_rk, 11), (8, 16, 1024), jnp.float32)
        _ctx_4096c = jax.random.dirichlet(jax.random.fold_in(_rk, 511), 0.3 * jnp.ones((16,), jnp.float32), (8, 375))
        _ctx_4096t = jnp.einsum('bsk,bkd->bsd', _ctx_4096c, _ctx_4096P)
        _ctx_4096t = _ctx_4096t * jax.lax.rsqrt(jnp.mean(jnp.square(_ctx_4096t)) + 1e-12) * 0.953939
        ctx_4096 = -2.6191e-05 + 0.999952 * (_ctx_4096t + 0.3 * jax.random.normal(jax.random.fold_in(_rk, 611), (8, 375, 1024), jnp.float32))
        _validS = jnp.arange(112)[None, :] < _lenS[:, None]
        _validS2 = jnp.arange(375)[None, :] < _lenS2[:, None]
        _causal = jnp.tril(jnp.ones((112, 112), dtype=bool))
        mask_BxSxS2_ff0 = jnp.where(jnp.ones((8, 112, 375), dtype=bool), 0.0, -1000000000.0).astype(jnp.float32)
        return (x, ctx_4096, mask_BxSxS2_ff0)
    x, ctx_4096, mask_BxSxS2_ff0 = _rec_inputs()

    def _L0_xattn_setup():
        import jax, jax.numpy as jnp
        import numpy as np
        TEXT_DIM = 1024
        FEATURE_DIM = 1024

        def _xavier_uniform(key, shape):
            fan_in, fan_out = (shape[1], shape[0])
            limit = float(np.sqrt(6.0 / (fan_in + fan_out)))
            return jax.random.uniform(key, shape, jnp.float32, -limit, limit)
        key = jax.random.key(seed)
        k1, k2, k3, k4 = jax.random.split(key, 4)
        text = jax.random.normal(k1, (8, 512, TEXT_DIM), jnp.float32)
        features = jax.random.normal(k2, (8, 144, FEATURE_DIM), jnp.float32)
        Wq = _xavier_uniform(k3, (FEATURE_DIM, TEXT_DIM))
        bq = jnp.zeros((FEATURE_DIM,), jnp.float32)
        Wk = _xavier_uniform(k4, (FEATURE_DIM, FEATURE_DIM))
        bk = jnp.zeros((FEATURE_DIM,), jnp.float32)
        return {'text': text, 'features': features, 'Wq': Wq, 'bq': bq, 'Wk': Wk, 'bk': bk}
    _L0_xattn_all = _L0_xattn_setup()
    _L0_xattn_in = {k: v for k, v in _L0_xattn_all.items() if k in ('Wq', 'bq', 'Wk', 'bk')}
    del _L0_xattn_all

    def _L0_ffn_setup():
        import jax, jax.numpy as jnp
        import numpy as np
        LORA_R = 16
        SCALE = 16.0 / np.sqrt(16.0)
        NUM_EXPERTS = 4
        TOP_K = 2
        IN_F = 1024
        OUT_F = 1024
        key = jax.random.key(seed)
        k_x, k_a, k_b, k_r = jax.random.split(key, 4)
        x = jax.random.normal(k_x, (2, 512, IN_F), dtype=jnp.float32)
        A = jax.random.normal(k_a, (NUM_EXPERTS, LORA_R, IN_F), dtype=jnp.float32) * (1.0 / np.sqrt(IN_F))
        B = jax.random.normal(k_b, (NUM_EXPERTS, OUT_F, LORA_R), dtype=jnp.float32) * 0.02
        Wr = jax.random.normal(k_r, (NUM_EXPERTS, IN_F), dtype=jnp.float32) * 0.02
        return {'x': x, 'A': A, 'B': B, 'Wr': Wr}
    _L0_ffn_all = _L0_ffn_setup()
    _L0_ffn_in = {k: v for k, v in _L0_ffn_all.items() if k in ('A', 'B', 'Wr')}
    del _L0_ffn_all

    def _L1_xattn_setup():
        import jax, jax.numpy as jnp
        import numpy as np
        B, S, D = (4, 256, 1024)
        HQ, HKV, DK, DV = (32, 8, 128, 128)

        def apply_rope(x, positions):
            d = x.shape[-1]
            inv_freq = 1.0 / 10000.0 ** (jnp.arange(0, d, 2, dtype=jnp.float32) / d)
            ang = positions.astype(jnp.float32)[:, None] * inv_freq[None, :]
            cos = jnp.cos(ang)[None, None]
            sin = jnp.sin(ang)[None, None]
            x1, x2 = (x[..., :d // 2], x[..., d // 2:])
            return jnp.concatenate([x1 * cos - x2 * sin, x2 * cos + x1 * sin], axis=-1)
        key = jax.random.key(seed)
        ks = jax.random.split(key, 8)
        return {'query': jax.random.normal(ks[0], (B, S, D), jnp.float32), 'key': jax.random.normal(ks[1], (B, S, D), jnp.float32), 'value': jax.random.normal(ks[2], (B, S, D), jnp.float32), 'mask': jnp.zeros((B, S, S), jnp.float32), 'wq': jax.random.normal(ks[3], (D, HQ * DK), jnp.float32) * 0.02, 'wk': jax.random.normal(ks[4], (D, HKV * DK), jnp.float32) * 0.02, 'wv': jax.random.normal(ks[5], (D, HKV * DV), jnp.float32) * 0.02, 'wo': jax.random.normal(ks[6], (HQ * DV, D), jnp.float32) * 0.02, 'curr_seq_pos': 0}
    _L1_xattn_all = _L1_xattn_setup()
    _L1_xattn_in = {k: v for k, v in _L1_xattn_all.items() if k in ('wq', 'wk', 'wv', 'wo')}
    del _L1_xattn_all

    def _L1_ffn_setup():
        import jax, jax.numpy as jnp
        import numpy as np
        R = 16
        LORA_ALPHA = 16
        SCALING = LORA_ALPHA / R
        key = jax.random.key(seed)
        kx, kr, ka = jax.random.split(key, 3)
        B, S, D, DO, E = (4, 512, 1024, 1024, 8)
        x = jax.random.normal(kx, (B, S, D), dtype=jnp.float32)
        bound_r = 1.0 / np.sqrt(D)
        route_w = jax.random.uniform(kr, (E, D), jnp.float32, -bound_r, bound_r)
        bound_a = 1.0 / np.sqrt(D)
        A = jax.random.uniform(ka, (E, R, D), jnp.float32, -bound_a, bound_a)
        kb = jax.random.fold_in(key, 7)
        Bw = jax.random.normal(kb, (E, DO, R), dtype=jnp.float32) * 0.02
        return {'x': x, 'route_w': route_w, 'A': A, 'Bw': Bw}
    _L1_ffn_all = _L1_ffn_setup()
    _L1_ffn_in = {k: v for k, v in _L1_ffn_all.items() if k in ('route_w', 'A', 'Bw')}
    del _L1_ffn_all
    return {'x': x, 'ctx_4096': ctx_4096, 'mask_BxSxS2_ff0': mask_BxSxS2_ff0, 'L0_xattn_Wq': _L0_xattn_in['Wq'], 'L0_xattn_bq': _L0_xattn_in['bq'], 'L0_xattn_Wk': _L0_xattn_in['Wk'], 'L0_xattn_bk': _L0_xattn_in['bk'], 'L0_ffn_A': _L0_ffn_in['A'], 'L0_ffn_B': _L0_ffn_in['B'], 'L0_ffn_Wr': _L0_ffn_in['Wr'], 'L1_xattn_wq': _L1_xattn_in['wq'], 'L1_xattn_wk': _L1_xattn_in['wk'], 'L1_xattn_wv': _L1_xattn_in['wv'], 'L1_xattn_wo': _L1_xattn_in['wo'], 'L1_ffn_route_w': _L1_ffn_in['route_w'], 'L1_ffn_A': _L1_ffn_in['A'], 'L1_ffn_Bw': _L1_ffn_in['Bw']}

def reference(x, ctx_4096, mask_BxSxS2_ff0, L0_xattn_Wq, L0_xattn_bq, L0_xattn_Wk, L0_xattn_bk, L0_ffn_A, L0_ffn_B, L0_ffn_Wr, L1_xattn_wq, L1_xattn_wk, L1_xattn_wv, L1_xattn_wo, L1_ffn_route_w, L1_ffn_A, L1_ffn_Bw):
    import jax
    import jax.numpy as jnp

    def _L0_xattn_ref(text, features, Wq, bq, Wk, bk):
        import jax, jax.numpy as jnp
        import numpy as np
        TEXT_DIM = 1024
        FEATURE_DIM = 1024

        def _xavier_uniform(key, shape):
            fan_in, fan_out = (shape[1], shape[0])
            limit = float(np.sqrt(6.0 / (fan_in + fan_out)))
            return jax.random.uniform(key, shape, jnp.float32, -limit, limit)
        Q = jnp.einsum('btx,dx->btd', text, Wq) + bq
        K = jnp.einsum('bpx,dx->bpd', features, Wk) + bk
        scale = 1.0 / jnp.sqrt(jnp.asarray(K.shape[-1], K.dtype))
        scores = jnp.einsum('btd,bpd->btp', Q, K) * scale
        attn = jax.nn.softmax(scores, axis=-1)
        attended = jnp.einsum('btp,bpd->btd', attn, features)
        return attended

    def _L0_ffn_ref(x, A, B, Wr):
        import jax, jax.numpy as jnp
        import numpy as np
        LORA_R = 16
        SCALE = 16.0 / np.sqrt(16.0)
        NUM_EXPERTS = 4
        TOP_K = 2
        IN_F = 1024
        OUT_F = 1024
        orig_shape = x.shape
        flat = x.reshape(-1, orig_shape[-1])
        logits = flat @ Wr.T
        topk_vals, topk_idx = jax.lax.top_k(logits, TOP_K)
        T = flat.shape[0]
        neg_inf = jnp.finfo(logits.dtype).min
        sparse = jnp.full_like(logits, neg_inf)
        rows = jnp.arange(T)[:, None]
        sparse = sparse.at[rows, topk_idx].set(topk_vals)
        gates = jax.nn.softmax(sparse, axis=-1)
        mid = jnp.einsum('tf,erf->ter', flat, A)
        all_deltas = jnp.einsum('ter,eor->teo', mid, B) * SCALE
        delta = jnp.sum(gates[:, :, None] * all_deltas, axis=1)
        return delta.reshape(*orig_shape[:-1], -1)

    def _L1_xattn_ref(query, key, value, mask, wq, wk, wv, wo, curr_seq_pos):
        import jax, jax.numpy as jnp
        import numpy as np
        B, S, D = (4, 256, 1024)
        HQ, HKV, DK, DV = (32, 8, 128, 128)

        def apply_rope(x, positions):
            d = x.shape[-1]
            inv_freq = 1.0 / 10000.0 ** (jnp.arange(0, d, 2, dtype=jnp.float32) / d)
            ang = positions.astype(jnp.float32)[:, None] * inv_freq[None, :]
            cos = jnp.cos(ang)[None, None]
            sin = jnp.sin(ang)[None, None]
            x1, x2 = (x[..., :d // 2], x[..., d // 2:])
            return jnp.concatenate([x1 * cos - x2 * sin, x2 * cos + x1 * sin], axis=-1)
        bs, sq, _ = query.shape
        sk = key.shape[1]
        n_groups = HQ // HKV
        q = (query @ wq).reshape(bs, sq, HQ, DK).transpose(0, 2, 1, 3)
        k = (key @ wk).reshape(bs, sk, HKV, DK)
        v = (value @ wv).reshape(bs, sk, HKV, DV)
        k = jnp.repeat(k, n_groups, axis=2).transpose(0, 2, 1, 3)
        v = jnp.repeat(v, n_groups, axis=2).transpose(0, 2, 1, 3)
        scale = jnp.sqrt(jnp.float32(DK))
        pos = curr_seq_pos + jnp.arange(sq)
        q = apply_rope(q, pos)
        k = apply_rope(k, curr_seq_pos + jnp.arange(sk))
        scores = jnp.einsum('bhqd,bhkd->bhqk', q, k) / scale
        m = jax.lax.dynamic_slice(mask, (0, curr_seq_pos, 0), (bs, sq, sk))
        attn = jax.nn.softmax(scores + m[:, None, :, :], axis=-1)
        out = jnp.einsum('bhqk,bhkd->bhqd', attn, v)
        out = out.transpose(0, 2, 1, 3).reshape(bs, sq, HQ * DV)
        return out @ wo

    def _L1_ffn_ref(x, route_w, A, Bw):
        import jax, jax.numpy as jnp
        import numpy as np
        R = 16
        LORA_ALPHA = 16
        SCALING = LORA_ALPHA / R
        logits = jnp.einsum('bsd,ed->bse', x, route_w)
        topk_v, topk_idx = jax.lax.top_k(logits, 1)
        E = logits.shape[-1]
        route_weight = jax.nn.one_hot(topk_idx[..., 0], E, dtype=logits.dtype) * topk_v
        h = jnp.einsum('bsd,erd->bser', x, A)
        wh = route_weight[..., None] * h
        out = jnp.einsum('bser,eor->bso', wh, Bw) * SCALING
        return out
    x = x + _L0_xattn_ref(_layernorm(x, axis=-1), ctx_4096, L0_xattn_Wq, L0_xattn_bq, L0_xattn_Wk, L0_xattn_bk)
    x = x + _L0_ffn_ref(_layernorm(x, axis=-1), L0_ffn_A, L0_ffn_B, L0_ffn_Wr)
    x = x + _L1_xattn_ref(_layernorm(x, axis=-1), ctx_4096, ctx_4096, mask_BxSxS2_ff0, L1_xattn_wq, L1_xattn_wk, L1_xattn_wv, L1_xattn_wo, 0)
    x = x + _L1_ffn_ref(_layernorm(x, axis=-1), L1_ffn_route_w, L1_ffn_A, L1_ffn_Bw)
    return x

_drawn_inputs = setup_inputs


def setup_inputs(seed=0):
    import zlib

    import numpy as np

    out = dict(_drawn_inputs(seed))
    spreads = {'L0_xattn_bq': (0.0, 0.1), 'L0_xattn_bk': (0.0, 0.8)}
    factors = {}
    for name, (base, spread) in spreads.items():
        noise = np.random.default_rng([zlib.crc32(name.encode()), seed]).standard_normal(out[name].shape)
        drawn = base * np.exp(spread * noise) if base else spread * noise
        out[name] = jnp.asarray(drawn.astype(out[name].dtype))
    for name, factor in factors.items():
        out[name] = (out[name] * factor).astype(out[name].dtype)
    return out
```

```python
from contextlib import ExitStack

import concourse.bass as bass
from concourse import mybir

F32 = mybir.dt.float32
F32R = mybir.dt.float32r
ALU = mybir.AluOpType
ACT = mybir.ActivationFunctionType
AX = mybir.AxisListType.X

P = 128
BATCH, SEQ, DIM = 8, 112, 1024
KEYS = 375
KEYS_EVEN = 376
KEY_TILES, KEY_TILE = 3, 125
CH = DIM // P
TOK = BATCH * SEQ
HALF = TOK // 2
QUAD = HALF // SEQ
GROUPS, PER_GROUP = 8, 4
HEADS = GROUPS * PER_GROUP
L0_EXPERTS, L0_TOP = 4, 2
L1_EXPERTS, L1_TOP = 8, 1
RANK = 16
L0_SCALE = 4.0
EPS = 1e-5
LOWEST = -3.4028234663852886e38
PASSES = ((0, 0), (0, 1), (1, 0))


class Shared:
    pass


def f32(ap):
    return ap.bitcast(F32)


def take_waits(eng, passed):
    eng.sem_inc(passed, 1)


class NormSems:
    def __init__(self, sem, name):
        self.moments = sem(f"{name}_moments")
        self.rstd = sem(f"{name}_rstd")
        self.normed = sem(f"{name}_normed")
        self.turned = sem(f"{name}_turned")
        self.evacuated = sem(f"{name}_evac")


class NormBuffers:
    def __init__(self, sb, name, slots):
        self.stats = sb(f"{name}_stats", [SEQ, slots, 2, 6])
        self.mv = sb(f"{name}_mv", [SEQ, slots, 2])
        self.ve = sb(f"{name}_ve", [SEQ, slots])
        self.rstd = sb(f"{name}_rstd", [SEQ, slots])
        self.xn = sb(f"{name}_xn", [SEQ, slots, DIM])


def norm_moments(dve, s, buf, n, k, x, passed):
    for h in range(2):
        dve.bn_stats(buf.stats[:, k, h, :], x[:, h * 512:(h + 1) * 512]).then_inc(s.moments, 1)
    dve.wait_ge(s.moments, 4 * n + 2)
    take_waits(dve, passed)
    dve.bn_aggr(buf.mv[:, k, :], buf.stats[:, k]).then_inc(s.moments, 1)
    dve.wait_ge(s.moments, 4 * n + 3)
    dve.tensor_scalar(buf.ve[:, k:k + 1], buf.mv[:, k, 1:2], EPS, None, ALU.add).then_inc(s.moments, 1)


def norm_rstd(pool, s, buf, n, k, minus_half):
    pool.wait_ge(s.moments, 4 * n + 4)
    pool.tensor_tensor(buf.rstd[:, k:k + 1], buf.ve[:, k:k + 1], minus_half, ALU.pow).then_inc(s.rstd, 1)


def norm_apply(dve, s, buf, n, k, x):
    dve.wait_ge(s.rstd, n + 1)
    dve.tensor_scalar(buf.xn[:, k, :], x, buf.mv[:, k, 0:1], buf.rstd[:, k:k + 1],
                      ALU.subtract, ALU.mult).then_inc(s.normed, 1)


def norm_turn(pe, s, buf, n, k, banks, ident):
    pe.wait_ge(s.normed, n + 1)
    for j in range(2):
        for c in range(4):
            ch = 4 * j + c
            last = pe.transpose(banks[j][:, c * SEQ:(c + 1) * SEQ], buf.xn[:, k, ch * P:(ch + 1) * P],
                                ident[0:SEQ, 0:SEQ])
        last.then_inc(s.turned, 1)


class LoraSems:
    def __init__(self, sem, name):
        self.mid = sem(f"{name}_mid")
        self.chain = sem(f"{name}_chain")
        self.gate_exp = sem(f"{name}_gexp")
        self.gated = sem(f"{name}_gated")
        self.turned = sem(f"{name}_mturned")
        self.staged = sem(f"{name}_staged")
        self.up = sem(f"{name}_up")
        self.added = sem(f"{name}_added")


class LoraBuffers:
    def __init__(self, sb, name, experts):
        self.e = e = experts
        self.lg = sb(f"{name}_lg", [SEQ, e])
        self.gt = sb(f"{name}_gt", [SEQ, e, e])
        self.eq = sb(f"{name}_eq", [SEQ, e, e])
        self.rank = sb(f"{name}_rank", [SEQ, e])
        self.sel = sb(f"{name}_sel", [SEQ, e])
        self.nmax = sb(f"{name}_nmax", [SEQ, 1])
        self.ex = sb(f"{name}_ex", [SEQ, e])
        self.exs = sb(f"{name}_exs", [SEQ, e])
        self.tot = sb(f"{name}_tot", [SEQ, 1])
        self.inv = sb(f"{name}_inv", [SEQ, 1])
        self.gate = sb(f"{name}_gate", [SEQ, e])
        self.mw = sb(f"{name}_mw", [SEQ, e * RANK])
        self.mwt = sb(f"{name}_mwt", [e * RANK, SEQ])


def lora_gates(dve, s, buf, n, mid, tri, top, softmax):
    e = buf.e
    steps = 11 if softmax else 7
    base = steps * n
    first = e * RANK
    over = [SEQ, e, e]
    dve.wait_ge(s.mid, n + 1)
    dve.tensor_copy(buf.lg[:, :], mid[:, first:first + e]).then_inc(s.chain, 1)
    other = buf.lg[:, :].unsqueeze(1).broadcast_to(over)
    own = buf.lg[:, :].unsqueeze(2).broadcast_to(over)
    dve.wait_ge(s.chain, base + 1)
    dve.tensor_tensor(buf.gt[:, :, :], other, own, ALU.is_gt).then_inc(s.chain, 1)
    dve.tensor_tensor(buf.eq[:, :, :], other, own, ALU.is_equal).then_inc(s.chain, 1)
    dve.wait_ge(s.chain, base + 3)
    dve.tensor_tensor(buf.eq[:, :, :], buf.eq[:, :, :], tri, ALU.mult).then_inc(s.chain, 1)
    dve.wait_ge(s.chain, base + 4)
    dve.tensor_tensor(buf.gt[:, :, :], buf.gt[:, :, :], buf.eq[:, :, :], ALU.add).then_inc(s.chain, 1)
    dve.wait_ge(s.chain, base + 5)
    dve.tensor_reduce(buf.rank[:, :], buf.gt[:, :, :], AX, ALU.add).then_inc(s.chain, 1)
    dve.wait_ge(s.chain, base + 6)
    if softmax:
        dve.tensor_scalar(buf.sel[:, :], buf.rank[:, :], float(top), None, ALU.is_lt).then_inc(s.chain, 1)
        dve.tensor_reduce(buf.nmax[:, :], buf.lg[:, :], AX, ALU.max, negate=True).then_inc(s.chain, 1)
        dve.wait_ge(s.chain, base + 8)
        dve.wait_ge(s.gate_exp, n + 1)
        dve.tensor_tensor(buf.exs[:, :], buf.ex[:, :], buf.sel[:, :], ALU.mult).then_inc(s.chain, 1)
        dve.wait_ge(s.chain, base + 9)
        dve.tensor_reduce(buf.tot[:, :], buf.exs[:, :], AX, ALU.add).then_inc(s.chain, 1)
        dve.wait_ge(s.chain, base + 10)
        dve.reciprocal(buf.inv[:, :], buf.tot[:, :]).then_inc(s.chain, 1)
        dve.wait_ge(s.chain, base + 11)
        dve.tensor_scalar(buf.gate[:, :], buf.exs[:, :], buf.inv[:, 0:1], L0_SCALE,
                          ALU.mult, ALU.mult).then_inc(s.gated, 1)
    else:
        dve.tensor_scalar(buf.sel[:, :], buf.rank[:, :], float(top), None, ALU.is_lt).then_inc(s.chain, 1)
        dve.wait_ge(s.chain, base + 7)
        dve.tensor_tensor(buf.gate[:, :], buf.lg[:, :], buf.sel[:, :], ALU.mult).then_inc(s.gated, 1)
    dve.wait_ge(s.gated, 2 * n + 1)
    dve.tensor_tensor(buf.mw[:, :].rearrange("t (e r) -> t e r", e=e),
                      mid[:, 0:first].rearrange("t (e r) -> t e r", e=e),
                      buf.gate[:, :].unsqueeze(2).broadcast_to([SEQ, e, RANK]), ALU.mult).then_inc(s.gated, 1)


def lora_mid(pe, s, n, mid, xnt, aw):
    width = aw.shape[-1]
    for c in range(CH):
        last = pe.matmul(mid[:, 0:width], xnt[:, c, :], aw[:, c, :], start=(c == 0), stop=(c == CH - 1))
    last.then_inc(s.mid, 1)


def lora_turn(pe, s, buf, n, bank, ident, passed):
    pe.wait_ge(s.gated, 2 * n + 2)
    take_waits(pe, passed)
    pe.transpose(bank[0:buf.e * RANK, 0:SEQ], buf.mw[:, :], ident[0:SEQ, 0:SEQ]).then_inc(s.turned, 1)


def lora_up(pe, s, buf, n, banks, bw):
    pe.wait_ge(s.staged, n + 1)
    for h in range(2):
        pe.matmul(banks[h], buf.mwt[:, :], bw[:, h * 512:(h + 1) * 512],
                  start=True, stop=True).then_inc(s.up, 1)


def split_product(pe, out, stationary, moving, first, last):
    for i, (a, b) in enumerate(PASSES):
        mm = pe.matmul(out, stationary[a], moving[b], start=(first and i == 0),
                       stop=(last and i == 2))
    return mm


def build(nc, x, ctx_nat, ctx_t, mask, wq0_t, wk0, bq, bk, a0, b0, wq1, wk1, wv1, wo1, a1, b1,
          rope_q, rope_k, ident_in, tri0_in, tri1_in, out):
    kt_dram = nc.dram_tensor("k_rotated", (BATCH, GROUPS, P, KEYS_EVEN), F32, kind="Internal").ap()
    v_dram = nc.dram_tensor("v_rows", (BATCH, KEY_TILES, KEY_TILE, DIM), F32, kind="Internal").ap()
    q_dram = nc.dram_tensor("q_rotated", (HEADS, P, TOK), F32, kind="Internal").ap()
    x2_dram = nc.dram_tensor("x_after_layer0", (BATCH, SEQ, DIM), F32, kind="Internal").ap()
    with ExitStack() as outer:
        def sb(name, shape, dt=F32, ctx=outer):
            return ctx.enter_context(nc.sbuf_tensor(name, shape, dt))

        def sem(name, ctx=outer):
            return ctx.enter_context(nc.semaphore(name))

        banks = [outer.enter_context(nc.psum_tensor(f"bank{i}", [P, 512], F32)) for i in range(8)]
        k = Shared()
        k.x, k.ctx_nat, k.ctx_t, k.mask, k.ident_in, k.out = x, ctx_nat, ctx_t, mask, ident_in, out
        k.wq0_t, k.wk0, k.bq, k.bk = wq0_t, wk0, bq, bk
        k.wq1, k.wk1, k.wv1, k.wo1 = wq1, wk1, wv1, wo1
        k.a0, k.b0, k.a1, k.b1, k.tri0, k.tri1 = a0, b0, a1, b1, tri0_in, tri1_in
        k.rope_q, k.rope_k = rope_q, rope_k
        k.kt_dram, k.v_dram, k.q_dram, k.x2_dram = kt_dram, v_dram, q_dram, x2_dram
        k.banks, k.passed = banks, sem("passed")
        k.ident, k.minus_half = sb("ident", [P, P]), sb("minus_half", [SEQ, 1])
        with ExitStack() as layer0:
            k.qp = sb("qp_then_xn3", [P, CH, TOK], ctx=layer0)
            k.qb = sb("q_dot_bk", [1, TOK], ctx=layer0)
            query_phase(nc, k)
            key_phase(nc, k)
            layer0_phase(nc, k)
            query1_phase(nc, k)
        with ExitStack() as layer1:
            k.yt = sb("y_t", [P, CH, TOK], ctx=layer1)
            attention_phase(nc, k)


def buffers_of(nc, ctx):
    def sb(name, shape, dt=F32):
        return ctx.enter_context(nc.sbuf_tensor(name, shape, dt))

    def pair(name, shape):
        return [ctx.enter_context(nc.sbuf_tensor(f"{name}_{p}", shape, F32R)) for p in ("high", "low")]

    def sem(name):
        return ctx.enter_context(nc.semaphore(name))

    return sb, pair, sem


def query_phase(nc, k):
    with ExitStack() as ctx:
        sb, pair, sem = buffers_of(nc, ctx)
        bank = k.banks
        x_rows = sb("b_x_rows", [SEQ, 2, DIM])
        ln = NormBuffers(sb, "ln1", 2)
        xn = pair("xn1", [P, CH, TOK])
        qt = pair("q0_t", [P, CH, TOK])
        raw = sb("w0_raw", [P, 2, CH, P])
        w = pair("w0", [P, 2, CH, P])
        bq_sb, bk_sb = sb("bq_sb", [P, CH]), sb("bk_sb", [P, CH])
        bkp = pair("bk", [P, CH])

        consts = sem("b_consts")
        x_in = [sem(f"b_x_in{i}") for i in range(2)]
        s1 = NormSems(sem, "ln1")
        xn_low = sem("b_xn_low")
        half_set = sem("b_half_set")
        w_in = [sem(f"b_w_in{i}") for i in range(2)]
        w_high = sem("b_w_high")
        w_low = sem("b_w_low")
        acc = sem("b_acc")
        q_high = sem("b_q_high")
        q_done = sem("b_q_done")
        bk_high, bk_low = sem("b_bk_high"), sem("b_bk_low")
        qb_acc, qb_done = sem("b_qb_acc"), sem("b_qb_done")

        block = ctx.enter_context(nc.Block())

        @block.sync
        def _(sp):
            def load_x(i, slot):
                sp.dma_start(x_rows[:, slot, :], k.x[i]).then_inc(x_in[slot], 16)

            def load_w(tiles, i, n, slot):
                sp.wait_ge(w_low, n + 1)
                sp.dma_start(raw[:, slot], tiles[i]).then_inc(w_in[slot], 16)

            load_x(0, 0)
            load_x(1, 1)
            sp.dma_start(k.ident[:, :], k.ident_in).then_inc(consts, 16)
            sp.dma_start(bq_sb[:, :], k.bq).then_inc(consts, 16)
            sp.dma_start(bk_sb[:, :], k.bk).then_inc(consts, 16)
            load_w(k.wq0_t, 0, 0, 0)
            load_w(k.wq0_t, 1, 1, 1)
            with sp.Fori(1, BATCH // 2) as i:
                for slot in range(2):
                    sp.wait_ge(s1.normed, 2 * i + slot - 1)
                    load_x(2 * i + slot, slot)
            with sp.Fori(1, CH // 2) as i:
                for slot in range(2):
                    load_w(k.wq0_t, 2 * i + slot, 2 * i + slot, slot)
            with sp.Fori(0, CH // 2) as i:
                for slot in range(2):
                    load_w(k.wk0, 2 * i + slot, 2 * i + slot + CH, slot)

        @block.scalar
        def _(act):
            def weight_high(i, slot):
                act.wait_ge(w_in[slot], 16 * i + 16)
                act.wait_ge(acc, 4 * i + 2 * slot + 2)
                act.activation(w[0][:, slot], raw[:, slot], ACT.Copy).then_inc(w_high, 1)

            act.wait_ge(consts, 48)
            act.activation(bkp[0][:, :], bk_sb[:, :], ACT.Copy).then_inc(bk_high, 1)
            weight_high(0, 0)
            weight_high(0, 1)
            with act.Fori(0, BATCH // 2) as i:
                for slot in range(2):
                    for j in range(2):
                        act.wait_ge(s1.turned, 4 * i + 2 * slot + j + 1)
                        take_waits(act, k.passed)
                        act.activation(xn[0][:, 4 * j:4 * j + 4, bass.ds(SEQ * (2 * i + slot), SEQ)],
                                       bank[4 + 2 * slot + j][:, 0:HALF].rearrange("p (c t) -> p c t", c=4),
                                       ACT.Copy).then_inc(s1.evacuated, 1)
            with act.Fori(0, CH // 2) as i:
                for t in range(2):
                    for h in range(2):
                        act.wait_ge(acc, 4 * i + 2 * t + h + 5)
                        take_waits(act, k.passed)
                        act.activation(qt[0][:, bass.ds(2 * i + t, 1), h * HALF:(h + 1) * HALF],
                                       bank[2 * t + h][:, 0:HALF].unsqueeze(1), ACT.Identity,
                                       bias=bq_sb[:, bass.ds(2 * i + t, 1)]).then_inc(q_high, 1)
                    weight_high(i + 1, t)
            with act.Fori(0, CH // 2 - 1) as i:
                for t in range(2):
                    weight_high(i + 1 + CH // 2, t)
            act.wait_ge(qb_acc, 2)
            for h in range(2):
                act.activation(k.qb[0:1, h * HALF:(h + 1) * HALF], bank[4 + h][0:1, 0:HALF], ACT.Copy,
                               scale=1.0 / 32.0).then_inc(qb_done, 1)

        @block.gpsimd
        def _(pool):
            pool.sem_inc(w_low, 2)
            pool.memset(k.minus_half[:, :], -0.5).then_inc(half_set, 1)
            pool.wait_ge(half_set, 1)
            with pool.Fori(0, BATCH // 2) as i:
                for slot in range(2):
                    norm_rstd(pool, s1, ln, 2 * i + slot, slot, k.minus_half[:, :])
            pool.wait_ge(bk_high, 1)
            pool.tensor_tensor(bkp[1][:, :], bk_sb[:, :], f32(bkp[0][:, :]), ALU.subtract).then_inc(bk_low, 1)
            with pool.Fori(0, CH) as i:
                for slot in range(2):
                    pool.wait_ge(w_high, 2 * i + slot + 1)
                    pool.tensor_tensor(w[1][:, slot], raw[:, slot], f32(w[0][:, slot]),
                                       ALU.subtract).then_inc(w_low, 1)

        @block.vector
        def _(dve):
            dve.sem_inc(q_done, 4)
            dve.sem_inc(xn_low, 4)

            def turned_low(i, slot):
                for j in range(2):
                    dve.wait_ge(s1.evacuated, 4 * i + 2 * slot + j + 1)
                    at = bass.ds(SEQ * (2 * i + slot), SEQ)
                    dve.tensor_tensor(xn[1][:, 4 * j:4 * j + 4, at],
                                      bank[4 + 2 * slot + j][:, 0:HALF].rearrange("p (c t) -> p c t", c=4),
                                      f32(xn[0][:, 4 * j:4 * j + 4, at]), ALU.subtract).then_inc(xn_low, 1)

            def rows(i, slot):
                n = 2 * i + slot
                dve.wait_ge(x_in[slot], 16 * i + 16)
                norm_moments(dve, s1, ln, n, slot, x_rows[:, slot, :], k.passed)
                norm_apply(dve, s1, ln, n, slot, x_rows[:, slot, :])

            rows(0, 0)
            rows(0, 1)
            with dve.Fori(0, BATCH // 2 - 1) as i:
                for slot in range(2):
                    turned_low(i, slot)
                    rows(i + 1, slot)
            turned_low(BATCH // 2 - 1, 0)
            turned_low(BATCH // 2 - 1, 1)
            with dve.Fori(0, CH // 2) as i:
                for t in range(2):
                    for h in range(2):
                        dve.wait_ge(q_high, 4 * i + 2 * t + h + 1)
                        cols = slice(h * HALF, (h + 1) * HALF)
                        dve.scalar_tensor_tensor(
                            out=qt[1][:, bass.ds(2 * i + t, 1), cols],
                            in0=bank[2 * t + h][:, 0:HALF].unsqueeze(1), scalar=bq_sb[:, bass.ds(2 * i + t, 1)],
                            in1=f32(qt[0][:, bass.ds(2 * i + t, 1), cols]),
                            op0=ALU.add, op1=ALU.subtract).then_inc(q_done, 1)
            with dve.Fori(0, CH // 2) as i:
                for t in range(2):
                    for h in range(2):
                        dve.wait_ge(acc, 4 * i + 2 * t + h + 5 + 2 * CH)
                        dve.tensor_scalar(k.qp[:, bass.ds(2 * i + t, 1), h * HALF:(h + 1) * HALF],
                                          bank[2 * t + h][:, 0:HALF].unsqueeze(1), 1.0 / 32.0, None,
                                          ALU.mult).then_inc(q_done, 1)

        @block.tensor
        def _(pe):
            pe.sem_inc(acc, 4)
            pe.wait_ge(consts, 48)
            with pe.Fori(0, BATCH // 2) as i:
                for slot in range(2):
                    pe.wait_ge(xn_low, 4 * i + 2 * slot + 2)
                    norm_turn(pe, s1, ln, 2 * i + slot, slot, bank[4 + 2 * slot:6 + 2 * slot], k.ident)

            def tile(n, t, moving):
                pe.wait_ge(w_low, n + 3)
                for h in range(2):
                    pe.wait_ge(q_done, 2 * n + h + 1)
                    for c in range(CH):
                        mm = split_product(pe, bank[2 * t + h][:, 0:HALF], [p[:, t, c, :] for p in w],
                                           [p[:, c, h * HALF:(h + 1) * HALF] for p in moving],
                                           c == 0, c == CH - 1)
                    mm.then_inc(acc, 1)

            pe.wait_ge(xn_low, 4 + 2 * BATCH)
            with pe.Fori(0, CH // 2) as i:
                for t in range(2):
                    tile(2 * i + t, t, xn)
            pe.wait_ge(q_done, 4 + 2 * CH)
            with pe.Fori(0, CH // 2) as i:
                for t in range(2):
                    tile(2 * i + t + CH, t, qt)
            pe.wait_ge(bk_low, 1)
            for h in range(2):
                for c in range(CH):
                    mm = split_product(pe, bank[4 + h][:, 0:HALF],
                                       [p[:, c:c + 1].broadcast_to([P, P]) for p in bkp],
                                       [p[:, c, h * HALF:(h + 1) * HALF] for p in qt], c == 0, c == CH - 1)
                mm.then_inc(qb_acc, 1)


def key_phase(nc, k):
    with ExitStack() as ctx:
        sb, pair, sem = buffers_of(nc, ctx)
        bank = k.banks
        w = pair("wk1", [P, GROUPS, CH, P])
        w_raw = sb("wk1_raw", [P, 2, CH, P])
        ct = pair("k_ctx_t", [P, 2, CH, KEYS_EVEN])
        c_raw = sb("k_ctx_raw", [P, 2, 2, KEYS_EVEN])
        rope = sb("k_rope", [P, 2, KEYS_EVEN])
        straight, crossed = sb("k_straight", [P, 2, KEYS_EVEN]), sb("k_crossed", [P, 2, KEYS_EVEN])
        rotated = sb("k_rotated_sb", [P, 4, KEYS_EVEN])

        consts = sem("k_consts")
        w_in = [sem(f"k_w_in{i}") for i in range(2)]
        w_high = sem("k_w_high")
        w_low = sem("k_w_low")
        c_in = [sem(f"k_c_in{i}") for i in range(2)]
        c_high = sem("k_c_high")
        c_low = sem("k_c_low")
        acc = sem("k_acc")
        read = sem("k_read")
        ready = sem("k_ready")
        stored = [sem(f"k_stored{i}") for i in range(4)]

        block = ctx.enter_context(nc.Block())
        pairs = CH // 2

        def in_order(eng, start, batch):
            batch(0, 0)
            start()
            with eng.Fori(0, BATCH // 2 - 1) as i:
                batch(2 * i + 1, 1)
                batch(2 * i + 2, 0)
            batch(BATCH - 1, 1)

        @block.sync
        def _(sp):
            def load_ctx(b, slot):
                for j in range(pairs):
                    sp.wait_ge(c_low, pairs * b + j + 1)
                    sp.dma_start(c_raw[:, j % 2], k.ctx_t[b, :, 2 * j:2 * j + 2, :]).then_inc(c_in[j % 2], 16)

            def store(b):
                for g in range(GROUPS):
                    sp.wait_ge(ready, GROUPS * b + g + 3)
                    sp.dma_start(k.kt_dram[b, g], rotated[:, g % 4]).then_inc(stored[g % 4], 16)

            load_ctx(0, 0)
            sp.dma_start(rope[:, :, :], k.rope_k).then_inc(consts, 16)
            with sp.Fori(0, GROUPS // 2) as i:
                for t in range(2):
                    sp.wait_ge(w_low, 2 * i + t + 1)
                    sp.dma_start(w_raw[:, t], k.wk1[2 * i + t]).then_inc(w_in[t], 16)
            with sp.Fori(0, BATCH // 2 - 1) as i:
                load_ctx(2 * i + 1, 1)
                store(2 * i)
                load_ctx(2 * i + 2, 0)
                store(2 * i + 1)
            load_ctx(BATCH - 1, 1)
            store(BATCH - 2)
            store(BATCH - 1)
            for s in stored:
                sp.wait_ge(s, 16 + 16 * BATCH * GROUPS // 4)

        @block.scalar
        def _(act):
            def ctx_high(b, slot):
                act.wait_ge(acc, GROUPS * b + GROUPS)
                for j in range(pairs):
                    act.wait_ge(c_in[j % 2], 16 * (2 * b + j // 2) + 16)
                    act.activation(ct[0][:, slot, 2 * j:2 * j + 2, :], c_raw[:, j % 2],
                                   ACT.Copy).then_inc(c_high, 1)

            def weights_high():
                with act.Fori(0, GROUPS // 2) as i:
                    for t in range(2):
                        act.wait_ge(w_in[t], 16 * i + 16)
                        take_waits(act, k.passed)
                        act.activation(w[0][:, bass.ds(2 * i + t, 1)], w_raw[:, t:t + 1],
                                       ACT.Copy).then_inc(w_high, 1)

            in_order(act, weights_high, ctx_high)

        @block.gpsimd
        def _(pool):
            pool.sem_inc(w_low, 2)
            pool.sem_inc(c_low, 2)

            def ctx_low(b, slot):
                for j in range(pairs):
                    pool.wait_ge(c_high, pairs * b + j + 1)
                    at = ct[0][:, slot, 2 * j:2 * j + 2, :]
                    pool.tensor_tensor(ct[1][:, slot, 2 * j:2 * j + 2, :], c_raw[:, j % 2], f32(at),
                                       ALU.subtract).then_inc(c_low, 1)

            def weights_low():
                with pool.Fori(0, GROUPS // 2) as i:
                    for t in range(2):
                        pool.wait_ge(w_high, 2 * i + t + 1)
                        pool.tensor_tensor(w[1][:, bass.ds(2 * i + t, 1)], w_raw[:, t:t + 1],
                                           f32(w[0][:, bass.ds(2 * i + t, 1)]), ALU.subtract).then_inc(w_low, 1)

            in_order(pool, weights_low, ctx_low)

        @block.vector
        def _(dve):
            dve.sem_inc(read, 8)
            dve.sem_inc(ready, 2)
            for s in stored:
                dve.sem_inc(s, 16)
            dve.wait_ge(consts, 16)
            with dve.Fori(0, BATCH // 2) as i:
                for t in range(2):
                    for g in range(GROUPS):
                        n = GROUPS * (2 * i + t) + g
                        dve.wait_ge(acc, n + 17)
                        dve.wait_ge(ready, n + 1)
                        rotate(dve, bank[g][:, 0:KEYS_EVEN], rope[:, 0, :], rope[:, 1, :],
                               straight[:, g % 2], crossed[:, g % 2]).then_inc(read, 1)
                        dve.wait_ge(read, n + 9)
                        dve.wait_ge(stored[g % 4], 16 * (2 * (2 * i + t) + g // 4) + 16)
                        dve.tensor_tensor(rotated[:, g % 4], straight[:, g % 2], crossed[:, g % 2],
                                          ALU.add).then_inc(ready, 1)

        @block.tensor
        def _(pe):
            pe.sem_inc(acc, 16)
            with pe.Fori(0, BATCH // 2) as i:
                for t in range(2):
                    b = 2 * i + t
                    for g in range(GROUPS):
                        pe.wait_ge(read, GROUPS * b + g + 1)
                        pe.wait_ge(w_low, g + 3)
                        for c in range(CH):
                            if g == 0 and c % 2 == 0:
                                pe.wait_ge(c_low, pairs * b + c // 2 + 3)
                            mm = split_product(pe, bank[g][:, 0:KEYS_EVEN], [p[:, g, c, :] for p in w],
                                               [p[:, t, c, :] for p in ct], c == 0, c == CH - 1)
                        mm.then_inc(acc, 1)


def rotate(dve, product, cos, sin, straight, crossed):
    half = P // 2
    dve.tensor_tensor(straight, product, cos, ALU.mult)
    dve.tensor_tensor(crossed[0:half], product[half:P], sin[half:P], ALU.mult)
    return dve.tensor_tensor(crossed[half:P], product[0:half], sin[0:half], ALU.mult)


def layer0_phase(nc, k):
    with ExitStack() as ctx:
        sb, pair, sem = buffers_of(nc, ctx)
        bank = k.banks
        score_bank, turn_bank, v_bank, row_banks, xn_banks = bank[0], bank[1], bank[2:4], bank[4:6], bank[6:8]
        width = L0_EXPERTS * RANK + L0_EXPERTS
        wv = pair("wv1", [P, CH, DIM])
        ct = pair("c_ctx_t", [P, 2, CH, KEYS_EVEN])
        c_raw = sb("c_ctx_raw", [P, 2, 2, KEYS_EVEN])
        cn = sb("ctx_rows", [P, KEY_TILES, DIM])
        xr = sb("c_x_rows", [SEQ, 2, DIM])
        qp = pair("q_prime", [P, CH, SEQ])
        qb = sb("qb_row", [1, SEQ])
        ones = sb("ones_row", [1, KEYS_EVEN])
        nmax, total, inv = sb("c_nmax", [SEQ, 1]), sb("c_total", [SEQ, 1]), sb("c_inv", [SEQ, 1])
        e = sb("c_exp", [SEQ, KEYS_EVEN])
        et = sb("c_exp_t", [KEY_TILE, KEY_TILES, SEQ])
        v_out = sb("v_out", [KEY_TILE, 2, 512])
        ln2, ln3 = NormBuffers(sb, "ln2", 1), NormBuffers(sb, "ln3", 1)
        xnt = sb("xn2_t", [P, CH, SEQ])
        lora = LoraBuffers(sb, "lora0", L0_EXPERTS)
        aw, bw = sb("a0_sb", [P, CH, width]), sb("b0_sb", [L0_EXPERTS * RANK, DIM])
        tri = sb("tri0_sb", [SEQ, L0_EXPERTS, L0_EXPERTS])

        consts, ones_set = sem("c_consts"), sem("c_ones_set")
        w_in = [sem(f"c_w_in{i}") for i in range(2)]
        w_high, w_low = sem("c_w_high"), sem("c_w_low")
        c_in = [sem(f"c_c_in{i}") for i in range(2)]
        c_high, c_low = sem("c_c_high"), sem("c_c_low")
        cn_in, x_in = sem("c_cn_in"), [sem(f"c_x_in{i}") for i in range(2)]
        x_out = [sem(f"c_x_out{i}") for i in range(2)]
        q_high, q_low = sem("c_q_high"), sem("c_q_low")
        scored, maxed, exped = sem("c_scored"), sem("c_maxed"), sem("c_exped")
        e_turned, e_staged = sem("c_e_turned"), sem("c_e_staged")
        v_acc = sem("c_v_acc")
        v_read = sem("c_v_read")
        v_stored = [sem(f"c_v_stored{i}") for i in range(2)]
        attended, inverted, attn_added = sem("c_attended"), sem("c_inverted"), sem("c_attn_added")
        s2, s3, sl = NormSems(sem, "ln2"), NormSems(sem, "ln3"), LoraSems(sem, "lora0")

        block = ctx.enter_context(nc.Block())
        pairs = CH // 2

        def batches(eng, batch):
            with eng.Fori(0, BATCH // 2 - 1) as i:
                batch(i, 0, True)
                batch(i, 1, True)
            batch(BATCH // 2 - 1, 0, True)
            batch(BATCH // 2 - 1, 1, False)

        @block.sync
        def _(sp):
            def load_ctx(b):
                for j in range(pairs):
                    sp.wait_ge(c_low, pairs * b + j + 1)
                    sp.dma_start(c_raw[:, j % 2], k.ctx_t[b, :, 2 * j:2 * j + 2, :]).then_inc(c_in[j % 2], 16)

            def load_rows(i, t):
                sp.wait_ge(x_out[t], 16 * i + 16)
                sp.dma_start(xr[:, t], k.x[2 * i + t]).then_inc(x_in[t], 16)

            def load_cn(b):
                sp.dma_start(cn[0:KEY_TILE, :, :],
                             k.ctx_nat[b].rearrange("(t p) d -> p t d", p=KEY_TILE)).then_inc(cn_in, 16)

            for dst, src in ((aw, k.a0), (tri, k.tri0)):
                sp.dma_start(dst[:, :, :], src).then_inc(consts, 16)
            sp.dma_start(bw[:, :], k.b0).then_inc(consts, 16)
            load_ctx(0)
            for c in range(CH):
                sp.wait_ge(w_low, c + 1)
                sp.dma_start(cn[:, c % 2, :], k.wv1[:, c, :]).then_inc(w_in[c % 2], 16)
            load_rows(0, 0)
            sp.wait_ge(w_low, CH + 2)
            load_cn(0)

            def batch(i, t, ahead):
                b = 2 * i + t

                def store_v(p):
                    sp.wait_ge(v_read, 6 * b + p + 3)
                    kt, h = divmod(p, 2)
                    sp.dma_start(k.v_dram[b, kt, :, h * 512:(h + 1) * 512],
                                 v_out[:, p % 2]).then_inc(v_stored[p % 2], 16)

                if ahead:
                    load_ctx(b + 1)
                    load_rows(i + t, 1 - t)
                for p in range(3):
                    store_v(p)
                if ahead:
                    sp.wait_ge(attended, 2 * b + 2)
                    load_cn(b + 1)
                for p in range(3, 6):
                    store_v(p)
                sp.wait_ge(sl.added, 2 * b + 2)
                sp.dma_start(k.x2_dram[b], xr[:, t]).then_inc(x_out[t], 16)

            batches(sp, batch)
            for t in range(2):
                sp.wait_ge(v_stored[t], 16 + 16 * 3 * BATCH)
                sp.wait_ge(x_out[t], 16 + 16 * BATCH // 2)

        @block.scalar
        def _(act):
            for s in v_stored:
                act.sem_inc(s, 16)
            act.sem_inc(v_read, 2)

            def ctx_high(b, slot, js):
                for j in js:
                    act.wait_ge(c_in[j % 2], 16 * (2 * b + j // 2) + 16)
                    act.activation(ct[0][:, slot, 2 * j:2 * j + 2, :], c_raw[:, j % 2],
                                   ACT.Copy).then_inc(c_high, 1)

            def query_high(b):
                act.activation(qp[0][:, :, :], k.qp[:, :, bass.ds(SEQ * b, SEQ)], ACT.Copy).then_inc(q_high, 1)
                act.activation(qb[:, :], k.qb[:, bass.ds(SEQ * b, SEQ)], ACT.Copy).then_inc(q_high, 1)

            query_high(0)
            ctx_high(0, 0, range(pairs))
            for c in range(CH):
                act.wait_ge(w_in[c % 2], 16 * (c // 2) + 16)
                act.activation(wv[0][:, c, :], cn[:, c % 2, :], ACT.Copy).then_inc(w_high, 1)

            def batch(i, t, ahead):
                b = 2 * i + t

                def read_v(p):
                    act.wait_ge(v_acc, 6 * b + p + 1)
                    act.wait_ge(v_stored[p % 2], 16 * (3 * b + p // 2) + 16)
                    act.activation(v_out[:, p % 2], v_bank[p % 2][0:KEY_TILE, :], ACT.Copy).then_inc(v_read, 1)

                act.wait_ge(maxed, b + 1)
                act.activation(e[:, 0:KEYS], score_bank[0:SEQ, 0:KEYS], ACT.Exp, bias=nmax[:, :],
                               accum_out=total[:, :]).then_inc(exped, 1)
                if ahead:
                    query_high(b + 1)
                read_v(0)
                if ahead:
                    ctx_high(b + 1, 1 - t, (0, 1))
                act.wait_ge(e_turned, b + 1)
                act.activation(et[:, :, :], turn_bank[0:KEY_TILE, 0:KEY_TILES * SEQ].rearrange(
                    "p (c t) -> p c t", c=KEY_TILES), ACT.Copy).then_inc(e_staged, 1)
                read_v(1)
                if ahead:
                    ctx_high(b + 1, 1 - t, (2, 3))
                read_v(2)
                for j in range(2):
                    act.wait_ge(s2.turned, 2 * b + j + 1)
                    act.activation(xnt[:, 4 * j:4 * j + 4, :],
                                   xn_banks[j][:, 0:HALF].rearrange("p (c t) -> p c t", c=4),
                                   ACT.Copy).then_inc(s2.evacuated, 1)
                read_v(3)
                act.wait_ge(sl.chain, 11 * b + 8)
                act.activation(lora.ex[:, :], lora.lg[:, :], ACT.Exp, bias=lora.nmax[:, :]).then_inc(sl.gate_exp, 1)
                read_v(4)
                act.wait_ge(sl.turned, b + 1)
                act.activation(lora.mwt[:, :], turn_bank[0:L0_EXPERTS * RANK, 0:SEQ],
                               ACT.Copy).then_inc(sl.staged, 1)
                read_v(5)
                for j in range(2):
                    act.wait_ge(s3.turned, 2 * b + j + 1)
                    take_waits(act, k.passed)
                    act.activation(k.qp[:, 4 * j:4 * j + 4, bass.ds(SEQ * b, SEQ)],
                                   xn_banks[j][:, 0:HALF].rearrange("p (c t) -> p c t", c=4),
                                   ACT.Copy).then_inc(s3.evacuated, 1)

            batches(act, batch)

        @block.gpsimd
        def _(pool):
            pool.sem_inc(w_low, 2)
            pool.sem_inc(c_low, 2)

            def ctx_low(b, slot):
                for j in range(pairs):
                    pool.wait_ge(c_high, pairs * b + j + 1)
                    pool.tensor_tensor(ct[1][:, slot, 2 * j:2 * j + 2, :], c_raw[:, j % 2],
                                       f32(ct[0][:, slot, 2 * j:2 * j + 2, :]), ALU.subtract).then_inc(c_low, 1)

            def query_low(b):
                pool.wait_ge(q_high, 2 * b + 1)
                pool.tensor_tensor(qp[1][:, :, :], k.qp[:, :, bass.ds(SEQ * b, SEQ)], f32(qp[0][:, :, :]),
                                   ALU.subtract).then_inc(q_low, 1)

            query_low(0)
            ctx_low(0, 0)
            for c in range(CH):
                pool.wait_ge(w_high, c + 1)
                pool.tensor_tensor(wv[1][:, c, :], cn[:, c % 2, :], f32(wv[0][:, c, :]),
                                   ALU.subtract).then_inc(w_low, 1)

            def batch(i, t, ahead):
                b = 2 * i + t
                if ahead:
                    query_low(b + 1)
                    ctx_low(b + 1, 1 - t)
                norm_rstd(pool, s2, ln2, b, 0, k.minus_half[:, :])
                norm_rstd(pool, s3, ln3, b, 0, k.minus_half[:, :])

            batches(pool, batch)

        @block.vector
        def _(dve):
            for s in x_out:
                dve.sem_inc(s, 16)
            dve.memset(ones[:, :], 1.0).then_inc(ones_set, 1)
            dve.wait_ge(consts, 48)

            def batch(i, t, ahead):
                b = 2 * i + t
                dve.wait_ge(scored, b + 1)
                dve.tensor_reduce(nmax[:, :], score_bank[0:SEQ, 0:KEYS], AX, ALU.max,
                                  negate=True).then_inc(maxed, 1)
                dve.wait_ge(exped, b + 1)
                dve.reciprocal(inv[:, :], total[:, :]).then_inc(inverted, 1)
                dve.wait_ge(inverted, b + 1)
                dve.wait_ge(x_in[t], 16 * i + 16)
                for h in range(2):
                    dve.wait_ge(attended, 2 * b + h + 1)
                    cols = slice(h * 512, (h + 1) * 512)
                    dve.scalar_tensor_tensor(out=xr[:, t, cols], in0=row_banks[h][0:SEQ, :], scalar=inv[:, 0:1],
                                             in1=xr[:, t, cols], op0=ALU.mult,
                                             op1=ALU.add).then_inc(attn_added, 1)
                dve.wait_ge(attn_added, 2 * b + 2)
                norm_moments(dve, s2, ln2, b, 0, xr[:, t], k.passed)
                norm_apply(dve, s2, ln2, b, 0, xr[:, t])
                lora_gates(dve, sl, lora, b, score_bank[0:SEQ], tri[:, :, :], L0_TOP, True)
                for h in range(2):
                    dve.wait_ge(sl.up, 2 * b + h + 1)
                    cols = slice(h * 512, (h + 1) * 512)
                    dve.tensor_tensor(xr[:, t, cols], row_banks[h][0:SEQ, :], xr[:, t, cols],
                                      ALU.add).then_inc(sl.added, 1)
                dve.wait_ge(sl.added, 2 * b + 2)
                norm_moments(dve, s3, ln3, b, 0, xr[:, t], k.passed)
                norm_apply(dve, s3, ln3, b, 0, xr[:, t])

            batches(dve, batch)

        @block.tensor
        def _(pe):
            pe.wait_ge(ones_set, 1)
            pe.wait_ge(consts, 48)

            def batch(i, t, ahead):
                b = 2 * i + t

                def v_piece(p):
                    kt, h = divmod(p, 2)
                    pe.wait_ge(v_read, 6 * b + p + 1)
                    for c in range(CH):
                        if p == 0:
                            pe.wait_ge(w_low, c + 3)
                        mm = split_product(pe, v_bank[p % 2][0:KEY_TILE, :],
                                           [q[:, t, c, kt * KEY_TILE:(kt + 1) * KEY_TILE] for q in ct],
                                           [q[:, c, h * 512:(h + 1) * 512] for q in wv], c == 0, c == CH - 1)
                    mm.then_inc(v_acc, 1)

                pe.wait_ge(q_low, b + 1)
                pe.wait_ge(q_high, 2 * b + 2)
                for c in range(CH):
                    if c % 2 == 0:
                        pe.wait_ge(c_low, pairs * b + c // 2 + 3)
                    split_product(pe, score_bank[0:SEQ, 0:KEYS_EVEN], [q[:, c, :] for q in qp],
                                  [q[:, t, c, :] for q in ct], c == 0, False)
                pe.matmul(score_bank[0:SEQ, 0:KEYS_EVEN], qb[:, :], ones[:, :], start=False,
                          stop=True).then_inc(scored, 1)
                v_piece(0)
                pe.wait_ge(exped, b + 1)
                for kt in range(KEY_TILES):
                    mm = pe.transpose(turn_bank[0:KEY_TILE, kt * SEQ:(kt + 1) * SEQ],
                                      e[:, kt * KEY_TILE:(kt + 1) * KEY_TILE], k.ident[0:SEQ, 0:SEQ])
                mm.then_inc(e_turned, 1)
                v_piece(1)
                pe.wait_ge(e_staged, b + 1)
                pe.wait_ge(cn_in, 16 * b + 16)
                for h in range(2):
                    for kt in range(KEY_TILES):
                        mm = pe.matmul(row_banks[h][0:SEQ, :], et[:, kt, :],
                                       cn[0:KEY_TILE, kt, h * 512:(h + 1) * 512],
                                       start=(kt == 0), stop=(kt == KEY_TILES - 1))
                    mm.then_inc(attended, 1)
                v_piece(2)
                norm_turn(pe, s2, ln2, b, 0, xn_banks, k.ident)
                v_piece(3)
                pe.wait_ge(s2.evacuated, 2 * b + 2)
                lora_mid(pe, sl, b, score_bank[0:SEQ], xnt, aw)
                v_piece(4)
                lora_turn(pe, sl, lora, b, turn_bank, k.ident, k.passed)
                lora_up(pe, sl, lora, b, [r[0:SEQ, :] for r in row_banks], bw)
                v_piece(5)
                norm_turn(pe, s3, ln3, b, 0, xn_banks, k.ident)

            batches(pe, batch)


def query1_phase(nc, k):
    with ExitStack() as ctx:
        sb, pair, sem = buffers_of(nc, ctx)
        bank = k.banks
        xn = pair("xn3", [P, CH, TOK])
        raw = sb("wq1_raw", [P, 2, CH, P])
        w = pair("wq1", [P, 2, CH, P])
        rope = sb("q_rope", [P, 2, SEQ])
        straight, crossed = sb("q_straight", [P, 2, HALF]), sb("q_crossed", [P, 2, HALF])
        rotated = sb("q_rotated_sb", [P, 4, HALF])

        consts = sem("d_consts")
        x_high, x_low = sem("d_x_high"), sem("d_x_low")
        w_in = [sem(f"d_w_in{i}") for i in range(2)]
        w_high = sem("d_w_high")
        w_low = sem("d_w_low")
        acc = sem("d_acc")
        read = sem("d_read")
        ready = sem("d_ready")
        stored = [sem(f"d_stored{i}") for i in range(4)]

        block = ctx.enter_context(nc.Block())

        @block.sync
        def _(sp):
            sp.dma_start(rope[:, :, :], k.rope_q).then_inc(consts, 16)

            def load_w(i, t):
                sp.wait_ge(w_low, 2 * i + t + 1)
                sp.dma_start(raw[:, t], k.wq1[2 * i + t]).then_inc(w_in[t], 16)

            def store(i):
                for t in range(2):
                    for h in range(2):
                        sp.wait_ge(ready, 4 * i + 2 * t + h + 3)
                        sp.dma_start(k.q_dram[2 * i + t, :, h * HALF:(h + 1) * HALF],
                                     rotated[:, 2 * t + h]).then_inc(stored[2 * t + h], 16)

            load_w(0, 0)
            load_w(0, 1)
            with sp.Fori(0, HEADS // 2 - 1) as i:
                load_w(i + 1, 0)
                load_w(i + 1, 1)
                store(i)
            store(HEADS // 2 - 1)
            for s in stored:
                sp.wait_ge(s, 16 + 16 * HEADS // 2)

        @block.scalar
        def _(act):
            for c in range(CH):
                act.activation(xn[0][:, c, :], k.qp[:, c, :], ACT.Copy).then_inc(x_high, 1)
            with act.Fori(0, HEADS // 2) as i:
                for t in range(2):
                    act.wait_ge(w_in[t], 16 * i + 16)
                    act.wait_ge(acc, 4 * i + 2 * t + 2)
                    act.activation(w[0][:, t], raw[:, t], ACT.Copy).then_inc(w_high, 1)

        @block.gpsimd
        def _(pool):
            pool.sem_inc(w_low, 2)
            with pool.Fori(0, HEADS // 2) as i:
                for t in range(2):
                    pool.wait_ge(w_high, 2 * i + t + 1)
                    pool.tensor_tensor(w[1][:, t], raw[:, t], f32(w[0][:, t]), ALU.subtract).then_inc(w_low, 1)

        @block.vector
        def _(dve):
            dve.sem_inc(read, 4)
            dve.sem_inc(ready, 2)
            for s in stored:
                dve.sem_inc(s, 16)
            for c in range(CH):
                dve.wait_ge(x_high, c + 1)
                dve.tensor_tensor(xn[1][:, c, :], k.qp[:, c, :], f32(xn[0][:, c, :]),
                                  ALU.subtract).then_inc(x_low, 1)
            dve.wait_ge(consts, 16)
            cos, sin = (rope[:, j, :].unsqueeze(1).broadcast_to([P, QUAD, SEQ]) for j in range(2))

            def by_batch(ap):
                return ap.rearrange("p (b t) -> p b t", b=QUAD)

            with dve.Fori(0, HEADS // 2) as i:
                for t in range(2):
                    for h in range(2):
                        n = 4 * i + 2 * t + h
                        dve.wait_ge(acc, n + 5)
                        dve.wait_ge(ready, n + 1)
                        rotate(dve, by_batch(bank[2 * t + h][:, 0:HALF]), cos, sin,
                               by_batch(straight[:, h]), by_batch(crossed[:, h])).then_inc(read, 1)
                        dve.wait_ge(read, n + 5)
                        dve.wait_ge(stored[2 * t + h], 16 * i + 16)
                        dve.tensor_tensor(rotated[:, 2 * t + h], straight[:, h], crossed[:, h],
                                          ALU.add).then_inc(ready, 1)

        @block.tensor
        def _(pe):
            pe.sem_inc(acc, 4)
            with pe.Fori(0, HEADS // 2) as i:
                for t in range(2):
                    pe.wait_ge(w_low, 2 * i + t + 3)
                    for h in range(2):
                        pe.wait_ge(read, 4 * i + 2 * t + h + 1)
                        for c in range(CH):
                            if t == 0 and h == 0:
                                pe.wait_ge(x_low, c + 1)
                            mm = split_product(pe, bank[2 * t + h][:, 0:HALF], [q[:, t, c, :] for q in w],
                                               [q[:, c, h * HALF:(h + 1) * HALF] for q in xn],
                                               c == 0, c == CH - 1)
                        mm.then_inc(acc, 1)


def attention_phase(nc, k):
    with ExitStack() as ctx:
        sb, pair, sem = buffers_of(nc, ctx)
        bank = k.banks
        s_bank, p_bank, o_bank, y_bank = bank[0:2], bank[2:5], bank[5], bank[6:8]
        H = PER_GROUP
        STEPS = GROUPS * BATCH
        raw_q, raw_k = sb("e_raw_q", [P, 2, H, SEQ]), sb("e_raw_k", [P, 2, KEYS_EVEN])
        raw_v = sb("e_raw_v", [KEY_TILE, 2, KEY_TILES, P])
        q, kt = pair("e_q", [P, 2, H, SEQ]), pair("e_k", [P, 2, KEYS_EVEN])
        v = pair("e_v", [KEY_TILE, 2, KEY_TILES, P])
        raw_wo = sb("e_raw_wo", [P, 2, H, 256])
        wo = pair("e_wo", [P, 4, H, 256])
        mask = sb("e_mask", [SEQ, BATCH, KEYS])
        s_buf = sb("e_scores", [SEQ, 2, H, KEYS])
        mx, nm = sb("e_max", [SEQ, 2, H]), sb("e_nmax", [SEQ, 2, H])
        total, inv = sb("e_total", [SEQ, 2, H]), sb("e_inv", [SEQ, 2, H])
        pt = pair("e_p_t", [KEY_TILE, KEY_TILES, H * SEQ])
        ot = pair("e_o_t", [P, 2, H, HALF])

        mask_in = sem("e_mask_in")
        q_in, k_in, v_in, wo_in = ([sem(f"e_{n}_in{i}") for i in range(2)] for n in ("q", "k", "v", "wo"))
        qk_high, qk_low = sem("e_qk_high"), sem("e_qk_low")
        v_high, v_low = sem("e_v_high"), sem("e_v_low")
        wo_high, wo_low = sem("e_wo_high"), sem("e_wo_low")
        scored, masked, negated, exped = sem("e_scored"), sem("e_masked"), sem("e_negated"), sem("e_exped")
        inverted, normed = sem("e_inverted"), sem("e_normed")
        turned, pt_high, pt_low = sem("e_turned"), sem("e_pt_high"), sem("e_pt_low")
        o_acc, o_high, o_low = sem("e_o_acc"), sem("e_o_high"), sem("e_o_low")
        y_acc = sem("e_y_acc")
        y_added = sem("e_y_added")

        block = ctx.enter_context(nc.Block())

        def steps(eng, step):
            for s in range(4):
                step(s, s, 0)
            with eng.Fori(0, GROUPS - 1) as j:
                for u in range(4, 12):
                    step(8 * j + u, u % 8, j + u // 8)
            for s in range(STEPS - 4, STEPS):
                step(s, s % 8, GROUPS - 1)

        def known(s):
            return isinstance(s, int)

        def half_of(s, u):
            return s // 2 if known(s) else (s - u % 2) // 2

        @block.sync
        def _(sp):
            sp.dma_start(mask[:, :, :], k.mask.rearrange("b q s -> q b s")).then_inc(mask_in, 16)

            def load_qk(s, b, g):
                if not (known(s) and s < 2):
                    sp.wait_ge(qk_low, 2 * s - 2)
                sp.dma_start(raw_q[:, b % 2], k.q_dram[bass.ds(H * g, H), :, b * SEQ:(b + 1) * SEQ].rearrange(
                    "h p t -> p h t")).then_inc(q_in[b % 2], 16)
                sp.dma_start(raw_k[:, b % 2], k.kt_dram[b, g]).then_inc(k_in[b % 2], 16)

            def load_v(s, b, g):
                if not (known(s) and s < 2):
                    sp.wait_ge(v_low, s - 1)
                sp.dma_start(raw_v[:, b % 2], k.v_dram[b, :, :, bass.ds(P * g, P)].rearrange(
                    "c p d -> p c d")).then_inc(v_in[b % 2], 16)

            def load_wo(b, g, first):
                if not (first and b < 2):
                    sp.wait_ge(wo_low, 4 * g + b - 1)
                sp.dma_start(raw_wo[:, b % 2], k.wo1[g, :, :, b * 256:(b + 1) * 256]).then_inc(wo_in[b % 2], 16)

            load_qk(0, 0, 0)
            load_qk(1, 1, 0)
            load_v(0, 0, 0)

            def step(s, u, g):
                last = known(s) and s >= STEPS - 4
                if not (last and s + 2 >= STEPS):
                    load_qk(s + 2, (u + 2) % 8, g + (u + 2) // 8)
                if not (last and s + 1 >= STEPS):
                    load_v(s + 1, (u + 1) % 8, g + (u + 1) // 8)
                if u < 4:
                    load_wo(u, g, known(s))

            steps(sp, step)

        @block.scalar
        def _(act):
            def copy(dst, src, done):
                act.activation(dst, src, ACT.Copy).then_inc(done, 1)

            def qk_split(s, u):
                t = u % 2
                act.wait_ge(q_in[t], 16 * half_of(s, u) + 16)
                if not (known(s) and s < 2):
                    act.wait_ge(scored, 4 * s - 4)
                copy(q[0][:, t], raw_q[:, t], qk_high)
                act.wait_ge(k_in[t], 16 * half_of(s, u) + 16)
                copy(kt[0][:, t], raw_k[:, t], qk_high)

            def v_split(s, u):
                t = u % 2
                act.wait_ge(v_in[t], 16 * half_of(s, u) + 16)
                if not (known(s) and s < 2):
                    act.wait_ge(o_acc, s - 1)
                copy(v[0][:, t], raw_v[:, t], v_high)

            def exps(s, u, heads):
                t = u % 2
                for h in heads:
                    act.wait_ge(negated, 4 * s + h + 1)
                    act.activation(s_buf[:, t, h, :], s_buf[:, t, h, :], ACT.Exp, bias=nm[:, t, h:h + 1],
                                   accum_out=total[:, t, h:h + 1]).then_inc(exped, 1)

            qk_split(0, 0)
            v_split(0, 0)
            exps(0, 0, range(H))
            qk_split(1, 1)

            def step(s, u, g):
                last = known(s) and s >= STEPS - 4
                more = not (last and s + 1 >= STEPS)
                for c in range(KEY_TILES):
                    act.wait_ge(turned, 3 * s + c + 1)
                    if not (known(s) and s < 1):
                        act.wait_ge(o_acc, s)
                    copy(pt[0][:, c, :], p_bank[c][0:KEY_TILE, 0:HALF], pt_high)
                if more:
                    exps(s + 1, (u + 1) % 8, (0, 1))
                if not (last and s + 2 >= STEPS):
                    qk_split(s + 2, (u + 2) % 8)
                if more:
                    exps(s + 1, (u + 1) % 8, (2, 3))
                    v_split(s + 1, (u + 1) % 8)
                act.wait_ge(o_acc, s + 1)
                copy(ot[0][:, (u // 4) % 2, :, (u % 4) * SEQ:(u % 4 + 1) * SEQ],
                     o_bank[:, 0:HALF].rearrange("p (h t) -> p h t", h=H), o_high)
                if u < 4:
                    act.wait_ge(wo_in[u % 2], 16 * (2 * g + u // 2) + 16)
                    if not (known(s) and s < 4):
                        act.wait_ge(y_acc, 2 * s - 6)
                    copy(wo[0][:, u], raw_wo[:, u % 2], wo_high)

            steps(act, step)

        @block.gpsimd
        def _(pool):
            def low(dst, src, high, done):
                pool.tensor_tensor(dst, src, f32(high), ALU.subtract).then_inc(done, 1)

            def qk_split(s, u):
                t = u % 2
                pool.wait_ge(qk_high, 2 * s + 1)
                low(q[1][:, t], raw_q[:, t], q[0][:, t], qk_low)
                pool.wait_ge(qk_high, 2 * s + 2)
                low(kt[1][:, t], raw_k[:, t], kt[0][:, t], qk_low)

            def v_split(s, u):
                t = u % 2
                pool.wait_ge(v_high, s + 1)
                low(v[1][:, t], raw_v[:, t], v[0][:, t], v_low)

            qk_split(0, 0)
            v_split(0, 0)
            qk_split(1, 1)

            def step(s, u, g):
                last = known(s) and s >= STEPS - 4
                if not (last and s + 2 >= STEPS):
                    qk_split(s + 2, (u + 2) % 8)
                if not (last and s + 1 >= STEPS):
                    v_split(s + 1, (u + 1) % 8)
                if u < 4:
                    pool.wait_ge(wo_high, 4 * g + u + 1)
                    low(wo[1][:, u], raw_wo[:, u % 2], wo[0][:, u], wo_low)

            steps(pool, step)

        def y_tile(s, u, t):
            return 2 * (u % 4) + t, (0 if u >= 4 else HALF)

        whole = 2 + 2 * (STEPS - 4)
        rounds, round_of_vectors, round_of_products = final_phase(nc, k, sb, sem, block, y_added,
                                                                  (whole, whole + 8))

        @block.vector
        def _(dve):
            dve.memset(k.yt[:, :, :], 0.0).then_inc(y_added, 2)
            dve.wait_ge(mask_in, 16)

            def mask_scores(s, u, heads):
                t = u % 2
                for h in heads:
                    dve.wait_ge(scored, 4 * s + h + 1)
                    if not (known(s) and s < 2):
                        dve.wait_ge(turned, 3 * s - 3)
                    take_waits(dve, k.passed)
                    dve.tensor_tensor_reduce(s_buf[:, t, h, :], s_bank[h % 2][0:SEQ, 0:KEYS], mask[:, u, :],
                                             1.0, LOWEST, ALU.add, ALU.max,
                                             mx[:, t, h:h + 1]).then_inc(masked, 1)
                    dve.wait_ge(masked, 4 * s + h + 1)
                    dve.tensor_scalar(nm[:, t, h:h + 1], mx[:, t, h:h + 1], -1.0, None,
                                      ALU.mult).then_inc(negated, 1)

            def normalise(s, u):
                t = u % 2
                dve.wait_ge(exped, 4 * s + 4)
                dve.reciprocal(inv[:, t, :], total[:, t, :]).then_inc(inverted, 1)
                dve.wait_ge(inverted, s + 1)
                for h in range(H):
                    dve.tensor_scalar(s_buf[:, t, h, :], s_buf[:, t, h, :], inv[:, t, h:h + 1], None,
                                      ALU.mult).then_inc(normed, 1)

            def add_y(s, u, t):
                tile, at = y_tile(s, u, t)
                dve.wait_ge(y_acc, 2 * s - 8 + t + 1)
                dve.wait_ge(y_added, 2 * s - 8 + t + 2)
                dve.tensor_tensor(k.yt[:, tile, at:at + HALF], y_bank[t][:, 0:HALF],
                                  k.yt[:, tile, at:at + HALF], ALU.add).then_inc(y_added, 1)

            mask_scores(0, 0, range(H))
            normalise(0, 0)

            def step(s, u, g):
                more = not (known(s) and s + 1 >= STEPS)
                adds = not (known(s) and s < 4)
                if more:
                    mask_scores(s + 1, (u + 1) % 8, (0, 1))
                for c in range(KEY_TILES):
                    dve.wait_ge(pt_high, 3 * s + c + 1)
                    dve.tensor_tensor(pt[1][:, c, :], p_bank[c][0:KEY_TILE, 0:HALF], f32(pt[0][:, c, :]),
                                      ALU.subtract).then_inc(pt_low, 1)
                if adds:
                    add_y(s, u, 0)
                if more:
                    mask_scores(s + 1, (u + 1) % 8, (2, 3))
                if adds:
                    add_y(s, u, 1)
                if more:
                    normalise(s + 1, (u + 1) % 8)
                dve.wait_ge(o_high, s + 1)
                at = (slice(None), (u // 4) % 2, slice(None), slice((u % 4) * SEQ, (u % 4 + 1) * SEQ))
                dve.tensor_tensor(ot[1][at], o_bank[:, 0:HALF].rearrange("p (h t) -> p h t", h=H),
                                  f32(ot[0][at]), ALU.subtract).then_inc(o_low, 1)

            steps(dve, step)
            for r in rounds:
                if r < 4:
                    add_y(STEPS + r, r, 0)
                    add_y(STEPS + r, r, 1)
                round_of_vectors(dve, r)

        @block.tensor
        def _(pe):
            def scores(s, u, heads):
                t = u % 2
                pe.wait_ge(qk_low, 2 * s + 2)
                for h in heads:
                    if not (known(s) and s < 1 and h < 2):
                        pe.wait_ge(masked, 4 * s + h - 1)
                    split_product(pe, s_bank[h % 2][0:SEQ, 0:KEYS_EVEN], [x[:, t, h, :] for x in q],
                                  [x[:, t, :] for x in kt], True, True).then_inc(scored, 1)

            def project(s, u, t):
                quad = 0 if u >= 4 else 1
                pe.wait_ge(o_low, s - u % 4)
                if u >= 4 and t == 0:
                    pe.wait_ge(wo_low, (s - u) // 2 + u - 3)
                pe.wait_ge(y_added, 2 * s - 8 + t + 1)
                for h in range(H):
                    mm = split_product(pe, y_bank[t][:, 0:HALF],
                                       [x[:, u % 4, h, t * P:(t + 1) * P] for x in wo],
                                       [x[:, quad, h, :] for x in ot], h == 0, h == H - 1)
                mm.then_inc(y_acc, 1)

            scores(0, 0, range(H))

            def step(s, u, g):
                more = not (known(s) and s + 1 >= STEPS)
                adds = not (known(s) and s < 4)
                t = u % 2
                if more:
                    scores(s + 1, (u + 1) % 8, (0, 1))
                pe.wait_ge(normed, 4 * s + 4)
                for c in range(KEY_TILES):
                    if not (known(s) and s < 1):
                        pe.wait_ge(pt_low, 3 * s - 3 + c + 1)
                    for h in range(H):
                        mm = pe.transpose(p_bank[c][0:KEY_TILE, h * SEQ:(h + 1) * SEQ],
                                          s_buf[:, t, h, c * KEY_TILE:(c + 1) * KEY_TILE],
                                          k.ident[0:SEQ, 0:SEQ])
                    mm.then_inc(turned, 1)
                if adds:
                    project(s, u, 0)
                if more:
                    scores(s + 1, (u + 1) % 8, (2, 3))
                if adds:
                    project(s, u, 1)
                pe.wait_ge(v_low, s + 1)
                if not (known(s) and s < 1):
                    pe.wait_ge(o_low, s)
                for c in range(KEY_TILES):
                    pe.wait_ge(pt_low, 3 * s + c + 1)
                    mm = split_product(pe, o_bank[:, 0:HALF], [x[:, t, c, :] for x in v],
                                       [x[:, c, :] for x in pt], c == 0, c == KEY_TILES - 1)
                mm.then_inc(o_acc, 1)

            steps(pe, step)
            for r in rounds:
                if r < 4:
                    project(STEPS + r, r, 0)
                    project(STEPS + r, r, 1)
                round_of_products(pe, r)


def final_phase(nc, k, sb, sem, block, y_added, y_of_quad):
    bank = k.banks
    y_banks, xn_banks, mid_bank, turn_bank, up_banks = bank[0:2], bank[2:4], bank[4], bank[5], bank[6:8]
    width = L1_EXPERTS * RANK + L1_EXPERTS
    SLOTS = 5
    xr = sb("f_x_rows", [SEQ, SLOTS, DIM])
    ln = NormBuffers(sb, "ln4", 2)
    xnt = sb("xn4_t", [P, 2, CH, SEQ])
    lora = LoraBuffers(sb, "lora1", L1_EXPERTS)
    aw, bw = sb("a1_sb", [P, CH, width]), sb("b1_sb", [L1_EXPERTS * RANK, DIM])
    tri = sb("tri1_sb", [SEQ, L1_EXPERTS, L1_EXPERTS])

    consts = sem("f_consts")
    x_in = [sem(f"f_x_in{i}") for i in range(SLOTS)]
    x_out = [sem(f"f_x_out{i}") for i in range(SLOTS)]
    y_turned, x_summed = sem("f_y_turned"), sem("f_x_summed")
    s4, sl = NormSems(sem, "ln4"), LoraSems(sem, "lora1")
    rounds = range(BATCH + 3)

    def stage(r, n):
        return r - n if 0 <= r - n < BATCH else None

    @block.sync
    def _(sp):
        for dst, src in ((aw, k.a1), (tri, k.tri1)):
            sp.dma_start(dst[:, :, :], src).then_inc(consts, 16)
        sp.dma_start(bw[:, :], k.b1).then_inc(consts, 16)

        def load(b):
            if b >= SLOTS:
                sp.wait_ge(x_out[b % SLOTS], 16 * (b // SLOTS))
            sp.dma_start(xr[:, b % SLOTS], k.x2_dram[b]).then_inc(x_in[b % SLOTS], 16)

        for b in range(SLOTS):
            load(b)
        for b in range(BATCH):
            sp.wait_ge(sl.added, 2 * b + 2)
            sp.dma_start(k.out[b], xr[:, b % SLOTS]).then_inc(x_out[b % SLOTS], 16)
            if b + SLOTS < BATCH:
                load(b + SLOTS)
        for i, s in enumerate(x_out):
            sp.wait_ge(s, 16 * len(range(i, BATCH, SLOTS)))

    @block.scalar
    def _(act):
        for r in rounds:
            if (b := stage(r, 3)) is not None:
                act.wait_ge(sl.turned, b + 1)
                act.activation(lora.mwt[:, :], turn_bank[0:L1_EXPERTS * RANK, 0:SEQ],
                               ACT.Copy).then_inc(sl.staged, 1)
            if (b := stage(r, 1)) is not None:
                for j in range(2):
                    act.wait_ge(s4.turned, 2 * b + j + 1)
                    act.activation(xnt[:, b % 2, 4 * j:4 * j + 4, :],
                                   xn_banks[j][:, 0:HALF].rearrange("p (c t) -> p c t", c=4),
                                   ACT.Copy).then_inc(s4.evacuated, 1)

    @block.gpsimd
    def _(pool):
        for b in range(BATCH):
            norm_rstd(pool, s4, ln, b, b % 2, k.minus_half[:, :])

    def round_of_vectors(dve, r):
        if (b := stage(r, 0)) is not None:
            x = xr[:, b % SLOTS]
            dve.wait_ge(x_in[b % SLOTS], 16 * (b // SLOTS) + 16)
            for h in range(2):
                dve.wait_ge(y_turned, 2 * b + h + 1)
                cols = slice(h * 512, (h + 1) * 512)
                dve.tensor_tensor(x[:, cols], y_banks[h][0:SEQ, :], x[:, cols],
                                  ALU.add).then_inc(x_summed, 1)
            dve.wait_ge(x_summed, 2 * b + 2)
            norm_moments(dve, s4, ln, b, b % 2, x, k.passed)
        if (b := stage(r, 1)) is not None:
            norm_apply(dve, s4, ln, b, b % 2, xr[:, b % SLOTS])
        if (b := stage(r, 2)) is not None:
            if b == 0:
                dve.wait_ge(consts, 48)
            lora_gates(dve, sl, lora, b, mid_bank[0:SEQ], tri[:, :, :], L1_TOP, False)
        if (b := stage(r, 3)) is not None:
            x = xr[:, b % SLOTS]
            for h in range(2):
                dve.wait_ge(sl.up, 2 * b + h + 1)
                cols = slice(h * 512, (h + 1) * 512)
                dve.tensor_tensor(x[:, cols], up_banks[h][0:SEQ, :], x[:, cols],
                                  ALU.add).then_inc(sl.added, 1)

    def round_of_products(pe, r):
        if (b := stage(r, 3)) is not None:
            if b == 0:
                pe.wait_ge(y_added, y_of_quad[1])
            lora_turn(pe, sl, lora, b, turn_bank, k.ident, k.passed)
        if (b := stage(r, 0)) is not None:
            pe.wait_ge(y_added, y_of_quad[b // QUAD])
            for h in range(2):
                if b:
                    pe.wait_ge(x_summed, 2 * b - 1 + h)
                for c in range(4):
                    mm = pe.transpose(y_banks[h][0:SEQ, c * P:(c + 1) * P],
                                      k.yt[:, 4 * h + c, b * SEQ:(b + 1) * SEQ], k.ident[:, :])
                mm.then_inc(y_turned, 1)
        if (b := stage(r, 2)) is not None:
            if b == 0:
                pe.wait_ge(consts, 48)
            pe.wait_ge(s4.evacuated, 2 * b + 2)
            if b:
                pe.wait_ge(sl.gated, 2 * b)
            lora_mid(pe, sl, b, mid_bank[0:SEQ], xnt[:, b % 2], aw)
        if (b := stage(r, 3)) is not None:
            if b:
                pe.wait_ge(sl.added, 2 * b)
            lora_up(pe, sl, lora, b, [x[0:SEQ, :] for x in up_banks], bw)
        if (b := stage(r, 1)) is not None:
            if b:
                pe.wait_ge(s4.evacuated, 2 * b)
            norm_turn(pe, s4, ln, b, b % 2, xn_banks, k.ident)

    return rounds, round_of_vectors, round_of_products


def rope_tables(positions, scale):
    import numpy as np
    half = P // 2
    inv_freq = (1.0 / np.float32(10000.0) ** (np.arange(0, P, 2, dtype=np.float32) / np.float32(P))).astype(np.float32)
    angle = (np.arange(positions, dtype=np.float32)[None, :] * inv_freq[:, None]).astype(np.float32)
    table = np.zeros((P, 2, positions), np.float64)
    table[:half, 0] = table[half:, 0] = np.cos(angle.astype(np.float64))
    table[:half, 1] = np.sin(angle.astype(np.float64))
    table[half:, 1] = -table[:half, 1]
    return (table * scale).astype(np.float32)


def kernel(x, ctx_4096, mask_BxSxS2_ff0, L0_xattn_Wq, L0_xattn_bq, L0_xattn_Wk, L0_xattn_bk, L0_ffn_A, L0_ffn_B,
           L0_ffn_Wr, L1_xattn_wq, L1_xattn_wk, L1_xattn_wv, L1_xattn_wo, L1_ffn_route_w, L1_ffn_A, L1_ffn_Bw):
    import numpy as np
    import concourse.bacc as bacc
    from concourse.bass_utils import run_bass_kernel_spmd

    def rows(a):
        return np.ascontiguousarray(a)

    ctx = np.asarray(ctx_4096)
    ctx_t = np.zeros((BATCH, P, CH, KEYS_EVEN), ctx.dtype)
    ctx_t[..., :KEYS] = ctx.transpose(0, 2, 1).reshape(BATCH, CH, P, KEYS).transpose(0, 2, 1, 3)

    def tiles(w):
        w = np.asarray(w)
        return rows(w.reshape(CH, P, w.shape[1] // P, P).transpose(2, 1, 0, 3))

    def down(a, router):
        a, router = np.asarray(a), np.asarray(router)
        both = np.concatenate([a.reshape(-1, DIM), router], axis=0)
        return rows(both.T.reshape(CH, P, -1).transpose(1, 0, 2))

    def up(b):
        return rows(np.asarray(b).transpose(0, 2, 1).reshape(-1, DIM))

    def triangle(experts):
        t = np.tril(np.ones((experts, experts), np.float32), -1)
        return rows(np.broadcast_to(t, (SEQ, experts, experts)))

    wo = np.asarray(L1_xattn_wo).reshape(GROUPS, PER_GROUP, P, DIM).transpose(0, 2, 1, 3)
    arrays = dict(
        x=rows(x), ctx_nat=rows(ctx), ctx_t=ctx_t, mask=rows(mask_BxSxS2_ff0),
        wq0_t=tiles(np.asarray(L0_xattn_Wq).T), wk0=tiles(L0_xattn_Wk),
        bq=rows(np.asarray(L0_xattn_bq).reshape(CH, P).T), bk=rows(np.asarray(L0_xattn_bk).reshape(CH, P).T),
        a0=down(L0_ffn_A, L0_ffn_Wr), b0=up(L0_ffn_B),
        wq1=tiles(L1_xattn_wq), wk1=tiles(L1_xattn_wk),
        wv1=rows(np.asarray(L1_xattn_wv).reshape(CH, P, DIM).transpose(1, 0, 2)), wo1=rows(wo),
        a1=down(L1_ffn_A, L1_ffn_route_w), b1=up(L1_ffn_Bw),
        rope_q=rope_tables(SEQ, float(P) ** -0.5), rope_k=rope_tables(KEYS_EVEN, 1.0),
        ident_in=np.eye(P, dtype=np.float32), tri0_in=triangle(L0_EXPERTS), tri1_in=triangle(L1_EXPERTS))
    nc = bacc.Bacc("TRN2", target_bir_lowering=False, num_devices=1)
    args = {n: nc.dram_tensor(f"in_{n}", a.shape, mybir.dt.from_np(a.dtype), kind="ExternalInput").ap()
            for n, a in arrays.items()}
    out = nc.dram_tensor("out_0", (BATCH, SEQ, DIM), F32, kind="ExternalOutput").ap()
    build(nc, out=out, **args)
    r = run_bass_kernel_spmd(nc, [{f"in_{n}": a for n, a in arrays.items()}], core_ids=[0])
    return r.results[0]["out_0"]
```

```python
from contextlib import ExitStack

import concourse.bass as bass
from concourse import mybir

F32 = mybir.dt.float32
F32R = mybir.dt.float32r
ALU = mybir.AluOpType
ACT = mybir.ActivationFunctionType
AX = mybir.AxisListType.X

P = 128
BATCH, SEQ, DIM = 8, 112, 1024
KEYS = 375
KEYS_EVEN = 376
KEY_TILES, KEY_TILE = 3, 125
CH = DIM // P
TOK = BATCH * SEQ
HALF = TOK // 2
QUAD = HALF // SEQ
GROUPS, PER_GROUP = 8, 4
HEADS = GROUPS * PER_GROUP
L0_EXPERTS, L0_TOP = 4, 2
L1_EXPERTS, L1_TOP = 8, 1
RANK = 16
L0_SCALE = 4.0
EPS = 1e-5
LOWEST = -3.4028234663852886e38
PASSES = ((0, 0), (0, 1), (1, 0))


class Shared:
    pass


def f32(ap):
    return ap.bitcast(F32)


def take_waits(eng, passed):
    eng.sem_inc(passed, 1)


class NormSems:
    def __init__(self, sem, name):
        self.moments = sem(f"{name}_moments")
        self.rstd = sem(f"{name}_rstd")
        self.normed = sem(f"{name}_normed")
        self.turned = sem(f"{name}_turned")
        self.evacuated = sem(f"{name}_evac")


class NormBuffers:
    def __init__(self, sb, name, slots, xn=True):
        self.stats = sb(f"{name}_stats", [SEQ, slots, 2, 6])
        self.mv = sb(f"{name}_mv", [SEQ, slots, 2])
        self.ve = sb(f"{name}_ve", [SEQ, slots])
        self.rstd = sb(f"{name}_rstd", [SEQ, slots])
        self.xn = sb(f"{name}_xn", [SEQ, slots, DIM]) if xn else None


def norm_moments(dve, s, buf, n, k, x, passed):
    for h in range(2):
        dve.bn_stats(buf.stats[:, k, h, :], x[:, h * 512:(h + 1) * 512]).then_inc(s.moments, 1)
    dve.wait_ge(s.moments, 4 * n + 2)
    take_waits(dve, passed)
    dve.bn_aggr(buf.mv[:, k, :], buf.stats[:, k]).then_inc(s.moments, 1)
    dve.wait_ge(s.moments, 4 * n + 3)
    dve.tensor_scalar(buf.ve[:, k:k + 1], buf.mv[:, k, 1:2], EPS, None, ALU.add).then_inc(s.moments, 1)


def norm_rstd(pool, s, buf, n, k, minus_half):
    pool.wait_ge(s.moments, 4 * n + 4)
    pool.tensor_tensor(buf.rstd[:, k:k + 1], buf.ve[:, k:k + 1], minus_half, ALU.pow).then_inc(s.rstd, 1)


def norm_apply(dve, s, buf, n, k, x):
    dve.wait_ge(s.rstd, n + 1)
    dve.tensor_scalar(buf.xn[:, k, :], x, buf.mv[:, k, 0:1], buf.rstd[:, k:k + 1],
                      ALU.subtract, ALU.mult).then_inc(s.normed, 1)


def norm_turn(pe, s, buf, n, k, banks, ident):
    pe.wait_ge(s.normed, n + 1)
    for j in range(2):
        for c in range(4):
            ch = 4 * j + c
            last = pe.transpose(banks[j][:, c * SEQ:(c + 1) * SEQ], buf.xn[:, k, ch * P:(ch + 1) * P],
                                ident[0:SEQ, 0:SEQ])
        last.then_inc(s.turned, 1)


class LoraSems:
    def __init__(self, sem, name):
        self.mid = sem(f"{name}_mid")
        self.chain = sem(f"{name}_chain")
        self.gate_exp = sem(f"{name}_gexp")
        self.gated = sem(f"{name}_gated")
        self.turned = sem(f"{name}_mturned")
        self.staged = sem(f"{name}_staged")
        self.up = sem(f"{name}_up")
        self.added = sem(f"{name}_added")


class LoraBuffers:
    def __init__(self, sb, name, experts):
        self.e = e = experts
        self.lg = sb(f"{name}_lg", [SEQ, e])
        self.gt = sb(f"{name}_gt", [SEQ, e, e])
        self.eq = sb(f"{name}_eq", [SEQ, e, e])
        self.rank = sb(f"{name}_rank", [SEQ, e])
        self.sel = sb(f"{name}_sel", [SEQ, e])
        self.nmax = sb(f"{name}_nmax", [SEQ, 1])
        self.ex = sb(f"{name}_ex", [SEQ, e])
        self.exs = sb(f"{name}_exs", [SEQ, e])
        self.tot = sb(f"{name}_tot", [SEQ, 1])
        self.inv = sb(f"{name}_inv", [SEQ, 1])
        self.gate = sb(f"{name}_gate", [SEQ, e])
        self.mw = sb(f"{name}_mw", [SEQ, e * RANK])
        self.mwt = sb(f"{name}_mwt", [e * RANK, SEQ])


def lora_gates(dve, s, buf, n, mid, tri, top, softmax):
    e = buf.e
    steps = 11 if softmax else 7
    base = steps * n
    first = e * RANK
    over = [SEQ, e, e]
    dve.wait_ge(s.mid, n + 1)
    dve.tensor_copy(buf.lg[:, :], mid[:, first:first + e]).then_inc(s.chain, 1)
    other = buf.lg[:, :].unsqueeze(1).broadcast_to(over)
    own = buf.lg[:, :].unsqueeze(2).broadcast_to(over)
    dve.wait_ge(s.chain, base + 1)
    dve.tensor_tensor(buf.gt[:, :, :], other, own, ALU.is_gt).then_inc(s.chain, 1)
    dve.tensor_tensor(buf.eq[:, :, :], other, own, ALU.is_equal).then_inc(s.chain, 1)
    dve.wait_ge(s.chain, base + 3)
    dve.tensor_tensor(buf.eq[:, :, :], buf.eq[:, :, :], tri, ALU.mult).then_inc(s.chain, 1)
    dve.wait_ge(s.chain, base + 4)
    dve.tensor_tensor(buf.gt[:, :, :], buf.gt[:, :, :], buf.eq[:, :, :], ALU.add).then_inc(s.chain, 1)
    dve.wait_ge(s.chain, base + 5)
    dve.tensor_reduce(buf.rank[:, :], buf.gt[:, :, :], AX, ALU.add).then_inc(s.chain, 1)
    dve.wait_ge(s.chain, base + 6)
    if softmax:
        dve.tensor_scalar(buf.sel[:, :], buf.rank[:, :], float(top), None, ALU.is_lt).then_inc(s.chain, 1)
        dve.tensor_reduce(buf.nmax[:, :], buf.lg[:, :], AX, ALU.max, negate=True).then_inc(s.chain, 1)
        dve.wait_ge(s.chain, base + 8)
        dve.wait_ge(s.gate_exp, n + 1)
        dve.tensor_tensor(buf.exs[:, :], buf.ex[:, :], buf.sel[:, :], ALU.mult).then_inc(s.chain, 1)
        dve.wait_ge(s.chain, base + 9)
        dve.tensor_reduce(buf.tot[:, :], buf.exs[:, :], AX, ALU.add).then_inc(s.chain, 1)
        dve.wait_ge(s.chain, base + 10)
        dve.reciprocal(buf.inv[:, :], buf.tot[:, :]).then_inc(s.chain, 1)
        dve.wait_ge(s.chain, base + 11)
        dve.tensor_scalar(buf.gate[:, :], buf.exs[:, :], buf.inv[:, 0:1], L0_SCALE,
                          ALU.mult, ALU.mult).then_inc(s.gated, 1)
    else:
        dve.tensor_scalar(buf.sel[:, :], buf.rank[:, :], float(top), None, ALU.is_lt).then_inc(s.chain, 1)
        dve.wait_ge(s.chain, base + 7)
        dve.tensor_tensor(buf.gate[:, :], buf.lg[:, :], buf.sel[:, :], ALU.mult).then_inc(s.gated, 1)
    dve.wait_ge(s.gated, 2 * n + 1)
    dve.tensor_tensor(buf.mw[:, :].rearrange("t (e r) -> t e r", e=e),
                      mid[:, 0:first].rearrange("t (e r) -> t e r", e=e),
                      buf.gate[:, :].unsqueeze(2).broadcast_to([SEQ, e, RANK]), ALU.mult).then_inc(s.gated, 1)


def lora_mid(pe, s, n, mid, xnt, aw):
    width = aw.shape[-1]
    for c in range(CH):
        last = pe.matmul(mid[:, 0:width], xnt[:, c, :], aw[:, c, :], start=(c == 0), stop=(c == CH - 1))
    last.then_inc(s.mid, 1)


def lora_turn(pe, s, buf, n, bank, ident, passed):
    pe.wait_ge(s.gated, 2 * n + 2)
    take_waits(pe, passed)
    pe.transpose(bank[0:buf.e * RANK, 0:SEQ], buf.mw[:, :], ident[0:SEQ, 0:SEQ]).then_inc(s.turned, 1)


def lora_up(pe, s, buf, n, banks, bw):
    pe.wait_ge(s.staged, n + 1)
    for h in range(2):
        pe.matmul(banks[h], buf.mwt[:, :], bw[:, h * 512:(h + 1) * 512],
                  start=True, stop=True).then_inc(s.up, 1)


def split_product(pe, out, stationary, moving, first, last):
    for i, (a, b) in enumerate(PASSES):
        mm = pe.matmul(out, stationary[a], moving[b], start=(first and i == 0),
                       stop=(last and i == 2))
    return mm


def build(nc, x, ctx_nat, ctx_t, mask, wq0_t, wk0, bq, bk, a0, b0, wq1, wk1, wv1, wo1, a1, b1,
          rope_q, rope_k, ident_in, tri0_in, tri1_in, out):
    kt_dram = nc.dram_tensor("k_rotated", (BATCH, GROUPS, P, KEYS_EVEN), F32, kind="Internal").ap()
    v_dram = nc.dram_tensor("v_rows", (BATCH, KEY_TILES, KEY_TILE, DIM), F32, kind="Internal").ap()
    q_dram = nc.dram_tensor("q_rotated", (HEADS, P, TOK), F32, kind="Internal").ap()
    x2_dram = nc.dram_tensor("x_after_layer0", (BATCH, SEQ, DIM), F32, kind="Internal").ap()
    with ExitStack() as outer:
        def sb(name, shape, dt=F32, ctx=outer):
            return ctx.enter_context(nc.sbuf_tensor(name, shape, dt))

        def sem(name, ctx=outer):
            return ctx.enter_context(nc.semaphore(name))

        banks = [outer.enter_context(nc.psum_tensor(f"bank{i}", [P, 512], F32)) for i in range(8)]
        k = Shared()
        k.x, k.ctx_nat, k.ctx_t, k.mask, k.ident_in, k.out = x, ctx_nat, ctx_t, mask, ident_in, out
        k.wq0_t, k.wk0, k.bq, k.bk = wq0_t, wk0, bq, bk
        k.wq1, k.wk1, k.wv1, k.wo1 = wq1, wk1, wv1, wo1
        k.a0, k.b0, k.a1, k.b1, k.tri0, k.tri1 = a0, b0, a1, b1, tri0_in, tri1_in
        k.rope_q, k.rope_k = rope_q, rope_k
        k.kt_dram, k.v_dram, k.q_dram, k.x2_dram = kt_dram, v_dram, q_dram, x2_dram
        k.banks, k.passed = banks, sem("passed")
        k.ident, k.minus_half = sb("ident", [P, P]), sb("minus_half", [SEQ, 1])
        with ExitStack() as layer0:
            k.qp = sb("qp_then_xn3", [P, CH, TOK], ctx=layer0)
            k.qb = sb("q_dot_bk", [1, TOK], ctx=layer0)
            with ExitStack() as products:
                share_operands(nc, k, products)
                query_phase(nc, k)
                k.w_rest = buffers_of(nc, products)[1]("w_rest", [P, CH - 2, DIM])
                key_phase(nc, k)
                layer0_phase(nc, k)
            query1_phase(nc, k)
        with ExitStack() as layer1:
            k.yt = sb("y_t", [P, CH, TOK], ctx=layer1)
            attention_phase(nc, k)


def share_operands(nc, k, ctx):
    sb, pair, sem = buffers_of(nc, ctx)
    both = pair("shared_operand", [P, CH * TOK])
    ring = 2 * CH * KEYS_EVEN
    k.xn1 = [x[:, :].rearrange("p (c t) -> p c t", c=CH) for x in both]
    k.ctx_ring = [x[:, 0:ring].rearrange("p (s c k) -> p s c k", s=2, c=CH) for x in both]
    k.qp_split = [x[:, ring:ring + CH * SEQ].rearrange("p (c t) -> p c t", c=CH) for x in both]
    k.raw = sb("raw_weights_then_ctx_rows", [P, KEY_TILES, DIM])
    k.w_first = pair("w_first", [P, 2, DIM])
    k.c_raw = sb("ctx_raw", [P, 2, 2, KEYS_EVEN])


def weight_tile(k, n):
    return [x[:, n] for x in k.w_first] if n < 2 else [x[:, n - 2] for x in k.w_rest]


def split_ctx_high(act, k, j, slot, done):
    act.activation(k.ctx_ring[0][:, slot, 2 * j:2 * j + 2, :], k.c_raw[:, j % 2], ACT.Copy).then_inc(done, 1)


def split_ctx_low(pool, k, j, slot, done):
    pool.tensor_tensor(k.ctx_ring[1][:, slot, 2 * j:2 * j + 2, :], k.c_raw[:, j % 2],
                       f32(k.ctx_ring[0][:, slot, 2 * j:2 * j + 2, :]), ALU.subtract).then_inc(done, 1)


def buffers_of(nc, ctx):
    def sb(name, shape, dt=F32):
        return ctx.enter_context(nc.sbuf_tensor(name, shape, dt))

    def pair(name, shape):
        return [ctx.enter_context(nc.sbuf_tensor(f"{name}_{p}", shape, F32R)) for p in ("high", "low")]

    def sem(name):
        return ctx.enter_context(nc.semaphore(name))

    return sb, pair, sem


def query_phase(nc, k):
    with ExitStack() as ctx:
        sb, pair, sem = buffers_of(nc, ctx)
        bank = k.banks
        XS = 4
        x_rows = sb("b_x_rows", [SEQ, XS, DIM])
        ln = NormBuffers(sb, "ln1", 2)
        xn, raw = k.xn1, k.raw
        qt = pair("q0_t", [P, CH, TOK])
        w = [x[:, :, :].rearrange("p s (c m) -> p s c m", c=CH) for x in k.w_first]
        bq_sb, bk_sb = sb("bq_sb", [P, CH]), sb("bk_sb", [P, CH])
        dots = sb("q_dot_terms", [P, TOK])
        ones = sb("b_ones", [P, P])

        consts = sem("b_consts")
        x_in = [sem(f"b_x_in{i}") for i in range(XS)]
        s1 = NormSems(sem, "ln1")
        xn_low = sem("b_xn_low")
        w_in = [sem(f"b_w_in{i}") for i in range(2)]
        w_high = sem("b_w_high")
        w_low = sem("b_w_low")
        acc = sem("b_acc")
        q_high = sem("b_q_high")
        q_done = sem("b_q_done")
        dotted = sem("b_dotted")
        ones_set, half_set = sem("b_ones_set"), sem("b_half_set")
        qb_acc = sem("b_qb_acc")
        c_in = [sem(f"b_c_in{i}") for i in range(2)]
        c_high, c_low = sem("b_c_high"), sem("b_c_low")
        FIRST = ((0, 0), (1, 0), (0, 1), (1, 1))

        block = ctx.enter_context(nc.Block())

        @block.sync
        def _(sp):
            def load_x(n):
                if n >= XS:
                    sp.wait_ge(s1.normed, n - XS + 1)
                sp.dma_start(x_rows[:, n % XS, :], k.x[n]).then_inc(x_in[n % XS], 16)

            def load_w(tiles, i, n, slot):
                sp.wait_ge(w_low, n + 1)
                sp.dma_start(raw[:, slot], tiles[i].rearrange("p c m -> p (c m)")).then_inc(w_in[slot], 16)

            load_x(0)
            load_x(1)
            sp.dma_start(k.ident[:, :], k.ident_in).then_inc(consts, 16)
            sp.dma_start(bq_sb[:, :], k.bq).then_inc(consts, 16)
            sp.dma_start(bk_sb[:, :], k.bk).then_inc(consts, 16)
            load_w(k.wq0_t, 0, 0, 0)
            load_w(k.wq0_t, 1, 1, 1)
            for n in range(2, BATCH):
                load_x(n)
            with sp.Fori(1, CH // 2) as i:
                for slot in range(2):
                    load_w(k.wq0_t, 2 * i + slot, 2 * i + slot, slot)
            with sp.Fori(0, CH // 2) as i:
                for slot in range(2):
                    load_w(k.wk0, 2 * i + slot, 2 * i + slot + CH, slot)
            for j in range(CH // 2):
                if j >= 2:
                    sp.wait_ge(c_low, j - 1)
                sp.dma_start(k.c_raw[:, j % 2], k.ctx_t[0, :, 2 * j:2 * j + 2, :]).then_inc(c_in[j % 2], 16)
            load_w(k.wk1, 0, 2 * CH, 0)
            load_w(k.wk1, 1, 2 * CH + 1, 1)

        @block.scalar
        def _(act):
            def weight_high(i, slot, used):
                act.wait_ge(w_in[slot], 16 * i + 16)
                act.wait_ge(acc, used)
                act.activation(k.w_first[0][:, slot], raw[:, slot], ACT.Copy).then_inc(w_high, 1)

            def rows_high(n):
                for j in range(2):
                    act.wait_ge(s1.turned, 2 * n + j + 1)
                    act.activation(xn[0][:, 4 * j:4 * j + 4, SEQ * n:SEQ * (n + 1)],
                                   bank[4 + 2 * (n % 2) + j][:, 0:HALF].rearrange("p (c t) -> p c t", c=4),
                                   ACT.Copy).then_inc(s1.evacuated, 1)

            def query_high(unit, i, t, h):
                act.wait_ge(acc, unit + 5)
                take_waits(act, k.passed)
                act.activation(qt[0][:, bass.ds(2 * i + t, 1), h * HALF:(h + 1) * HALF],
                               bank[2 * t + h][:, 0:HALF].unsqueeze(1), ACT.Identity,
                               bias=bq_sb[:, bass.ds(2 * i + t, 1)]).then_inc(q_high, 1)

            weight_high(0, 0, 4)
            weight_high(0, 1, 4)
            for n in range(QUAD):
                rows_high(n)
            act.wait_ge(consts, 48)
            query_high(0, 0, *FIRST[0])
            rows_high(QUAD)
            rows_high(QUAD + 1)
            query_high(1, 0, *FIRST[1])
            rows_high(QUAD + 2)
            rows_high(QUAD + 3)
            query_high(2, 0, *FIRST[2])
            weight_high(1, 0, 7)
            query_high(3, 0, *FIRST[3])
            weight_high(1, 1, 8)
            with act.Fori(1, CH // 2) as i:
                for t in range(2):
                    for h in range(2):
                        query_high(4 * i + 2 * t + h, i, t, h)
                    weight_high(i + 1, t, 4 * i + 2 * t + 6)
            with act.Fori(CH // 2 + 1, CH - 1) as i:
                for t in range(2):
                    weight_high(i, t, 4 * i + 2 * t + 2)
            for t in range(2):
                weight_high(CH - 1, t, 4 * (CH - 1) + 2 * t + 2)
                for j in (2 * t, 2 * t + 1):
                    act.wait_ge(c_in[j % 2], 16 * (j // 2) + 16)
                    split_ctx_high(act, k, j, 0, c_high)
            weight_high(CH, 0, 4 * CH + 2)
            weight_high(CH, 1, 4 * CH + 4)
            act.wait_ge(qb_acc, 2)
            for h in range(2):
                act.activation(k.qb[0:1, h * HALF:(h + 1) * HALF], bank[4 + h][0:1, 0:HALF], ACT.Copy,
                               scale=1.0 / 32.0)

        @block.gpsimd
        def _(pool):
            pool.sem_inc(w_low, 2)
            pool.memset(k.minus_half[:, :], -0.5).then_inc(half_set, 1)
            pool.wait_ge(half_set, 1)

            def weight_low(i, slot):
                pool.wait_ge(w_high, 2 * i + slot + 1)
                pool.tensor_tensor(k.w_first[1][:, slot], raw[:, slot], f32(k.w_first[0][:, slot]),
                                   ALU.subtract).then_inc(w_low, 1)

            for n in range(BATCH):
                norm_rstd(pool, s1, ln, n, n % 2, k.minus_half[:, :])
                if n in (1, 3):
                    weight_low(0, n // 2)
            with pool.Fori(1, CH - 1) as i:
                for slot in range(2):
                    weight_low(i, slot)
            for t in range(2):
                weight_low(CH - 1, t)
                for j in (2 * t, 2 * t + 1):
                    pool.wait_ge(c_high, j + 1)
                    split_ctx_low(pool, k, j, 0, c_low)
            weight_low(CH, 0)
            weight_low(CH, 1)

        @block.vector
        def _(dve):
            dve.sem_inc(q_done, 4)
            dve.sem_inc(xn_low, 4)
            dve.memset(ones[:, :], 1.0).then_inc(ones_set, 1)
            dve.memset(dots[:, :], 0.0).then_inc(dotted, 1)

            def moments(n):
                dve.wait_ge(x_in[n % XS], 16 * (n // XS) + 16)
                norm_moments(dve, s1, ln, n, n % 2, x_rows[:, n % XS, :], k.passed)

            def rows_low(n):
                for j in range(2):
                    dve.wait_ge(s1.evacuated, 2 * n + j + 1)
                    at = slice(SEQ * n, SEQ * (n + 1))
                    dve.tensor_tensor(xn[1][:, 4 * j:4 * j + 4, at],
                                      bank[4 + 2 * (n % 2) + j][:, 0:HALF].rearrange("p (c t) -> p c t", c=4),
                                      f32(xn[0][:, 4 * j:4 * j + 4, at]), ALU.subtract).then_inc(xn_low, 1)

            moments(0)
            for n in range(BATCH):
                if n + 1 < BATCH:
                    moments(n + 1)
                if n >= 2:
                    dve.wait_ge(s1.turned, 2 * n - 2)
                norm_apply(dve, s1, ln, n, n % 2, x_rows[:, n % XS, :])
                if n >= 1:
                    rows_low(n - 1)
            rows_low(BATCH - 1)

            def query_low(unit, i, t, h):
                cols = slice(h * HALF, (h + 1) * HALF)
                at = (slice(None), bass.ds(2 * i + t, 1), cols)
                dve.wait_ge(q_high, unit + 1)
                dve.scalar_tensor_tensor(
                    out=qt[1][at], in0=bank[2 * t + h][:, 0:HALF].unsqueeze(1),
                    scalar=bq_sb[:, bass.ds(2 * i + t, 1)], in1=f32(qt[0][at]),
                    op0=ALU.add, op1=ALU.subtract).then_inc(q_done, 1)
                for part in range(2):
                    if part == 1:
                        dve.wait_ge(q_done, unit + 5)
                    dve.wait_ge(dotted, 2 * unit + part + 1)
                    dve.scalar_tensor_tensor(
                        out=dots[:, cols].unsqueeze(1), in0=f32(qt[part][at]),
                        scalar=bk_sb[:, bass.ds(2 * i + t, 1)], in1=dots[:, cols].unsqueeze(1),
                        op0=ALU.mult, op1=ALU.add).then_inc(dotted, 1)

            for unit, (t, h) in enumerate(FIRST):
                query_low(unit, 0, t, h)
            with dve.Fori(1, CH // 2) as i:
                for t in range(2):
                    for h in range(2):
                        query_low(4 * i + 2 * t + h, i, t, h)
            with dve.Fori(0, CH // 2) as i:
                for t in range(2):
                    for h in range(2):
                        dve.wait_ge(acc, 4 * i + 2 * t + h + 5 + 2 * CH)
                        dve.tensor_scalar(k.qp[:, bass.ds(2 * i + t, 1), h * HALF:(h + 1) * HALF],
                                          bank[2 * t + h][:, 0:HALF].unsqueeze(1), 1.0 / 32.0, None,
                                          ALU.mult).then_inc(q_done, 1)

        @block.tensor
        def _(pe):
            pe.sem_inc(acc, 4)
            pe.wait_ge(consts, 48)

            def turn(n):
                pe.wait_ge(xn_low, 2 * n + 2)
                norm_turn(pe, s1, ln, n, n % 2, bank[4 + 2 * (n % 2):6 + 2 * (n % 2)], k.ident)

            def half_tile(unit, t, h, moving):
                pe.wait_ge(q_done, unit + (2 if (t, h) == (0, 1) else 1))
                for c in range(CH):
                    mm = split_product(pe, bank[2 * t + h][:, 0:HALF], [p[:, t, c, :] for p in w],
                                       [p[:, c, h * HALF:(h + 1) * HALF] for p in moving],
                                       c == 0, c == CH - 1)
                mm.then_inc(acc, 1)

            def tiles(i, first_tile, moving):
                for t in range(2):
                    n = 2 * i + t + first_tile
                    pe.wait_ge(w_low, n + 3)
                    for h in range(2):
                        half_tile(2 * n + h, t, h, moving)

            for n in range(QUAD):
                turn(n)
            for unit, (t, h) in enumerate(FIRST):
                pe.wait_ge(w_low, t + 3)
                pe.wait_ge(xn_low, 4 + (1 + h) * BATCH)
                half_tile(unit, t, h, xn)
                if h == 0:
                    turn(QUAD + 2 * t)
                    turn(QUAD + 2 * t + 1)
            with pe.Fori(1, CH // 2) as i:
                tiles(i, 0, xn)
            pe.wait_ge(q_done, 4 + 2 * CH)
            with pe.Fori(0, CH // 2) as i:
                tiles(i, CH, qt)
            pe.wait_ge(ones_set, 1)
            for h in range(2):
                pe.wait_ge(dotted, 1 + 4 * CH)
                pe.matmul(bank[4 + h][:, 0:HALF], ones[:, :], dots[:, h * HALF:(h + 1) * HALF],
                          start=True, stop=True).then_inc(qb_acc, 1)


def key_phase(nc, k):
    with ExitStack() as ctx:
        sb, pair, sem = buffers_of(nc, ctx)
        bank = k.banks
        rope = sb("k_rope", [P, 2, KEYS_EVEN])
        straight, crossed = sb("k_straight", [P, 2, KEYS_EVEN]), sb("k_crossed", [P, 2, KEYS_EVEN])
        rotated = sb("k_rotated_sb", [P, 4, KEYS_EVEN])

        consts = sem("k_consts")
        w_in = [sem(f"k_w_in{i}") for i in range(3)]
        w_high = sem("k_w_high")
        w_low = sem("k_w_low")
        c_in = [sem(f"k_c_in{i}") for i in range(2)]
        c_high = sem("k_c_high")
        c_low = sem("k_c_low")
        q_high = sem("k_q_high")
        q_low = sem("k_q_low")
        acc = sem("k_acc")
        read = sem("k_read")
        ready = sem("k_ready")
        stored = [sem(f"k_stored{i}") for i in range(4)]

        block = ctx.enter_context(nc.Block())
        pairs = CH // 2

        def two_by_two(eng, batch):
            with eng.Fori(0, BATCH // 2) as i:
                batch(2 * i + 1, 1)
                batch(2 * i + 2, 0)

        @block.sync
        def _(sp):
            def load_ctx(b, source, js=range(pairs)):
                for j in js:
                    sp.wait_ge(c_low, pairs * (b - 1) + j + 1)
                    sp.dma_start(k.c_raw[:, j % 2], k.ctx_t[source, :, 2 * j:2 * j + 2, :]).then_inc(
                        c_in[j % 2], 16)

            def store_head(b, g):
                sp.wait_ge(ready, GROUPS * b + g + 3)
                sp.dma_start(k.kt_dram[b, g], rotated[:, g % 4]).then_inc(stored[g % 4], 16)

            def store(b):
                for g in range(GROUPS):
                    store_head(b, g)

            def load_wv(c):
                sp.wait_ge(w_low, GROUPS if c < 3 else GROUPS + c - 2)
                sp.dma_start(k.raw[:, c % 3], k.wv1[:, c, :]).then_inc(w_in[c % 3], 16)

            with sp.Fori(0, GROUPS // 2 - 1) as i:
                for t in range(2):
                    sp.wait_ge(w_low, 2 * i + t + 1)
                    sp.dma_start(k.raw[:, t], k.wk1[2 * i + t + 2].rearrange("p c m -> p (c m)")).then_inc(
                        w_in[t], 16)
            sp.dma_start(rope[:, :, :], k.rope_k).then_inc(consts, 16)
            with sp.Fori(0, BATCH // 2 - 1) as i:
                load_ctx(2 * i + 1, 2 * i + 1)
                store(2 * i)
                load_ctx(2 * i + 2, 2 * i + 2)
                store(2 * i + 1)
            load_ctx(BATCH - 1, BATCH - 1)
            load_ctx(BATCH, 0, (0, 1))
            for c in range(3):
                load_wv(c)
            store(BATCH - 2)
            load_ctx(BATCH, 0, (2, 3))
            for g in range(GROUPS):
                store_head(BATCH - 1, g)
                if g + 3 < CH:
                    load_wv(g + 3)
            for s in stored:
                sp.wait_ge(s, 16 + 16 * BATCH * GROUPS // 4)

        @block.scalar
        def _(act):
            def ctx_high(b, slot):
                act.wait_ge(acc, GROUPS * b + GROUPS)
                for j in range(pairs):
                    act.wait_ge(c_in[j % 2], 16 * (2 * (b - 1) + j // 2) + 16)
                    split_ctx_high(act, k, j, slot, c_high)

            with act.Fori(0, GROUPS // 2 - 1) as i:
                for t in range(2):
                    act.wait_ge(w_in[t], 16 * i + 16)
                    take_waits(act, k.passed)
                    act.activation(k.w_rest[0][:, bass.ds(2 * i + t, 1)], k.raw[:, t:t + 1],
                                   ACT.Copy).then_inc(w_high, 1)
            two_by_two(act, ctx_high)
            act.activation(k.qp_split[0], k.qp[:, :, 0:SEQ], ACT.Copy).then_inc(q_high, 1)
            for c in range(CH):
                before = GROUPS // 2 - 1 if c % 3 < 2 else 0
                act.wait_ge(w_in[c % 3], 16 * (before + c // 3) + 16)
                act.wait_ge(acc, 16 + GROUPS * (BATCH - 1) + c + 1)
                act.activation(weight_tile(k, c)[0], k.raw[:, c % 3], ACT.Copy).then_inc(w_high, 1)

        @block.gpsimd
        def _(pool):
            pool.sem_inc(w_low, 2)
            pool.sem_inc(c_low, 2)

            def ctx_low(b, slot):
                for j in range(pairs):
                    pool.wait_ge(c_high, pairs * (b - 1) + j + 1)
                    split_ctx_low(pool, k, j, slot, c_low)

            with pool.Fori(0, GROUPS // 2 - 1) as i:
                for t in range(2):
                    pool.wait_ge(w_high, 2 * i + t + 1)
                    pool.tensor_tensor(k.w_rest[1][:, bass.ds(2 * i + t, 1)], k.raw[:, t:t + 1],
                                       f32(k.w_rest[0][:, bass.ds(2 * i + t, 1)]), ALU.subtract).then_inc(w_low, 1)
            two_by_two(pool, ctx_low)
            pool.wait_ge(q_high, 1)
            pool.tensor_tensor(k.qp_split[1], k.qp[:, :, 0:SEQ], f32(k.qp_split[0]), ALU.subtract).then_inc(q_low, 1)
            for c in range(CH):
                high, low = weight_tile(k, c)
                pool.wait_ge(w_high, GROUPS - 2 + c + 1)
                pool.tensor_tensor(low, k.raw[:, c % 3], f32(high), ALU.subtract).then_inc(w_low, 1)

        @block.vector
        def _(dve):
            dve.sem_inc(read, 8)
            dve.sem_inc(ready, 2)
            for s in stored:
                dve.sem_inc(s, 16)
            dve.wait_ge(consts, 16)
            with dve.Fori(0, BATCH // 2) as i:
                for t in range(2):
                    for g in range(GROUPS):
                        n = GROUPS * (2 * i + t) + g
                        dve.wait_ge(acc, n + 17)
                        dve.wait_ge(ready, n + 1)
                        rotate(dve, bank[g][:, 0:KEYS_EVEN], rope[:, 0, :], rope[:, 1, :],
                               straight[:, g % 2], crossed[:, g % 2]).then_inc(read, 1)
                        dve.wait_ge(read, n + 9)
                        dve.wait_ge(stored[g % 4], 16 * (2 * (2 * i + t) + g // 4) + 16)
                        dve.tensor_tensor(rotated[:, g % 4], straight[:, g % 2], crossed[:, g % 2],
                                          ALU.add).then_inc(ready, 1)

        @block.tensor
        def _(pe):
            pe.sem_inc(acc, 16)

            def batch(b, t):
                for g in range(GROUPS):
                    pe.wait_ge(read, GROUPS * b + g + 1)
                    if g >= 2:
                        pe.wait_ge(w_low, g + 1)
                    for c in range(CH):
                        if g == 0 and c % 2 == 0 and not (isinstance(b, int) and b == 0):
                            pe.wait_ge(c_low, pairs * (b - 1) + c // 2 + 3)
                        mm = split_product(pe, bank[g][:, 0:KEYS_EVEN],
                                           [p[:, c * P:(c + 1) * P] for p in weight_tile(k, g)],
                                           [p[:, t, c, :] for p in k.ctx_ring], c == 0, c == CH - 1)
                    mm.then_inc(acc, 1)

            batch(0, 0)
            batch(1, 1)
            with pe.Fori(1, BATCH // 2) as i:
                batch(2 * i, 0)
                batch(2 * i + 1, 1)


def rotate(dve, product, cos, sin, straight, crossed):
    half = P // 2
    dve.tensor_tensor(straight, product, cos, ALU.mult)
    dve.tensor_tensor(crossed[0:half], product[half:P], sin[half:P], ALU.mult)
    return dve.tensor_tensor(crossed[half:P], product[0:half], sin[0:half], ALU.mult)


def layer0_phase(nc, k):
    with ExitStack() as ctx:
        sb, pair, sem = buffers_of(nc, ctx)
        bank = k.banks
        score_bank, turn_bank, v_bank, row_banks, xn_banks = bank[0], bank[1], bank[2:4], bank[4:6], bank[6:8]
        width = L0_EXPERTS * RANK + L0_EXPERTS
        ct, cn, qp = k.ctx_ring, k.raw, k.qp_split
        wv = [weight_tile(k, c) for c in range(CH)]
        xr = sb("c_x_rows", [SEQ, 2, DIM])
        qb = sb("qb_row", [1, SEQ])
        ones = sb("ones_row", [1, KEYS_EVEN])
        nmax, total, inv = sb("c_nmax", [SEQ, 1]), sb("c_total", [SEQ, 1]), sb("c_inv", [SEQ, 1])
        e = sb("c_exp", [SEQ, KEYS_EVEN])
        et = sb("c_exp_t", [KEY_TILE, KEY_TILES, SEQ])
        v_out = sb("v_out", [KEY_TILE, 2, 512])
        ln2, ln3 = NormBuffers(sb, "ln2", 1), NormBuffers(sb, "ln3", 1, xn=False)
        ln3.xn = ln2.xn
        xnt = sb("xn2_t", [P, CH, SEQ])
        lora = LoraBuffers(sb, "lora0", L0_EXPERTS)
        aw, bw = sb("a0_sb", [P, CH, width]), sb("b0_sb", [L0_EXPERTS * RANK, DIM])
        tri = sb("tri0_sb", [SEQ, L0_EXPERTS, L0_EXPERTS])

        consts, ones_set = sem("c_consts"), sem("c_ones_set")
        c_in = [sem(f"c_c_in{i}") for i in range(2)]
        c_high, c_low = sem("c_c_high"), sem("c_c_low")
        cn_in, x_in = sem("c_cn_in"), [sem(f"c_x_in{i}") for i in range(2)]
        x_out = [sem(f"c_x_out{i}") for i in range(2)]
        q_high, q_low = sem("c_q_high"), sem("c_q_low")
        scored, maxed, exped = sem("c_scored"), sem("c_maxed"), sem("c_exped")
        e_turned, e_staged = sem("c_e_turned"), sem("c_e_staged")
        v_acc = sem("c_v_acc")
        v_read = sem("c_v_read")
        v_stored = [sem(f"c_v_stored{i}") for i in range(2)]
        attended, inverted, attn_added = sem("c_attended"), sem("c_inverted"), sem("c_attn_added")
        s2, s3, sl = NormSems(sem, "ln2"), NormSems(sem, "ln3"), LoraSems(sem, "lora0")

        block = ctx.enter_context(nc.Block())
        pairs = CH // 2

        def batches(eng, batch):
            with eng.Fori(0, BATCH // 2 - 1) as i:
                batch(i, 0, True)
                batch(i, 1, True)
            batch(BATCH // 2 - 1, 0, True)
            batch(BATCH // 2 - 1, 1, False)

        @block.sync
        def _(sp):
            def load_ctx(b):
                for j in range(pairs):
                    sp.wait_ge(c_low, pairs * b + j + 1)
                    sp.dma_start(k.c_raw[:, j % 2], k.ctx_t[b, :, 2 * j:2 * j + 2, :]).then_inc(c_in[j % 2], 16)

            def load_rows(i, t):
                sp.wait_ge(x_out[t], 16 * i + 16)
                sp.dma_start(xr[:, t], k.x[2 * i + t]).then_inc(x_in[t], 16)

            def load_cn(b):
                sp.dma_start(cn[0:KEY_TILE, :, :],
                             k.ctx_nat[b].rearrange("(t p) d -> p t d", p=KEY_TILE)).then_inc(cn_in, 16)

            for dst, src in ((aw, k.a0), (tri, k.tri0)):
                sp.dma_start(dst[:, :, :], src).then_inc(consts, 16)
            sp.dma_start(bw[:, :], k.b0).then_inc(consts, 16)
            load_cn(0)
            load_rows(0, 0)

            def batch(i, t, ahead):
                b = 2 * i + t

                def store_v(p):
                    sp.wait_ge(v_read, 6 * b + p + 3)
                    kt, h = divmod(p, 2)
                    sp.dma_start(k.v_dram[b, kt, :, h * 512:(h + 1) * 512],
                                 v_out[:, p % 2]).then_inc(v_stored[p % 2], 16)

                if ahead:
                    load_ctx(b + 1)
                    load_rows(i + t, 1 - t)
                for p in range(3):
                    store_v(p)
                if ahead:
                    sp.wait_ge(attended, 2 * b + 2)
                    load_cn(b + 1)
                for p in range(3, 6):
                    store_v(p)
                sp.wait_ge(sl.added, 2 * b + 2)
                sp.dma_start(k.x2_dram[b], xr[:, t]).then_inc(x_out[t], 16)

            batches(sp, batch)
            for t in range(2):
                sp.wait_ge(v_stored[t], 16 + 16 * 3 * BATCH)
                sp.wait_ge(x_out[t], 16 + 16 * BATCH // 2)

        @block.scalar
        def _(act):
            for s in v_stored:
                act.sem_inc(s, 16)
            act.sem_inc(v_read, 2)

            def ctx_high(b, slot, js):
                for j in js:
                    act.wait_ge(c_in[j % 2], 16 * (2 * b + j // 2) + 16)
                    split_ctx_high(act, k, j, slot, c_high)

            def query_high(b):
                act.activation(qp[0], k.qp[:, :, bass.ds(SEQ * b, SEQ)], ACT.Copy).then_inc(q_high, 1)
                act.activation(qb[:, :], k.qb[:, bass.ds(SEQ * b, SEQ)], ACT.Copy).then_inc(q_high, 1)

            for s in c_in:
                act.sem_inc(s, 16 * pairs // 2)
            act.sem_inc(c_high, pairs)
            act.activation(qb[:, :], k.qb[:, 0:SEQ], ACT.Copy).then_inc(q_high, 2)

            def batch(i, t, ahead):
                b = 2 * i + t

                def read_v(p):
                    act.wait_ge(v_acc, 6 * b + p + 1)
                    act.wait_ge(v_stored[p % 2], 16 * (3 * b + p // 2) + 16)
                    act.activation(v_out[:, p % 2], v_bank[p % 2][0:KEY_TILE, :], ACT.Copy).then_inc(v_read, 1)

                act.wait_ge(maxed, b + 1)
                act.activation(e[:, 0:KEYS], score_bank[0:SEQ, 0:KEYS], ACT.Exp, bias=nmax[:, :],
                               accum_out=total[:, :]).then_inc(exped, 1)
                if ahead:
                    query_high(b + 1)
                read_v(0)
                if ahead:
                    ctx_high(b + 1, 1 - t, (0, 1))
                act.wait_ge(e_turned, b + 1)
                act.activation(et[:, :, :], turn_bank[0:KEY_TILE, 0:KEY_TILES * SEQ].rearrange(
                    "p (c t) -> p c t", c=KEY_TILES), ACT.Copy).then_inc(e_staged, 1)
                read_v(1)
                if ahead:
                    ctx_high(b + 1, 1 - t, (2, 3))
                read_v(2)
                for j in range(2):
                    act.wait_ge(s2.turned, 2 * b + j + 1)
                    act.activation(xnt[:, 4 * j:4 * j + 4, :],
                                   xn_banks[j][:, 0:HALF].rearrange("p (c t) -> p c t", c=4),
                                   ACT.Copy).then_inc(s2.evacuated, 1)
                read_v(3)
                act.wait_ge(sl.chain, 11 * b + 8)
                act.activation(lora.ex[:, :], lora.lg[:, :], ACT.Exp, bias=lora.nmax[:, :]).then_inc(sl.gate_exp, 1)
                read_v(4)
                act.wait_ge(sl.turned, b + 1)
                act.activation(lora.mwt[:, :], turn_bank[0:L0_EXPERTS * RANK, 0:SEQ],
                               ACT.Copy).then_inc(sl.staged, 1)
                read_v(5)
                for j in range(2):
                    act.wait_ge(s3.turned, 2 * b + j + 1)
                    take_waits(act, k.passed)
                    act.activation(k.qp[:, 4 * j:4 * j + 4, bass.ds(SEQ * b, SEQ)],
                                   xn_banks[j][:, 0:HALF].rearrange("p (c t) -> p c t", c=4),
                                   ACT.Copy).then_inc(s3.evacuated, 1)

            batches(act, batch)

        @block.gpsimd
        def _(pool):
            pool.sem_inc(c_low, pairs + 2)
            pool.sem_inc(q_low, 1)

            def ctx_low(b, slot):
                for j in range(pairs):
                    pool.wait_ge(c_high, pairs * b + j + 1)
                    split_ctx_low(pool, k, j, slot, c_low)

            def query_low(b):
                pool.wait_ge(q_high, 2 * b + 1)
                pool.tensor_tensor(qp[1], k.qp[:, :, bass.ds(SEQ * b, SEQ)], f32(qp[0]),
                                   ALU.subtract).then_inc(q_low, 1)

            def batch(i, t, ahead):
                b = 2 * i + t
                if ahead:
                    query_low(b + 1)
                    ctx_low(b + 1, 1 - t)
                norm_rstd(pool, s2, ln2, b, 0, k.minus_half[:, :])
                norm_rstd(pool, s3, ln3, b, 0, k.minus_half[:, :])

            batches(pool, batch)

        @block.vector
        def _(dve):
            for s in x_out:
                dve.sem_inc(s, 16)
            dve.memset(ones[:, :], 1.0).then_inc(ones_set, 1)

            def batch(i, t, ahead):
                b = 2 * i + t
                dve.wait_ge(scored, b + 1)
                dve.tensor_reduce(nmax[:, :], score_bank[0:SEQ, 0:KEYS], AX, ALU.max,
                                  negate=True).then_inc(maxed, 1)
                dve.wait_ge(exped, b + 1)
                dve.reciprocal(inv[:, :], total[:, :]).then_inc(inverted, 1)
                dve.wait_ge(inverted, b + 1)
                dve.wait_ge(x_in[t], 16 * i + 16)
                for h in range(2):
                    dve.wait_ge(attended, 2 * b + h + 1)
                    cols = slice(h * 512, (h + 1) * 512)
                    dve.scalar_tensor_tensor(out=xr[:, t, cols], in0=row_banks[h][0:SEQ, :], scalar=inv[:, 0:1],
                                             in1=xr[:, t, cols], op0=ALU.mult,
                                             op1=ALU.add).then_inc(attn_added, 1)
                dve.wait_ge(attn_added, 2 * b + 2)
                norm_moments(dve, s2, ln2, b, 0, xr[:, t], k.passed)
                norm_apply(dve, s2, ln2, b, 0, xr[:, t])
                dve.wait_ge(consts, 48)
                lora_gates(dve, sl, lora, b, score_bank[0:SEQ], tri[:, :, :], L0_TOP, True)
                for h in range(2):
                    dve.wait_ge(sl.up, 2 * b + h + 1)
                    cols = slice(h * 512, (h + 1) * 512)
                    dve.tensor_tensor(xr[:, t, cols], row_banks[h][0:SEQ, :], xr[:, t, cols],
                                      ALU.add).then_inc(sl.added, 1)
                dve.wait_ge(sl.added, 2 * b + 2)
                norm_moments(dve, s3, ln3, b, 0, xr[:, t], k.passed)
                norm_apply(dve, s3, ln3, b, 0, xr[:, t])

            batches(dve, batch)

        @block.tensor
        def _(pe):
            pe.wait_ge(ones_set, 1)

            def batch(i, t, ahead):
                b = 2 * i + t

                def v_piece(p):
                    kt, h = divmod(p, 2)
                    pe.wait_ge(v_read, 6 * b + p + 1)
                    for c in range(CH):
                        mm = split_product(pe, v_bank[p % 2][0:KEY_TILE, :],
                                           [q[:, t, c, kt * KEY_TILE:(kt + 1) * KEY_TILE] for q in ct],
                                           [q[:, h * 512:(h + 1) * 512] for q in wv[c]], c == 0, c == CH - 1)
                    mm.then_inc(v_acc, 1)

                pe.wait_ge(q_low, b + 1)
                pe.wait_ge(q_high, 2 * b + 2)
                for c in range(CH):
                    if c % 2 == 0:
                        pe.wait_ge(c_low, pairs * b + c // 2 + 3)
                    split_product(pe, score_bank[0:SEQ, 0:KEYS_EVEN], [q[:, c, :] for q in qp],
                                  [q[:, t, c, :] for q in ct], c == 0, False)
                pe.matmul(score_bank[0:SEQ, 0:KEYS_EVEN], qb[:, :], ones[:, :], start=False,
                          stop=True).then_inc(scored, 1)
                v_piece(0)
                pe.wait_ge(exped, b + 1)
                for kt in range(KEY_TILES):
                    mm = pe.transpose(turn_bank[0:KEY_TILE, kt * SEQ:(kt + 1) * SEQ],
                                      e[:, kt * KEY_TILE:(kt + 1) * KEY_TILE], k.ident[0:SEQ, 0:SEQ])
                mm.then_inc(e_turned, 1)
                v_piece(1)
                pe.wait_ge(e_staged, b + 1)
                pe.wait_ge(cn_in, 16 * b + 16)
                for h in range(2):
                    for kt in range(KEY_TILES):
                        mm = pe.matmul(row_banks[h][0:SEQ, :], et[:, kt, :],
                                       cn[0:KEY_TILE, kt, h * 512:(h + 1) * 512],
                                       start=(kt == 0), stop=(kt == KEY_TILES - 1))
                    mm.then_inc(attended, 1)
                v_piece(2)
                norm_turn(pe, s2, ln2, b, 0, xn_banks, k.ident)
                v_piece(3)
                pe.wait_ge(consts, 48)
                pe.wait_ge(s2.evacuated, 2 * b + 2)
                lora_mid(pe, sl, b, score_bank[0:SEQ], xnt, aw)
                v_piece(4)
                lora_turn(pe, sl, lora, b, turn_bank, k.ident, k.passed)
                lora_up(pe, sl, lora, b, [r[0:SEQ, :] for r in row_banks], bw)
                v_piece(5)
                norm_turn(pe, s3, ln3, b, 0, xn_banks, k.ident)

            batches(pe, batch)


def query1_phase(nc, k):
    with ExitStack() as ctx:
        sb, pair, sem = buffers_of(nc, ctx)
        bank = k.banks
        xn = pair("xn3", [P, CH, TOK])
        raw = sb("wq1_raw", [P, 2, CH, P])
        w = pair("wq1", [P, 2, CH, P])
        rope = sb("q_rope", [P, 2, SEQ])
        straight, crossed = sb("q_straight", [P, 2, HALF]), sb("q_crossed", [P, 2, HALF])
        rotated = sb("q_rotated_sb", [P, 4, HALF])

        consts = sem("d_consts")
        x_high, x_low = sem("d_x_high"), sem("d_x_low")
        w_in = [sem(f"d_w_in{i}") for i in range(2)]
        w_high = sem("d_w_high")
        w_low = sem("d_w_low")
        acc = sem("d_acc")
        read = sem("d_read")
        ready = sem("d_ready")
        stored = [sem(f"d_stored{i}") for i in range(4)]

        block = ctx.enter_context(nc.Block())

        @block.sync
        def _(sp):
            sp.dma_start(rope[:, :, :], k.rope_q).then_inc(consts, 16)

            def load_w(i, t):
                sp.wait_ge(w_low, 2 * i + t + 1)
                sp.dma_start(raw[:, t], k.wq1[2 * i + t]).then_inc(w_in[t], 16)

            def store(i):
                for t in range(2):
                    for h in range(2):
                        sp.wait_ge(ready, 4 * i + 2 * t + h + 3)
                        sp.dma_start(k.q_dram[2 * i + t, :, h * HALF:(h + 1) * HALF],
                                     rotated[:, 2 * t + h]).then_inc(stored[2 * t + h], 16)

            load_w(0, 0)
            load_w(0, 1)
            with sp.Fori(0, HEADS // 2 - 1) as i:
                load_w(i + 1, 0)
                load_w(i + 1, 1)
                store(i)
            store(HEADS // 2 - 1)
            for s in stored:
                sp.wait_ge(s, 16 + 16 * HEADS // 2)

        @block.scalar
        def _(act):
            for c in range(CH):
                act.activation(xn[0][:, c, :], k.qp[:, c, :], ACT.Copy).then_inc(x_high, 1)
            with act.Fori(0, HEADS // 2) as i:
                for t in range(2):
                    act.wait_ge(w_in[t], 16 * i + 16)
                    act.wait_ge(acc, 4 * i + 2 * t + 2)
                    act.activation(w[0][:, t], raw[:, t], ACT.Copy).then_inc(w_high, 1)

        @block.gpsimd
        def _(pool):
            pool.sem_inc(w_low, 2)
            with pool.Fori(0, HEADS // 2) as i:
                for t in range(2):
                    pool.wait_ge(w_high, 2 * i + t + 1)
                    pool.tensor_tensor(w[1][:, t], raw[:, t], f32(w[0][:, t]), ALU.subtract).then_inc(w_low, 1)

        @block.vector
        def _(dve):
            dve.sem_inc(read, 4)
            dve.sem_inc(ready, 2)
            for s in stored:
                dve.sem_inc(s, 16)
            for c in range(CH):
                dve.wait_ge(x_high, c + 1)
                dve.tensor_tensor(xn[1][:, c, :], k.qp[:, c, :], f32(xn[0][:, c, :]),
                                  ALU.subtract).then_inc(x_low, 1)
            dve.wait_ge(consts, 16)
            cos, sin = (rope[:, j, :].unsqueeze(1).broadcast_to([P, QUAD, SEQ]) for j in range(2))

            def by_batch(ap):
                return ap.rearrange("p (b t) -> p b t", b=QUAD)

            with dve.Fori(0, HEADS // 2) as i:
                for t in range(2):
                    for h in range(2):
                        n = 4 * i + 2 * t + h
                        dve.wait_ge(acc, n + 5)
                        dve.wait_ge(ready, n + 1)
                        rotate(dve, by_batch(bank[2 * t + h][:, 0:HALF]), cos, sin,
                               by_batch(straight[:, h]), by_batch(crossed[:, h])).then_inc(read, 1)
                        dve.wait_ge(read, n + 5)
                        dve.wait_ge(stored[2 * t + h], 16 * i + 16)
                        dve.tensor_tensor(rotated[:, 2 * t + h], straight[:, h], crossed[:, h],
                                          ALU.add).then_inc(ready, 1)

        @block.tensor
        def _(pe):
            pe.sem_inc(acc, 4)
            with pe.Fori(0, HEADS // 2) as i:
                for t in range(2):
                    pe.wait_ge(w_low, 2 * i + t + 3)
                    for h in range(2):
                        pe.wait_ge(read, 4 * i + 2 * t + h + 1)
                        for c in range(CH):
                            if t == 0 and h == 0:
                                pe.wait_ge(x_low, c + 1)
                            mm = split_product(pe, bank[2 * t + h][:, 0:HALF], [q[:, t, c, :] for q in w],
                                               [q[:, c, h * HALF:(h + 1) * HALF] for q in xn],
                                               c == 0, c == CH - 1)
                        mm.then_inc(acc, 1)


def attention_phase(nc, k):
    with ExitStack() as ctx:
        sb, pair, sem = buffers_of(nc, ctx)
        bank = k.banks
        s_bank, p_bank, o_bank, y_bank = bank[0:2], bank[2:5], bank[5], bank[6:8]
        H = PER_GROUP
        STEPS = GROUPS * BATCH
        raw_q, raw_k = sb("e_raw_q", [P, 2, H, SEQ]), sb("e_raw_k", [P, 2, KEYS_EVEN])
        raw_v = sb("e_raw_v", [KEY_TILE, 2, KEY_TILES, P])
        q, kt = pair("e_q", [P, 2, H, SEQ]), pair("e_k", [P, 2, KEYS_EVEN])
        v = pair("e_v", [KEY_TILE, 2, KEY_TILES, P])
        raw_wo = sb("e_raw_wo", [P, 2, H, 256])
        wo = pair("e_wo", [P, 4, H, 256])
        mask = sb("e_mask", [SEQ, BATCH, KEYS])
        s_buf = sb("e_scores", [SEQ, 2, H, KEYS])
        mx, nm = sb("e_max", [SEQ, 2, H]), sb("e_nmax", [SEQ, 2, H])
        total, inv = sb("e_total", [SEQ, 2, H]), sb("e_inv", [SEQ, 2, H])
        pt = pair("e_p_t", [KEY_TILE, KEY_TILES, H * SEQ])
        ot = pair("e_o_t", [P, 2, H, HALF])

        mask_in = sem("e_mask_in")
        q_in, k_in, v_in, wo_in = ([sem(f"e_{n}_in{i}") for i in range(2)] for n in ("q", "k", "v", "wo"))
        qk_high, qk_low = sem("e_qk_high"), sem("e_qk_low")
        v_high, v_low = sem("e_v_high"), sem("e_v_low")
        wo_high, wo_low = sem("e_wo_high"), sem("e_wo_low")
        scored, masked, negated, exped = sem("e_scored"), sem("e_masked"), sem("e_negated"), sem("e_exped")
        inverted, normed = sem("e_inverted"), sem("e_normed")
        turned, pt_high, pt_low = sem("e_turned"), sem("e_pt_high"), sem("e_pt_low")
        o_acc, o_high, o_low = sem("e_o_acc"), sem("e_o_high"), sem("e_o_low")
        y_acc = sem("e_y_acc")
        y_added = sem("e_y_added")

        block = ctx.enter_context(nc.Block())

        def steps(eng, step):
            for s in range(4):
                step(s, s, 0)
            with eng.Fori(0, GROUPS - 1) as j:
                for u in range(4, 12):
                    step(8 * j + u, u % 8, j + u // 8)
            for s in range(STEPS - 4, STEPS):
                step(s, s % 8, GROUPS - 1)

        def known(s):
            return isinstance(s, int)

        def half_of(s, u):
            return s // 2 if known(s) else (s - u % 2) // 2

        @block.sync
        def _(sp):
            sp.dma_start(mask[:, :, :], k.mask.rearrange("b q s -> q b s")).then_inc(mask_in, 16)

            def load_qk(s, b, g):
                if not (known(s) and s < 2):
                    sp.wait_ge(qk_low, 2 * s - 2)
                sp.dma_start(raw_q[:, b % 2], k.q_dram[bass.ds(H * g, H), :, b * SEQ:(b + 1) * SEQ].rearrange(
                    "h p t -> p h t")).then_inc(q_in[b % 2], 16)
                sp.dma_start(raw_k[:, b % 2], k.kt_dram[b, g]).then_inc(k_in[b % 2], 16)

            def load_v(s, b, g):
                if not (known(s) and s < 2):
                    sp.wait_ge(v_low, s - 1)
                sp.dma_start(raw_v[:, b % 2], k.v_dram[b, :, :, bass.ds(P * g, P)].rearrange(
                    "c p d -> p c d")).then_inc(v_in[b % 2], 16)

            def load_wo(b, g, first):
                if not (first and b < 2):
                    sp.wait_ge(wo_low, 4 * g + b - 1)
                sp.dma_start(raw_wo[:, b % 2], k.wo1[g, :, :, b * 256:(b + 1) * 256]).then_inc(wo_in[b % 2], 16)

            load_qk(0, 0, 0)
            load_qk(1, 1, 0)
            load_v(0, 0, 0)

            def step(s, u, g):
                last = known(s) and s >= STEPS - 4
                if not (last and s + 2 >= STEPS):
                    load_qk(s + 2, (u + 2) % 8, g + (u + 2) // 8)
                if not (last and s + 1 >= STEPS):
                    load_v(s + 1, (u + 1) % 8, g + (u + 1) // 8)
                if u < 4:
                    load_wo(u, g, known(s))

            steps(sp, step)

        @block.scalar
        def _(act):
            def copy(dst, src, done):
                act.activation(dst, src, ACT.Copy).then_inc(done, 1)

            def qk_split(s, u):
                t = u % 2
                act.wait_ge(q_in[t], 16 * half_of(s, u) + 16)
                if not (known(s) and s < 2):
                    act.wait_ge(scored, 4 * s - 4)
                copy(q[0][:, t], raw_q[:, t], qk_high)
                act.wait_ge(k_in[t], 16 * half_of(s, u) + 16)
                copy(kt[0][:, t], raw_k[:, t], qk_high)

            def v_split(s, u):
                t = u % 2
                act.wait_ge(v_in[t], 16 * half_of(s, u) + 16)
                if not (known(s) and s < 2):
                    act.wait_ge(o_acc, s - 1)
                copy(v[0][:, t], raw_v[:, t], v_high)

            def exps(s, u, heads):
                t = u % 2
                for h in heads:
                    act.wait_ge(negated, 4 * s + h + 1)
                    act.activation(s_buf[:, t, h, :], s_buf[:, t, h, :], ACT.Exp, bias=nm[:, t, h:h + 1],
                                   accum_out=total[:, t, h:h + 1]).then_inc(exped, 1)

            qk_split(0, 0)
            v_split(0, 0)
            exps(0, 0, range(H))
            qk_split(1, 1)

            def step(s, u, g):
                last = known(s) and s >= STEPS - 4
                more = not (last and s + 1 >= STEPS)
                for c in range(KEY_TILES):
                    act.wait_ge(turned, 3 * s + c + 1)
                    if not (known(s) and s < 1):
                        act.wait_ge(o_acc, s)
                    copy(pt[0][:, c, :], p_bank[c][0:KEY_TILE, 0:HALF], pt_high)
                if more:
                    exps(s + 1, (u + 1) % 8, (0, 1))
                if not (last and s + 2 >= STEPS):
                    qk_split(s + 2, (u + 2) % 8)
                if more:
                    exps(s + 1, (u + 1) % 8, (2, 3))
                    v_split(s + 1, (u + 1) % 8)
                act.wait_ge(o_acc, s + 1)
                copy(ot[0][:, (u // 4) % 2, :, (u % 4) * SEQ:(u % 4 + 1) * SEQ],
                     o_bank[:, 0:HALF].rearrange("p (h t) -> p h t", h=H), o_high)
                if u < 4:
                    act.wait_ge(wo_in[u % 2], 16 * (2 * g + u // 2) + 16)
                    if not (known(s) and s < 4):
                        act.wait_ge(y_acc, 2 * s - 6)
                    copy(wo[0][:, u], raw_wo[:, u % 2], wo_high)

            steps(act, step)

        @block.gpsimd
        def _(pool):
            def low(dst, src, high, done):
                pool.tensor_tensor(dst, src, f32(high), ALU.subtract).then_inc(done, 1)

            def qk_split(s, u):
                t = u % 2
                pool.wait_ge(qk_high, 2 * s + 1)
                low(q[1][:, t], raw_q[:, t], q[0][:, t], qk_low)
                pool.wait_ge(qk_high, 2 * s + 2)
                low(kt[1][:, t], raw_k[:, t], kt[0][:, t], qk_low)

            def v_split(s, u):
                t = u % 2
                pool.wait_ge(v_high, s + 1)
                low(v[1][:, t], raw_v[:, t], v[0][:, t], v_low)

            qk_split(0, 0)
            v_split(0, 0)
            qk_split(1, 1)

            def step(s, u, g):
                last = known(s) and s >= STEPS - 4
                if not (last and s + 2 >= STEPS):
                    qk_split(s + 2, (u + 2) % 8)
                if not (last and s + 1 >= STEPS):
                    v_split(s + 1, (u + 1) % 8)
                if u < 4:
                    pool.wait_ge(wo_high, 4 * g + u + 1)
                    low(wo[1][:, u], raw_wo[:, u % 2], wo[0][:, u], wo_low)

            steps(pool, step)

        def y_tile(s, u, t):
            return 2 * (u % 4) + t, (0 if u >= 4 else HALF)

        whole = 2 + 2 * (STEPS - 4)
        rounds, round_of_vectors, round_of_products = final_phase(nc, k, sb, sem, block, y_added,
                                                                  (whole, whole + 8))

        @block.vector
        def _(dve):
            dve.memset(k.yt[:, :, :], 0.0).then_inc(y_added, 2)
            dve.wait_ge(mask_in, 16)

            def mask_scores(s, u, heads):
                t = u % 2
                for h in heads:
                    dve.wait_ge(scored, 4 * s + h + 1)
                    if not (known(s) and s < 2):
                        dve.wait_ge(turned, 3 * s - 3)
                    take_waits(dve, k.passed)
                    dve.tensor_tensor_reduce(s_buf[:, t, h, :], s_bank[h % 2][0:SEQ, 0:KEYS], mask[:, u, :],
                                             1.0, LOWEST, ALU.add, ALU.max,
                                             mx[:, t, h:h + 1]).then_inc(masked, 1)
                    dve.wait_ge(masked, 4 * s + h + 1)
                    dve.tensor_scalar(nm[:, t, h:h + 1], mx[:, t, h:h + 1], -1.0, None,
                                      ALU.mult).then_inc(negated, 1)

            def normalise(s, u):
                t = u % 2
                dve.wait_ge(exped, 4 * s + 4)
                dve.reciprocal(inv[:, t, :], total[:, t, :]).then_inc(inverted, 1)
                dve.wait_ge(inverted, s + 1)
                for h in range(H):
                    dve.tensor_scalar(s_buf[:, t, h, :], s_buf[:, t, h, :], inv[:, t, h:h + 1], None,
                                      ALU.mult).then_inc(normed, 1)

            def add_y(s, u, t):
                tile, at = y_tile(s, u, t)
                dve.wait_ge(y_acc, 2 * s - 8 + t + 1)
                dve.wait_ge(y_added, 2 * s - 8 + t + 2)
                dve.tensor_tensor(k.yt[:, tile, at:at + HALF], y_bank[t][:, 0:HALF],
                                  k.yt[:, tile, at:at + HALF], ALU.add).then_inc(y_added, 1)

            mask_scores(0, 0, range(H))
            normalise(0, 0)

            def step(s, u, g):
                more = not (known(s) and s + 1 >= STEPS)
                adds = not (known(s) and s < 4)
                if more:
                    mask_scores(s + 1, (u + 1) % 8, (0, 1))
                for c in range(KEY_TILES):
                    dve.wait_ge(pt_high, 3 * s + c + 1)
                    dve.tensor_tensor(pt[1][:, c, :], p_bank[c][0:KEY_TILE, 0:HALF], f32(pt[0][:, c, :]),
                                      ALU.subtract).then_inc(pt_low, 1)
                if adds:
                    add_y(s, u, 0)
                if more:
                    mask_scores(s + 1, (u + 1) % 8, (2, 3))
                if adds:
                    add_y(s, u, 1)
                if more:
                    normalise(s + 1, (u + 1) % 8)
                dve.wait_ge(o_high, s + 1)
                at = (slice(None), (u // 4) % 2, slice(None), slice((u % 4) * SEQ, (u % 4 + 1) * SEQ))
                dve.tensor_tensor(ot[1][at], o_bank[:, 0:HALF].rearrange("p (h t) -> p h t", h=H),
                                  f32(ot[0][at]), ALU.subtract).then_inc(o_low, 1)

            steps(dve, step)
            for r in rounds:
                if r < 4:
                    add_y(STEPS + r, r, 0)
                    add_y(STEPS + r, r, 1)
                round_of_vectors(dve, r)

        @block.tensor
        def _(pe):
            def scores(s, u, heads):
                t = u % 2
                pe.wait_ge(qk_low, 2 * s + 2)
                for h in heads:
                    if not (known(s) and s < 1 and h < 2):
                        pe.wait_ge(masked, 4 * s + h - 1)
                    split_product(pe, s_bank[h % 2][0:SEQ, 0:KEYS_EVEN], [x[:, t, h, :] for x in q],
                                  [x[:, t, :] for x in kt], True, True).then_inc(scored, 1)

            def project(s, u, t):
                quad = 0 if u >= 4 else 1
                pe.wait_ge(o_low, s - u % 4)
                if u >= 4 and t == 0:
                    pe.wait_ge(wo_low, (s - u) // 2 + u - 3)
                pe.wait_ge(y_added, 2 * s - 8 + t + 1)
                for h in range(H):
                    mm = split_product(pe, y_bank[t][:, 0:HALF],
                                       [x[:, u % 4, h, t * P:(t + 1) * P] for x in wo],
                                       [x[:, quad, h, :] for x in ot], h == 0, h == H - 1)
                mm.then_inc(y_acc, 1)

            scores(0, 0, range(H))

            def step(s, u, g):
                more = not (known(s) and s + 1 >= STEPS)
                adds = not (known(s) and s < 4)
                t = u % 2
                if more:
                    scores(s + 1, (u + 1) % 8, (0, 1))
                pe.wait_ge(normed, 4 * s + 4)
                for c in range(KEY_TILES):
                    if not (known(s) and s < 1):
                        pe.wait_ge(pt_low, 3 * s - 3 + c + 1)
                    for h in range(H):
                        mm = pe.transpose(p_bank[c][0:KEY_TILE, h * SEQ:(h + 1) * SEQ],
                                          s_buf[:, t, h, c * KEY_TILE:(c + 1) * KEY_TILE],
                                          k.ident[0:SEQ, 0:SEQ])
                    mm.then_inc(turned, 1)
                if adds:
                    project(s, u, 0)
                if more:
                    scores(s + 1, (u + 1) % 8, (2, 3))
                if adds:
                    project(s, u, 1)
                pe.wait_ge(v_low, s + 1)
                if not (known(s) and s < 1):
                    pe.wait_ge(o_low, s)
                for c in range(KEY_TILES):
                    pe.wait_ge(pt_low, 3 * s + c + 1)
                    mm = split_product(pe, o_bank[:, 0:HALF], [x[:, t, c, :] for x in v],
                                       [x[:, c, :] for x in pt], c == 0, c == KEY_TILES - 1)
                mm.then_inc(o_acc, 1)

            steps(pe, step)
            for r in rounds:
                if r < 4:
                    project(STEPS + r, r, 0)
                    project(STEPS + r, r, 1)
                round_of_products(pe, r)


def final_phase(nc, k, sb, sem, block, y_added, y_of_quad):
    bank = k.banks
    y_banks, xn_banks, mid_bank, turn_bank, up_banks = bank[0:2], bank[2:4], bank[4], bank[5], bank[6:8]
    width = L1_EXPERTS * RANK + L1_EXPERTS
    SLOTS = 5
    xr = sb("f_x_rows", [SEQ, SLOTS, DIM])
    ln = NormBuffers(sb, "ln4", 2)
    xnt = sb("xn4_t", [P, 2, CH, SEQ])
    lora = LoraBuffers(sb, "lora1", L1_EXPERTS)
    aw, bw = sb("a1_sb", [P, CH, width]), sb("b1_sb", [L1_EXPERTS * RANK, DIM])
    tri = sb("tri1_sb", [SEQ, L1_EXPERTS, L1_EXPERTS])

    consts = sem("f_consts")
    moved = [sem(f"f_moved{i}") for i in range(SLOTS)]
    y_turned, x_summed = sem("f_y_turned"), sem("f_x_summed")
    s4, sl = NormSems(sem, "ln4"), LoraSems(sem, "lora1")
    rounds = range(BATCH + 3)

    def stage(r, n):
        return r - n if 0 <= r - n < BATCH else None

    @block.sync
    def _(sp):
        for dst, src in ((aw, k.a1), (tri, k.tri1)):
            sp.dma_start(dst[:, :, :], src).then_inc(consts, 16)
        sp.dma_start(bw[:, :], k.b1).then_inc(consts, 16)

        def load(b):
            if b >= SLOTS:
                sp.wait_ge(moved[b % SLOTS], 32 * (b // SLOTS))
            sp.dma_start(xr[:, b % SLOTS], k.x2_dram[b]).then_inc(moved[b % SLOTS], 16)

        for b in range(SLOTS):
            load(b)
        for b in range(BATCH):
            sp.wait_ge(sl.added, 2 * b + 2)
            sp.dma_start(k.out[b], xr[:, b % SLOTS]).then_inc(moved[b % SLOTS], 16)
            if b + SLOTS < BATCH:
                load(b + SLOTS)
        for i, s in enumerate(moved):
            sp.wait_ge(s, 32 * len(range(i, BATCH, SLOTS)))

    @block.scalar
    def _(act):
        for r in rounds:
            if (b := stage(r, 3)) is not None:
                act.wait_ge(sl.turned, b + 1)
                act.activation(lora.mwt[:, :], turn_bank[0:L1_EXPERTS * RANK, 0:SEQ],
                               ACT.Copy).then_inc(sl.staged, 1)
            if (b := stage(r, 1)) is not None:
                for j in range(2):
                    act.wait_ge(s4.turned, 2 * b + j + 1)
                    act.activation(xnt[:, b % 2, 4 * j:4 * j + 4, :],
                                   xn_banks[j][:, 0:HALF].rearrange("p (c t) -> p c t", c=4),
                                   ACT.Copy).then_inc(s4.evacuated, 1)

    @block.gpsimd
    def _(pool):
        for b in range(BATCH):
            norm_rstd(pool, s4, ln, b, b % 2, k.minus_half[:, :])

    def round_of_vectors(dve, r):
        if (b := stage(r, 0)) is not None:
            x = xr[:, b % SLOTS]
            dve.wait_ge(moved[b % SLOTS], 32 * (b // SLOTS) + 16)
            for h in range(2):
                dve.wait_ge(y_turned, 2 * b + h + 1)
                cols = slice(h * 512, (h + 1) * 512)
                dve.tensor_tensor(x[:, cols], y_banks[h][0:SEQ, :], x[:, cols],
                                  ALU.add).then_inc(x_summed, 1)
            dve.wait_ge(x_summed, 2 * b + 2)
            norm_moments(dve, s4, ln, b, b % 2, x, k.passed)
        if (b := stage(r, 1)) is not None:
            norm_apply(dve, s4, ln, b, b % 2, xr[:, b % SLOTS])
        if (b := stage(r, 2)) is not None:
            if b == 0:
                dve.wait_ge(consts, 48)
            lora_gates(dve, sl, lora, b, mid_bank[0:SEQ], tri[:, :, :], L1_TOP, False)
        if (b := stage(r, 3)) is not None:
            x = xr[:, b % SLOTS]
            for h in range(2):
                dve.wait_ge(sl.up, 2 * b + h + 1)
                cols = slice(h * 512, (h + 1) * 512)
                dve.tensor_tensor(x[:, cols], up_banks[h][0:SEQ, :], x[:, cols],
                                  ALU.add).then_inc(sl.added, 1)

    def round_of_products(pe, r):
        if (b := stage(r, 3)) is not None:
            if b == 0:
                pe.wait_ge(y_added, y_of_quad[1])
            lora_turn(pe, sl, lora, b, turn_bank, k.ident, k.passed)
        if (b := stage(r, 0)) is not None:
            pe.wait_ge(y_added, y_of_quad[b // QUAD])
            for h in range(2):
                if b:
                    pe.wait_ge(x_summed, 2 * b - 1 + h)
                for c in range(4):
                    mm = pe.transpose(y_banks[h][0:SEQ, c * P:(c + 1) * P],
                                      k.yt[:, 4 * h + c, b * SEQ:(b + 1) * SEQ], k.ident[:, :])
                mm.then_inc(y_turned, 1)
        if (b := stage(r, 2)) is not None:
            if b == 0:
                pe.wait_ge(consts, 48)
            pe.wait_ge(s4.evacuated, 2 * b + 2)
            if b:
                pe.wait_ge(sl.gated, 2 * b)
            lora_mid(pe, sl, b, mid_bank[0:SEQ], xnt[:, b % 2], aw)
        if (b := stage(r, 3)) is not None:
            if b:
                pe.wait_ge(sl.added, 2 * b)
            lora_up(pe, sl, lora, b, [x[0:SEQ, :] for x in up_banks], bw)
        if (b := stage(r, 1)) is not None:
            if b:
                pe.wait_ge(s4.evacuated, 2 * b)
            norm_turn(pe, s4, ln, b, b % 2, xn_banks, k.ident)

    return rounds, round_of_vectors, round_of_products


def rope_tables(positions, scale):
    import numpy as np
    half = P // 2
    inv_freq = (1.0 / np.float32(10000.0) ** (np.arange(0, P, 2, dtype=np.float32) / np.float32(P))).astype(np.float32)
    angle = (np.arange(positions, dtype=np.float32)[None, :] * inv_freq[:, None]).astype(np.float32)
    table = np.zeros((P, 2, positions), np.float64)
    table[:half, 0] = table[half:, 0] = np.cos(angle.astype(np.float64))
    table[:half, 1] = np.sin(angle.astype(np.float64))
    table[half:, 1] = -table[:half, 1]
    return (table * scale).astype(np.float32)


def kernel(x, ctx_4096, mask_BxSxS2_ff0, L0_xattn_Wq, L0_xattn_bq, L0_xattn_Wk, L0_xattn_bk, L0_ffn_A, L0_ffn_B,
           L0_ffn_Wr, L1_xattn_wq, L1_xattn_wk, L1_xattn_wv, L1_xattn_wo, L1_ffn_route_w, L1_ffn_A, L1_ffn_Bw):
    import numpy as np
    import concourse.bacc as bacc
    from concourse.bass_utils import run_bass_kernel_spmd

    def rows(a):
        return np.ascontiguousarray(a)

    ctx = np.asarray(ctx_4096)
    ctx_t = np.zeros((BATCH, P, CH, KEYS_EVEN), ctx.dtype)
    ctx_t[..., :KEYS] = ctx.transpose(0, 2, 1).reshape(BATCH, CH, P, KEYS).transpose(0, 2, 1, 3)

    def tiles(w):
        w = np.asarray(w)
        return rows(w.reshape(CH, P, w.shape[1] // P, P).transpose(2, 1, 0, 3))

    def down(a, router):
        a, router = np.asarray(a), np.asarray(router)
        both = np.concatenate([a.reshape(-1, DIM), router], axis=0)
        return rows(both.T.reshape(CH, P, -1).transpose(1, 0, 2))

    def up(b):
        return rows(np.asarray(b).transpose(0, 2, 1).reshape(-1, DIM))

    def triangle(experts):
        t = np.tril(np.ones((experts, experts), np.float32), -1)
        return rows(np.broadcast_to(t, (SEQ, experts, experts)))

    wo = np.asarray(L1_xattn_wo).reshape(GROUPS, PER_GROUP, P, DIM).transpose(0, 2, 1, 3)
    arrays = dict(
        x=rows(x), ctx_nat=rows(ctx), ctx_t=ctx_t, mask=rows(mask_BxSxS2_ff0),
        wq0_t=tiles(np.asarray(L0_xattn_Wq).T), wk0=tiles(L0_xattn_Wk),
        bq=rows(np.asarray(L0_xattn_bq).reshape(CH, P).T), bk=rows(np.asarray(L0_xattn_bk).reshape(CH, P).T),
        a0=down(L0_ffn_A, L0_ffn_Wr), b0=up(L0_ffn_B),
        wq1=tiles(L1_xattn_wq), wk1=tiles(L1_xattn_wk),
        wv1=rows(np.asarray(L1_xattn_wv).reshape(CH, P, DIM).transpose(1, 0, 2)), wo1=rows(wo),
        a1=down(L1_ffn_A, L1_ffn_route_w), b1=up(L1_ffn_Bw),
        rope_q=rope_tables(SEQ, float(P) ** -0.5), rope_k=rope_tables(KEYS_EVEN, 1.0),
        ident_in=np.eye(P, dtype=np.float32), tri0_in=triangle(L0_EXPERTS), tri1_in=triangle(L1_EXPERTS))
    nc = bacc.Bacc("TRN2", target_bir_lowering=False, num_devices=1)
    args = {n: nc.dram_tensor(f"in_{n}", a.shape, mybir.dt.from_np(a.dtype), kind="ExternalInput").ap()
            for n, a in arrays.items()}
    out = nc.dram_tensor("out_0", (BATCH, SEQ, DIM), F32, kind="ExternalOutput").ap()
    build(nc, out=out, **args)
    r = run_bass_kernel_spmd(nc, [{f"in_{n}": a for n, a in arrays.items()}], core_ids=[0])
    return r.results[0]["out_0"]
```

```python
from contextlib import ExitStack

import concourse.bass as bass
from concourse import mybir

F32 = mybir.dt.float32
F32R = mybir.dt.float32r
ALU = mybir.AluOpType
ACT = mybir.ActivationFunctionType
AX = mybir.AxisListType.X

P = 128
BATCH, SEQ, DIM = 8, 112, 1024
KEYS = 375
KEYS_EVEN = 376
KEY_TILES, KEY_TILE = 3, 125
CH = DIM // P
TOK = BATCH * SEQ
HALF = TOK // 2
QUAD = HALF // SEQ
GROUPS, PER_GROUP = 8, 4
HEADS = GROUPS * PER_GROUP
L0_EXPERTS, L0_TOP = 4, 2
L1_EXPERTS, L1_TOP = 8, 1
RANK = 16
L0_SCALE = 4.0
EPS = 1e-5
X_SLOTS = 5
LOWEST = -3.4028234663852886e38
PASSES = ((0, 0), (0, 1), (1, 0))


class Shared:
    pass


def f32(ap):
    return ap.bitcast(F32)


def take_waits(eng, passed):
    eng.sem_inc(passed, 1)


class NormSems:
    def __init__(self, sem, name):
        self.moments = sem(f"{name}_moments")
        self.rstd = sem(f"{name}_rstd")
        self.normed = sem(f"{name}_normed")
        self.turned = sem(f"{name}_turned")
        self.evacuated = sem(f"{name}_evac")


class NormBuffers:
    def __init__(self, sb, name, slots):
        self.stats = sb(f"{name}_stats", [SEQ, slots, 2, 6])
        self.mv = sb(f"{name}_mv", [SEQ, slots, 2])
        self.ve = sb(f"{name}_ve", [SEQ, slots])
        self.rstd = sb(f"{name}_rstd", [SEQ, slots])
        self.xn = sb(f"{name}_xn", [SEQ, slots, DIM])


def norm_moments(dve, s, buf, n, k, x, passed):
    for h in range(2):
        dve.bn_stats(buf.stats[:, k, h, :], x[:, h * 512:(h + 1) * 512]).then_inc(s.moments, 1)
    dve.wait_ge(s.moments, 4 * n + 2)
    take_waits(dve, passed)
    dve.bn_aggr(buf.mv[:, k, :], buf.stats[:, k]).then_inc(s.moments, 1)
    dve.wait_ge(s.moments, 4 * n + 3)
    dve.tensor_scalar(buf.ve[:, k:k + 1], buf.mv[:, k, 1:2], EPS, None, ALU.add).then_inc(s.moments, 1)


def norm_rstd(pool, s, buf, n, k, minus_half):
    pool.wait_ge(s.moments, 4 * n + 4)
    pool.tensor_tensor(buf.rstd[:, k:k + 1], buf.ve[:, k:k + 1], minus_half, ALU.pow).then_inc(s.rstd, 1)


def norm_apply(dve, s, buf, n, k, x):
    dve.wait_ge(s.rstd, n + 1)
    dve.tensor_scalar(buf.xn[:, k, :], x, buf.mv[:, k, 0:1], buf.rstd[:, k:k + 1],
                      ALU.subtract, ALU.mult).then_inc(s.normed, 1)


def norm_turn(pe, s, buf, n, k, banks, ident):
    pe.wait_ge(s.normed, n + 1)
    for j in range(2):
        for c in range(4):
            ch = 4 * j + c
            last = pe.transpose(banks[j][:, c * SEQ:(c + 1) * SEQ], buf.xn[:, k, ch * P:(ch + 1) * P],
                                ident[0:SEQ, 0:SEQ])
        last.then_inc(s.turned, 1)


class LoraSems:
    def __init__(self, sem, name):
        self.mid = sem(f"{name}_mid")
        self.chain = sem(f"{name}_chain")
        self.gate_exp = sem(f"{name}_gexp")
        self.gated = sem(f"{name}_gated")
        self.turned = sem(f"{name}_mturned")
        self.staged = sem(f"{name}_staged")
        self.up = sem(f"{name}_up")
        self.added = sem(f"{name}_added")


class LoraBuffers:
    def __init__(self, sb, name, experts):
        self.e = e = experts
        self.lg = sb(f"{name}_lg", [SEQ, e])
        self.gt = sb(f"{name}_gt", [SEQ, e, e])
        self.eq = sb(f"{name}_eq", [SEQ, e, e])
        self.rank = sb(f"{name}_rank", [SEQ, e])
        self.sel = sb(f"{name}_sel", [SEQ, e])
        self.nmax = sb(f"{name}_nmax", [SEQ, 1])
        self.ex = sb(f"{name}_ex", [SEQ, e])
        self.exs = sb(f"{name}_exs", [SEQ, e])
        self.tot = sb(f"{name}_tot", [SEQ, 1])
        self.inv = sb(f"{name}_inv", [SEQ, 1])
        self.gate = sb(f"{name}_gate", [SEQ, e])
        self.mw = sb(f"{name}_mw", [SEQ, e * RANK])
        self.mwt = sb(f"{name}_mwt", [e * RANK, SEQ])


def lora_gates(dve, s, buf, n, mid, tri, top, softmax):
    e = buf.e
    steps = 11 if softmax else 7
    base = steps * n
    first = e * RANK
    over = [SEQ, e, e]
    dve.wait_ge(s.mid, n + 1)
    dve.tensor_copy(buf.lg[:, :], mid[:, first:first + e]).then_inc(s.chain, 1)
    other = buf.lg[:, :].unsqueeze(1).broadcast_to(over)
    own = buf.lg[:, :].unsqueeze(2).broadcast_to(over)
    dve.wait_ge(s.chain, base + 1)
    dve.tensor_tensor(buf.gt[:, :, :], other, own, ALU.is_gt).then_inc(s.chain, 1)
    dve.tensor_tensor(buf.eq[:, :, :], other, own, ALU.is_equal).then_inc(s.chain, 1)
    dve.wait_ge(s.chain, base + 3)
    dve.tensor_tensor(buf.eq[:, :, :], buf.eq[:, :, :], tri, ALU.mult).then_inc(s.chain, 1)
    dve.wait_ge(s.chain, base + 4)
    dve.tensor_tensor(buf.gt[:, :, :], buf.gt[:, :, :], buf.eq[:, :, :], ALU.add).then_inc(s.chain, 1)
    dve.wait_ge(s.chain, base + 5)
    dve.tensor_reduce(buf.rank[:, :], buf.gt[:, :, :], AX, ALU.add).then_inc(s.chain, 1)
    dve.wait_ge(s.chain, base + 6)
    if softmax:
        dve.tensor_scalar(buf.sel[:, :], buf.rank[:, :], float(top), None, ALU.is_lt).then_inc(s.chain, 1)
        dve.tensor_reduce(buf.nmax[:, :], buf.lg[:, :], AX, ALU.max, negate=True).then_inc(s.chain, 1)
        dve.wait_ge(s.chain, base + 8)
        dve.wait_ge(s.gate_exp, n + 1)
        dve.tensor_tensor(buf.exs[:, :], buf.ex[:, :], buf.sel[:, :], ALU.mult).then_inc(s.chain, 1)
        dve.wait_ge(s.chain, base + 9)
        dve.tensor_reduce(buf.tot[:, :], buf.exs[:, :], AX, ALU.add).then_inc(s.chain, 1)
        dve.wait_ge(s.chain, base + 10)
        dve.reciprocal(buf.inv[:, :], buf.tot[:, :]).then_inc(s.chain, 1)
        dve.wait_ge(s.chain, base + 11)
        dve.tensor_scalar(buf.gate[:, :], buf.exs[:, :], buf.inv[:, 0:1], L0_SCALE,
                          ALU.mult, ALU.mult).then_inc(s.gated, 1)
    else:
        dve.tensor_scalar(buf.sel[:, :], buf.rank[:, :], float(top), None, ALU.is_lt).then_inc(s.chain, 1)
        dve.wait_ge(s.chain, base + 7)
        dve.tensor_tensor(buf.gate[:, :], buf.lg[:, :], buf.sel[:, :], ALU.mult).then_inc(s.gated, 1)
    dve.wait_ge(s.gated, 2 * n + 1)
    dve.tensor_tensor(buf.mw[:, :].rearrange("t (e r) -> t e r", e=e),
                      mid[:, 0:first].rearrange("t (e r) -> t e r", e=e),
                      buf.gate[:, :].unsqueeze(2).broadcast_to([SEQ, e, RANK]), ALU.mult).then_inc(s.gated, 1)


def lora_mid(pe, s, n, mid, xnt, aw):
    width = aw.shape[-1]
    for c in range(CH):
        last = pe.matmul(mid[:, 0:width], xnt[:, c, :], aw[:, c, :], start=(c == 0), stop=(c == CH - 1))
    last.then_inc(s.mid, 1)


def lora_turn(pe, s, buf, n, bank, ident, passed):
    pe.wait_ge(s.gated, 2 * n + 2)
    take_waits(pe, passed)
    pe.transpose(bank[0:buf.e * RANK, 0:SEQ], buf.mw[:, :], ident[0:SEQ, 0:SEQ]).then_inc(s.turned, 1)


def lora_up(pe, s, buf, n, banks, bw):
    pe.wait_ge(s.staged, n + 1)
    for h in range(2):
        pe.matmul(banks[h], buf.mwt[:, :], bw[:, h * 512:(h + 1) * 512],
                  start=True, stop=True).then_inc(s.up, 1)


def split_product(pe, out, stationary, moving, first, last):
    for i, (a, b) in enumerate(PASSES):
        mm = pe.matmul(out, stationary[a], moving[b], start=(first and i == 0),
                       stop=(last and i == 2))
    return mm


def build(nc, x, ctx_nat, ctx_t, mask, wq0_t, wk0, bq, bk, a0, b0, wq1, wk1, wv1, wo1, a1, b1,
          rope_q, rope_k, ident_in, tri0_in, tri1_in, out):
    kt_dram = nc.dram_tensor("k_rotated", (BATCH, GROUPS, P, KEYS_EVEN), F32, kind="Internal").ap()
    v_dram = nc.dram_tensor("v_rows", (BATCH, KEY_TILES, KEY_TILE, DIM), F32, kind="Internal").ap()
    q_dram = nc.dram_tensor("q_rotated", (HEADS, P, TOK), F32, kind="Internal").ap()
    x2_dram = nc.dram_tensor("x_after_layer0", (BATCH, SEQ, DIM), F32, kind="Internal").ap()
    with ExitStack() as outer:
        def sb(name, shape, dt=F32, ctx=outer):
            return ctx.enter_context(nc.sbuf_tensor(name, shape, dt))

        def sem(name, ctx=outer):
            return ctx.enter_context(nc.semaphore(name))

        banks = [outer.enter_context(nc.psum_tensor(f"bank{i}", [P, 512], F32)) for i in range(8)]
        k = Shared()
        k.x, k.ctx_nat, k.ctx_t, k.mask, k.ident_in, k.out = x, ctx_nat, ctx_t, mask, ident_in, out
        k.wq0_t, k.wk0, k.bq, k.bk = wq0_t, wk0, bq, bk
        k.wq1, k.wk1, k.wv1, k.wo1 = wq1, wk1, wv1, wo1
        k.a0, k.b0, k.a1, k.b1, k.tri0, k.tri1 = a0, b0, a1, b1, tri0_in, tri1_in
        k.rope_q, k.rope_k = rope_q, rope_k
        k.kt_dram, k.v_dram, k.q_dram, k.x2_dram = kt_dram, v_dram, q_dram, x2_dram
        k.banks, k.passed = banks, sem("passed")
        k.ident, k.minus_half = sb("ident", [P, P]), sb("minus_half", [SEQ, 1])
        with ExitStack() as heads, ExitStack() as layer0:
            k.qp = sb("qp_then_xn3", [P, CH, TOK], ctx=layer0)
            k.qb = sb("q_dot_bk", [1, TOK], ctx=layer0)
            share_operands(nc, k, layer0)
            query_phase(nc, k)
            with ExitStack() as context:
                keep, keep_pair, keep_sem = buffers_of(nc, context)
                k.w_rest = keep_pair("w_rest", [P, CH - 2, DIM])
                k.k_rotated = keep("k_rotated_sb", [P, 4, KEYS_EVEN])
                k.k_stored = [keep_sem(f"k_stored{i}") for i in range(4)]
                key_phase(nc, k)
                layer0_phase(nc, k)
            first = AttentionSteps(nc, heads, k)
            query1_phase(nc, k, first)
            layer0.close()
            attention_phase(nc, k, first)


def share_operands(nc, k, ctx):
    sb, pair, sem = buffers_of(nc, ctx)
    both = pair("shared_operand", [P, CH * TOK])
    slot, half = CH * KEYS_EVEN, CH * HALF
    k.xn1 = [x[:, :].rearrange("p (c t) -> p c t", c=CH) for x in both]
    k.ctx_ring = [[x[:, at:at + slot].rearrange("p (c k) -> p c k", c=CH) for at in (0, 2 * half - slot)]
                  for x in both]
    k.qp_split = [x[:, slot:slot + CH * SEQ].rearrange("p (c t) -> p c t", c=CH) for x in both]
    k.qb_split = [x[0:1, slot + CH * SEQ:slot + (CH + 1) * SEQ] for x in both]
    k.xn3 = [[x[:, h * half:(h + 1) * half].rearrange("p (c t) -> p c t", c=CH) for h in range(2)] for x in both]
    k.raw = sb("raw_weights_then_ctx_rows", [P, KEY_TILES, DIM])
    k.w_first = pair("w_first", [P, 2, DIM])
    k.c_raw = sb("ctx_raw", [P, 2, 2, KEYS_EVEN])


def weight_tile(k, n):
    return [x[:, n] for x in k.w_first] if n < 2 else [x[:, n - 2] for x in k.w_rest]


def split_ctx_high(act, k, j, slot, done):
    act.activation(k.ctx_ring[0][slot][:, 2 * j:2 * j + 2, :], k.c_raw[:, j % 2], ACT.Copy).then_inc(done, 1)


def split_ctx_low(pool, k, j, slot, done):
    pool.tensor_tensor(k.ctx_ring[1][slot][:, 2 * j:2 * j + 2, :], k.c_raw[:, j % 2],
                       f32(k.ctx_ring[0][slot][:, 2 * j:2 * j + 2, :]), ALU.subtract).then_inc(done, 1)


def buffers_of(nc, ctx, side="left"):
    def sb(name, shape, dt=F32):
        return ctx.enter_context(nc.sbuf_tensor(name, shape, dt, side=side))

    def pair(name, shape):
        return [ctx.enter_context(nc.sbuf_tensor(f"{name}_{p}", shape, F32R, side=side)) for p in ("high", "low")]

    def sem(name):
        return ctx.enter_context(nc.semaphore(name))

    return sb, pair, sem


def query_phase(nc, k):
    with ExitStack() as ctx:
        sb, pair, sem = buffers_of(nc, ctx)
        bank = k.banks
        XS = 4
        x_rows = sb("b_x_rows", [SEQ, XS, DIM])
        ln = NormBuffers(sb, "ln1", 2)
        xn, raw = k.xn1, k.raw
        qt = pair("q0_t", [P, CH, TOK])
        w = [x[:, :, :].rearrange("p s (c m) -> p s c m", c=CH) for x in k.w_first]
        bq_sb, bk_sb = sb("bq_sb", [P, CH]), sb("bk_sb", [P, CH])
        dots = sb("q_dot_terms", [P, TOK])
        ones = sb("b_ones", [P, P])

        consts = sem("b_consts")
        x_in = [sem(f"b_x_in{i}") for i in range(XS)]
        s1 = NormSems(sem, "ln1")
        xn_low = sem("b_xn_low")
        w_in = [sem(f"b_w_in{i}") for i in range(2)]
        w_high = sem("b_w_high")
        w_low = sem("b_w_low")
        acc = sem("b_acc")
        q_high = sem("b_q_high")
        q_done = sem("b_q_done")
        dotted = sem("b_dotted")
        ones_set, half_set = sem("b_ones_set"), sem("b_half_set")
        qb_acc = sem("b_qb_acc")
        c_in = [sem(f"b_c_in{i}") for i in range(2)]
        c_high, c_low = sem("b_c_high"), sem("b_c_low")
        FIRST = ((0, 0), (1, 0), (0, 1), (1, 1))

        block = ctx.enter_context(nc.Block())

        @block.sync
        def _(sp):
            def load_x(n):
                if n >= XS:
                    sp.wait_ge(s1.normed, n - XS + 1)
                sp.dma_start(x_rows[:, n % XS, :], k.x[n]).then_inc(x_in[n % XS], 16)

            def load_w(tiles, i, n, slot):
                sp.wait_ge(w_low, n + 1)
                sp.dma_start(raw[:, slot], tiles[i].rearrange("p c m -> p (c m)")).then_inc(w_in[slot], 16)

            load_x(0)
            load_x(1)
            sp.dma_start(k.ident[:, :], k.ident_in).then_inc(consts, 16)
            sp.dma_start(bq_sb[:, :], k.bq).then_inc(consts, 16)
            sp.dma_start(bk_sb[:, :], k.bk).then_inc(consts, 16)
            load_w(k.wq0_t, 0, 0, 0)
            load_w(k.wq0_t, 1, 1, 1)
            for n in range(2, BATCH):
                load_x(n)
            with sp.Fori(1, CH // 2) as i:
                for slot in range(2):
                    load_w(k.wq0_t, 2 * i + slot, 2 * i + slot, slot)
            with sp.Fori(0, CH // 2) as i:
                for slot in range(2):
                    load_w(k.wk0, 2 * i + slot, 2 * i + slot + CH, slot)
            for j in range(CH // 2):
                if j >= 2:
                    sp.wait_ge(c_low, j - 1)
                sp.dma_start(k.c_raw[:, j % 2], k.ctx_t[0, :, 2 * j:2 * j + 2, :]).then_inc(c_in[j % 2], 16)
            load_w(k.wk1, 0, 2 * CH, 0)
            load_w(k.wk1, 1, 2 * CH + 1, 1)
            sp.wait_ge(w_in[1], 16 * CH + 16)

        @block.scalar
        def _(act):
            def weight_high(i, slot, used):
                act.wait_ge(w_in[slot], 16 * i + 16)
                act.wait_ge(acc, used)
                act.activation(k.w_first[0][:, slot], raw[:, slot], ACT.Copy).then_inc(w_high, 1)

            def rows_high(n):
                for j in range(2):
                    act.wait_ge(s1.turned, 2 * n + j + 1)
                    act.activation(xn[0][:, 4 * j:4 * j + 4, SEQ * n:SEQ * (n + 1)],
                                   bank[4 + 2 * (n % 2) + j][:, 0:HALF].rearrange("p (c t) -> p c t", c=4),
                                   ACT.Copy).then_inc(s1.evacuated, 1)

            def query_high(unit, i, t, h):
                act.wait_ge(acc, unit + 5)
                take_waits(act, k.passed)
                act.activation(qt[0][:, bass.ds(2 * i + t, 1), h * HALF:(h + 1) * HALF],
                               bank[2 * t + h][:, 0:HALF].unsqueeze(1), ACT.Identity,
                               bias=bq_sb[:, bass.ds(2 * i + t, 1)]).then_inc(q_high, 1)

            weight_high(0, 0, 4)
            weight_high(0, 1, 4)
            for n in range(QUAD):
                rows_high(n)
            act.wait_ge(consts, 48)
            query_high(0, 0, *FIRST[0])
            rows_high(QUAD)
            rows_high(QUAD + 1)
            query_high(1, 0, *FIRST[1])
            rows_high(QUAD + 2)
            rows_high(QUAD + 3)
            query_high(2, 0, *FIRST[2])
            weight_high(1, 0, 7)
            query_high(3, 0, *FIRST[3])
            weight_high(1, 1, 8)
            with act.Fori(1, CH // 2) as i:
                for t in range(2):
                    for h in range(2):
                        query_high(4 * i + 2 * t + h, i, t, h)
                    weight_high(i + 1, t, 4 * i + 2 * t + 6)
            with act.Fori(CH // 2 + 1, CH - 1) as i:
                for t in range(2):
                    weight_high(i, t, 4 * i + 2 * t + 2)
            for t in range(2):
                weight_high(CH - 1, t, 4 * (CH - 1) + 2 * t + 2)
                for j in (2 * t, 2 * t + 1):
                    act.wait_ge(c_in[j % 2], 16 * (j // 2) + 16)
                    split_ctx_high(act, k, j, 0, c_high)
            weight_high(CH, 0, 4 * CH + 2)
            act.wait_ge(qb_acc, 2)
            for h in range(2):
                act.activation(k.qb[0:1, h * HALF:(h + 1) * HALF], bank[4 + h][0:1, 0:HALF], ACT.Copy,
                               scale=1.0 / 32.0)

        @block.gpsimd
        def _(pool):
            pool.sem_inc(w_low, 2)
            pool.memset(k.minus_half[:, :], -0.5).then_inc(half_set, 1)
            pool.wait_ge(half_set, 1)

            def weight_low(i, slot):
                pool.wait_ge(w_high, 2 * i + slot + 1)
                pool.tensor_tensor(k.w_first[1][:, slot], raw[:, slot], f32(k.w_first[0][:, slot]),
                                   ALU.subtract).then_inc(w_low, 1)

            for n in range(BATCH):
                norm_rstd(pool, s1, ln, n, n % 2, k.minus_half[:, :])
                if n in (1, 3):
                    weight_low(0, n // 2)
            with pool.Fori(1, CH - 1) as i:
                for slot in range(2):
                    weight_low(i, slot)
            for t in range(2):
                weight_low(CH - 1, t)
                for j in (2 * t, 2 * t + 1):
                    pool.wait_ge(c_high, j + 1)
                    split_ctx_low(pool, k, j, 0, c_low)
            weight_low(CH, 0)

        @block.vector
        def _(dve):
            dve.sem_inc(q_done, 4)
            dve.sem_inc(xn_low, 4)
            dve.memset(ones[:, :], 1.0).then_inc(ones_set, 1)
            dve.memset(dots[:, :], 0.0).then_inc(dotted, 1)

            def moments(n):
                dve.wait_ge(x_in[n % XS], 16 * (n // XS) + 16)
                norm_moments(dve, s1, ln, n, n % 2, x_rows[:, n % XS, :], k.passed)

            def rows_low(n):
                for j in range(2):
                    dve.wait_ge(s1.evacuated, 2 * n + j + 1)
                    at = slice(SEQ * n, SEQ * (n + 1))
                    dve.tensor_tensor(xn[1][:, 4 * j:4 * j + 4, at],
                                      bank[4 + 2 * (n % 2) + j][:, 0:HALF].rearrange("p (c t) -> p c t", c=4),
                                      f32(xn[0][:, 4 * j:4 * j + 4, at]), ALU.subtract).then_inc(xn_low, 1)

            moments(0)
            for n in range(BATCH):
                if n + 1 < BATCH:
                    moments(n + 1)
                if n >= 2:
                    dve.wait_ge(s1.turned, 2 * n - 2)
                norm_apply(dve, s1, ln, n, n % 2, x_rows[:, n % XS, :])
                if n >= 1:
                    rows_low(n - 1)
            rows_low(BATCH - 1)

            def query_low(unit, i, t, h):
                cols = slice(h * HALF, (h + 1) * HALF)
                at = (slice(None), bass.ds(2 * i + t, 1), cols)
                dve.wait_ge(q_high, unit + 1)
                dve.scalar_tensor_tensor(
                    out=qt[1][at], in0=bank[2 * t + h][:, 0:HALF].unsqueeze(1),
                    scalar=bq_sb[:, bass.ds(2 * i + t, 1)], in1=f32(qt[0][at]),
                    op0=ALU.add, op1=ALU.subtract).then_inc(q_done, 1)
                for part in range(2):
                    if part == 1:
                        dve.wait_ge(q_done, unit + 5)
                    dve.wait_ge(dotted, 2 * unit + part + 1)
                    dve.scalar_tensor_tensor(
                        out=dots[:, cols].unsqueeze(1), in0=f32(qt[part][at]),
                        scalar=bk_sb[:, bass.ds(2 * i + t, 1)], in1=dots[:, cols].unsqueeze(1),
                        op0=ALU.mult, op1=ALU.add).then_inc(dotted, 1)

            for unit, (t, h) in enumerate(FIRST):
                query_low(unit, 0, t, h)
            with dve.Fori(1, CH // 2) as i:
                for t in range(2):
                    for h in range(2):
                        query_low(4 * i + 2 * t + h, i, t, h)
            with dve.Fori(0, CH // 2) as i:
                for t in range(2):
                    for h in range(2):
                        dve.wait_ge(acc, 4 * i + 2 * t + h + 5 + 2 * CH)
                        dve.tensor_scalar(k.qp[:, bass.ds(2 * i + t, 1), h * HALF:(h + 1) * HALF],
                                          bank[2 * t + h][:, 0:HALF].unsqueeze(1), 1.0 / 32.0, None,
                                          ALU.mult).then_inc(q_done, 1)

        @block.tensor
        def _(pe):
            pe.sem_inc(acc, 4)
            pe.wait_ge(consts, 48)

            def turn(n):
                pe.wait_ge(xn_low, 2 * n + 2)
                norm_turn(pe, s1, ln, n, n % 2, bank[4 + 2 * (n % 2):6 + 2 * (n % 2)], k.ident)

            def half_tile(unit, t, h, moving, early=False):
                pe.wait_ge(q_done, unit + (2 if (t, h) == (0, 1) else 1))
                for c in range(CH):
                    if early and c == CH - 1:
                        pe.wait_ge(q_done, 4 + 2 * CH - 1 + h)
                    mm = split_product(pe, bank[2 * t + h][:, 0:HALF], [p[:, t, c, :] for p in w],
                                       [p[:, c, h * HALF:(h + 1) * HALF] for p in moving],
                                       c == 0, c == CH - 1)
                mm.then_inc(acc, 1)

            def tiles(i, first_tile, moving, early=False):
                for t in range(2):
                    n = 2 * i + t + first_tile
                    pe.wait_ge(w_low, n + 3)
                    for h in range(2):
                        half_tile(2 * n + h, t, h, moving, early and t == 0)

            for n in range(QUAD):
                turn(n)
            for unit, (t, h) in enumerate(FIRST):
                pe.wait_ge(w_low, t + 3)
                pe.wait_ge(xn_low, 4 + (1 + h) * BATCH)
                half_tile(unit, t, h, xn)
                if h == 0:
                    turn(QUAD + 2 * t)
                    turn(QUAD + 2 * t + 1)
            with pe.Fori(1, CH // 2) as i:
                tiles(i, 0, xn)
            pe.wait_ge(q_done, 4 + 2 * CH - 2)
            tiles(0, CH, qt, True)
            with pe.Fori(1, CH // 2) as i:
                tiles(i, CH, qt)
            pe.wait_ge(ones_set, 1)
            for h in range(2):
                pe.wait_ge(dotted, 1 + 4 * CH)
                pe.matmul(bank[4 + h][:, 0:HALF], ones[:, :], dots[:, h * HALF:(h + 1) * HALF],
                          start=True, stop=True).then_inc(qb_acc, 1)


def key_phase(nc, k):
    with ExitStack() as ctx:
        sb, pair, sem = buffers_of(nc, ctx)
        bank = k.banks
        rope = sb("k_rope", [P, 2, KEYS_EVEN])
        straight, crossed = sb("k_straight", [P, 2, KEYS_EVEN]), sb("k_crossed", [P, 2, KEYS_EVEN])
        rotated, stored = k.k_rotated, k.k_stored

        consts = sem("k_consts")
        w_in = [sem(f"k_w_in{i}") for i in range(3)]
        w_high = sem("k_w_high")
        w_low = sem("k_w_low")
        c_in = [sem(f"k_c_in{i}") for i in range(2)]
        c_high = sem("k_c_high")
        c_low = sem("k_c_low")
        q_high = sem("k_q_high")
        q_low = sem("k_q_low")
        acc = sem("k_acc")
        read = sem("k_read")
        ready = sem("k_ready")

        block = ctx.enter_context(nc.Block())
        pairs = CH // 2

        def two_by_two(eng, batch):
            with eng.Fori(0, BATCH // 2) as i:
                batch(2 * i + 1, 1)
                batch(2 * i + 2, 0)

        @block.sync
        def _(sp):
            def load_ctx(b, source, js=range(pairs)):
                for j in js:
                    sp.wait_ge(c_low, pairs * (b - 1) + j + 1)
                    sp.dma_start(k.c_raw[:, j % 2], k.ctx_t[source, :, 2 * j:2 * j + 2, :]).then_inc(
                        c_in[j % 2], 16)

            def store_head(b, g):
                sp.wait_ge(ready, GROUPS * b + g + 3)
                sp.dma_start(k.kt_dram[b, g], rotated[:, g % 4]).then_inc(stored[g % 4], 16)

            def store(b):
                for g in range(GROUPS):
                    store_head(b, g)

            def load_wv(c):
                sp.wait_ge(w_low, GROUPS + 1 if c < 3 else GROUPS + c - 1)
                sp.dma_start(k.raw[:, c % 3], k.wv1[:, c, :]).then_inc(w_in[c % 3], 16)

            with sp.Fori(0, GROUPS // 2 - 1) as i:
                for t in range(2):
                    sp.wait_ge(w_low, 2 * i + t + 2)
                    sp.dma_start(k.raw[:, t], k.wk1[2 * i + t + 2].rearrange("p c m -> p (c m)")).then_inc(
                        w_in[t], 16)
            sp.dma_start(rope[:, :, :], k.rope_k).then_inc(consts, 16)
            with sp.Fori(0, BATCH // 2 - 1) as i:
                load_ctx(2 * i + 1, 2 * i + 1)
                store(2 * i)
                load_ctx(2 * i + 2, 2 * i + 2)
                store(2 * i + 1)
            load_ctx(BATCH - 1, BATCH - 1)
            load_ctx(BATCH, 0, (0, 1))
            for c in range(3):
                load_wv(c)
            store(BATCH - 2)
            load_ctx(BATCH, 0, (2, 3))
            for g in range(GROUPS):
                store_head(BATCH - 1, g)
                if g + 3 < CH:
                    load_wv(g + 3)
            sp.wait_ge(w_in[1], 16 * (GROUPS // 2 - 1 + 3))

        @block.scalar
        def _(act):
            def ctx_high(b, slot):
                act.wait_ge(acc, GROUPS * b + GROUPS)
                for j in range(pairs):
                    act.wait_ge(c_in[j % 2], 16 * (2 * (b - 1) + j // 2) + 16)
                    split_ctx_high(act, k, j, slot, c_high)

            act.activation(k.w_first[0][:, 1], k.raw[:, 1], ACT.Copy).then_inc(w_high, 1)
            with act.Fori(0, GROUPS // 2 - 1) as i:
                for t in range(2):
                    act.wait_ge(w_in[t], 16 * i + 16)
                    take_waits(act, k.passed)
                    act.activation(k.w_rest[0][:, bass.ds(2 * i + t, 1)], k.raw[:, t:t + 1],
                                   ACT.Copy).then_inc(w_high, 1)
            two_by_two(act, ctx_high)
            act.activation(k.qp_split[0], k.qp[:, :, 0:SEQ], ACT.Copy).then_inc(q_high, 1)
            for c in range(CH - 1):
                before = GROUPS // 2 - 1 if c % 3 < 2 else 0
                act.wait_ge(w_in[c % 3], 16 * (before + c // 3) + 16)
                act.wait_ge(acc, 16 + GROUPS * (BATCH - 1) + c + 1)
                act.activation(weight_tile(k, c)[0], k.raw[:, c % 3], ACT.Copy).then_inc(w_high, 1)

        @block.gpsimd
        def _(pool):
            pool.sem_inc(w_low, 2)
            pool.sem_inc(c_low, 2)

            def ctx_low(b, slot):
                for j in range(pairs):
                    pool.wait_ge(c_high, pairs * (b - 1) + j + 1)
                    split_ctx_low(pool, k, j, slot, c_low)

            pool.wait_ge(w_high, 1)
            pool.tensor_tensor(k.w_first[1][:, 1], k.raw[:, 1], f32(k.w_first[0][:, 1]),
                               ALU.subtract).then_inc(w_low, 1)
            with pool.Fori(0, GROUPS // 2 - 1) as i:
                for t in range(2):
                    pool.wait_ge(w_high, 2 * i + t + 2)
                    pool.tensor_tensor(k.w_rest[1][:, bass.ds(2 * i + t, 1)], k.raw[:, t:t + 1],
                                       f32(k.w_rest[0][:, bass.ds(2 * i + t, 1)]), ALU.subtract).then_inc(w_low, 1)
            two_by_two(pool, ctx_low)
            pool.wait_ge(q_high, 1)
            pool.tensor_tensor(k.qp_split[1], k.qp[:, :, 0:SEQ], f32(k.qp_split[0]), ALU.subtract).then_inc(q_low, 1)
            for c in range(CH - 1):
                high, low = weight_tile(k, c)
                pool.wait_ge(w_high, GROUPS + c)
                pool.tensor_tensor(low, k.raw[:, c % 3], f32(high), ALU.subtract).then_inc(w_low, 1)

        @block.vector
        def _(dve):
            dve.sem_inc(read, 8)
            dve.sem_inc(ready, 2)
            for s in stored:
                dve.sem_inc(s, 16)
            dve.wait_ge(consts, 16)
            with dve.Fori(0, BATCH // 2) as i:
                for t in range(2):
                    for g in range(GROUPS):
                        n = GROUPS * (2 * i + t) + g
                        dve.wait_ge(acc, n + 17)
                        dve.wait_ge(ready, n + 1)
                        rotate(dve, bank[g][:, 0:KEYS_EVEN], rope[:, 0, :], rope[:, 1, :],
                               straight[:, g % 2], crossed[:, g % 2]).then_inc(read, 1)
                        dve.wait_ge(read, n + 9)
                        dve.wait_ge(stored[g % 4], 16 * (2 * (2 * i + t) + g // 4) + 16)
                        dve.tensor_tensor(rotated[:, g % 4], straight[:, g % 2], crossed[:, g % 2],
                                          ALU.add).then_inc(ready, 1)

        @block.tensor
        def _(pe):
            pe.sem_inc(acc, 16)

            def batch(b, t):
                for g in range(GROUPS):
                    pe.wait_ge(read, GROUPS * b + g + 1)
                    if g >= 1:
                        pe.wait_ge(w_low, g + 2)
                    for c in range(CH):
                        if g == 0 and c % 2 == 0 and not (known(b) and b == 0):
                            pe.wait_ge(c_low, pairs * (b - 1) + c // 2 + 3)
                        mm = split_product(pe, bank[g][:, 0:KEYS_EVEN],
                                           [p[:, c * P:(c + 1) * P] for p in weight_tile(k, g)],
                                           [p[t][:, c, :] for p in k.ctx_ring], c == 0, c == CH - 1)
                    mm.then_inc(acc, 1)

            batch(0, 0)
            batch(1, 1)
            with pe.Fori(1, BATCH // 2) as i:
                batch(2 * i, 0)
                batch(2 * i + 1, 1)


def rotate(dve, product, cos, sin, straight, crossed):
    half = P // 2
    dve.tensor_tensor(straight, product, cos, ALU.mult)
    dve.tensor_tensor(crossed[0:half], product[half:P], sin[half:P], ALU.mult)
    return dve.tensor_tensor(crossed[half:P], product[0:half], sin[0:half], ALU.mult)


def layer0_phase(nc, k):
    with ExitStack() as ctx:
        sb, pair, sem = buffers_of(nc, ctx)
        bank = k.banks
        score_bank, turn_bank, v_bank, row_banks, xn_banks = bank[0], bank[1], bank[2:4], bank[4:6], bank[6:8]
        width = L0_EXPERTS * RANK + L0_EXPERTS
        ct, cn, qp = k.ctx_ring, k.raw, k.qp_split
        wv = [weight_tile(k, c) for c in range(CH)]
        xr = sb("c_x_rows", [SEQ, 2, DIM])
        qb = k.qb_split
        ones = sb("ones_row", [1, KEYS_EVEN], F32R)
        nmax, total, inv = sb("c_nmax", [SEQ, 1]), sb("c_total", [SEQ, 1]), sb("c_inv", [SEQ, 1])
        e = sb("c_exp", [SEQ, KEYS_EVEN])
        et = sb("c_exp_t", [KEY_TILE, KEY_TILES, SEQ])
        v_out = sb("v_out", [KEY_TILE, 2, 512])
        ln = NormBuffers(sb, "ln23", 1)
        xnt = sb("xn2_t", [P, CH, SEQ])
        lora = LoraBuffers(sb, "lora0", L0_EXPERTS)
        aw, bw = sb("a0_sb", [P, CH, width]), sb("b0_sb", [L0_EXPERTS * RANK, DIM])
        tri = sb("tri0_sb", [SEQ, L0_EXPERTS, L0_EXPERTS])

        consts, ones_set = sem("c_consts"), sem("c_ones_set")
        c_in = [sem(f"c_c_in{i}") for i in range(2)]
        c_high, c_low = sem("c_c_high"), sem("c_c_low")
        cn_in, x_in = sem("c_cn_in"), [sem(f"c_x_in{i}") for i in range(2)]
        x_out = [sem(f"c_x_out{i}") for i in range(2)]
        q_high, q_low = sem("c_q_high"), sem("c_q_low")
        scored, maxed, exped = sem("c_scored"), sem("c_maxed"), sem("c_exped")
        e_turned, e_staged = sem("c_e_turned"), sem("c_e_staged")
        v_acc = sem("c_v_acc")
        v_read = sem("c_v_read")
        v_stored = [sem(f"c_v_stored{i}") for i in range(2)]
        attended, inverted, attn_added = sem("c_attended"), sem("c_inverted"), sem("c_attn_added")
        sn, sl = NormSems(sem, "ln23"), LoraSems(sem, "lora0")
        x_high, x_low = sem("c_x_high"), sem("c_x_low")
        tile_used = sem("c_tile_used")
        w_in = sem("c_w_in")
        w_high, w_low = sem("c_w_high"), sem("c_w_low")

        block = ctx.enter_context(nc.Block())
        pairs = CH // 2

        def batches(eng, batch):
            with eng.Fori(0, BATCH // 2 - 1) as i:
                batch(i, 0, True)
                batch(i, 1, True)
            batch(BATCH // 2 - 1, 0, True)
            batch(BATCH // 2 - 1, 1, False)

        @block.sync
        def _(sp):
            def load_ctx(b):
                for j in range(pairs):
                    sp.wait_ge(c_low, pairs * b + j + 1)
                    sp.dma_start(k.c_raw[:, j % 2], k.ctx_t[b, :, 2 * j:2 * j + 2, :]).then_inc(c_in[j % 2], 16)

            def load_rows(i, t):
                sp.wait_ge(x_out[t], 16 * i + 16)
                sp.dma_start(xr[:, t], k.x[2 * i + t]).then_inc(x_in[t], 16)

            def load_cn(b):
                sp.dma_start(cn[0:KEY_TILE, :, :],
                             k.ctx_nat[b].rearrange("(t p) d -> p t d", p=KEY_TILE)).then_inc(cn_in, 16)

            for dst, src in ((aw, k.a0), (tri, k.tri0)):
                sp.dma_start(dst[:, :, :], src).then_inc(consts, 16)
            sp.dma_start(bw[:, :], k.b0).then_inc(consts, 16)
            load_rows(0, 0)
            sp.wait_ge(w_low, 1)
            load_cn(0)

            def batch(i, t, ahead):
                b = 2 * i + t

                def store_v(p):
                    sp.wait_ge(v_read, 6 * b + p + 3)
                    kt, h = divmod(p, 2)
                    sp.dma_start(k.v_dram[b, kt, :, h * 512:(h + 1) * 512],
                                 v_out[:, p % 2]).then_inc(v_stored[p % 2], 16)

                if ahead:
                    load_ctx(b + 1)
                    load_rows(i + t, 1 - t)
                for p in range(3):
                    store_v(p)
                sp.wait_ge(attended, 2 * b + 2)
                if ahead:
                    load_cn(b + 1)
                else:
                    sp.dma_start(k.raw[:, 0:2], k.wq1[0:2].rearrange("n p c m -> p n (c m)")).then_inc(w_in, 16)
                for p in range(3, 5):
                    store_v(p)
                sp.wait_ge(sl.added, 2 * b + 2)
                sp.dma_start(k.x2_dram[b], xr[:, t]).then_inc(x_out[t], 16)
                store_v(5)

            batches(sp, batch)
            for s in k.k_stored:
                sp.wait_ge(s, 16 + 16 * BATCH * GROUPS // 4)
            for t in range(2):
                sp.wait_ge(v_stored[t], 16 + 16 * 3 * BATCH)
                sp.wait_ge(x_out[t], 16 + 16 * BATCH // 2)

        @block.scalar
        def _(act):
            for s in v_stored:
                act.sem_inc(s, 16)
            act.sem_inc(v_read, 2)

            def ctx_high(b, slot, js):
                for j in js:
                    act.wait_ge(c_in[j % 2], 16 * (2 * b + j // 2) + 16)
                    split_ctx_high(act, k, j, slot, c_high)

            def next_x_high(js):
                for j in js:
                    act.activation(k.xn3[0][0][:, 2 * j:2 * j + 2, :], k.qp[:, 2 * j:2 * j + 2, 0:HALF],
                                   ACT.Copy).then_inc(x_high, 1)

            def query_high(b):
                act.activation(qp[0], k.qp[:, :, bass.ds(SEQ * b, SEQ)], ACT.Copy).then_inc(q_high, 1)
                act.activation(qb[0], k.qb[:, bass.ds(SEQ * b, SEQ)], ACT.Copy).then_inc(q_high, 1)

            for s in c_in:
                act.sem_inc(s, 16 * pairs // 2)
            act.sem_inc(c_high, pairs)
            act.activation(qb[0], k.qb[:, 0:SEQ], ACT.Copy).then_inc(q_high, 2)
            act.activation(wv[CH - 1][0], k.raw[:, (CH - 1) % 3], ACT.Copy).then_inc(w_high, 1)

            def batch(i, t, ahead):
                b = 2 * i + t

                def read_v(p):
                    act.wait_ge(v_acc, 6 * b + p + 1)
                    act.wait_ge(v_stored[p % 2], 16 * (3 * b + p // 2) + 16)
                    act.activation(v_out[:, p % 2], v_bank[p % 2][0:KEY_TILE, :], ACT.Copy).then_inc(v_read, 1)

                act.wait_ge(maxed, b + 1)
                act.activation(e[:, 0:KEYS], score_bank[0:SEQ, 0:KEYS], ACT.Exp, bias=nmax[:, :],
                               accum_out=total[:, :]).then_inc(exped, 1)
                if ahead:
                    query_high(b + 1)
                read_v(0)
                if ahead:
                    ctx_high(b + 1, 1 - t, (0, 1))
                else:
                    next_x_high((0, 1))
                act.wait_ge(e_turned, b + 1)
                act.activation(et[:, :, :], turn_bank[0:KEY_TILE, 0:KEY_TILES * SEQ].rearrange(
                    "p (c t) -> p c t", c=KEY_TILES), ACT.Copy).then_inc(e_staged, 1)
                read_v(1)
                if ahead:
                    ctx_high(b + 1, 1 - t, (2, 3))
                else:
                    next_x_high((2, 3))
                read_v(2)
                for j in range(2):
                    act.wait_ge(sn.turned, 4 * b + j + 1)
                    act.activation(xnt[:, 4 * j:4 * j + 4, :],
                                   xn_banks[j][:, 0:HALF].rearrange("p (c t) -> p c t", c=4),
                                   ACT.Copy).then_inc(sn.evacuated, 1)
                read_v(3)
                act.wait_ge(sl.chain, 11 * b + 8)
                act.activation(lora.ex[:, :], lora.lg[:, :], ACT.Exp, bias=lora.nmax[:, :]).then_inc(sl.gate_exp, 1)
                act.wait_ge(sl.turned, b + 1)
                act.activation(lora.mwt[:, :], turn_bank[0:L0_EXPERTS * RANK, 0:SEQ],
                               ACT.Copy).then_inc(sl.staged, 1)
                read_v(4)
                if not ahead:
                    act.wait_ge(w_in, 16)
                    act.wait_ge(tile_used, 1)
                    act.activation(k.w_first[0][:, 0], k.raw[:, 0], ACT.Copy).then_inc(w_high, 1)
                read_v(5)
                for j in range(2):
                    act.wait_ge(sn.turned, 4 * b + j + 3)
                    take_waits(act, k.passed)
                    act.activation(k.qp[:, 4 * j:4 * j + 4, bass.ds(SEQ * b, SEQ)],
                                   xn_banks[j][:, 0:HALF].rearrange("p (c t) -> p c t", c=4),
                                   ACT.Copy).then_inc(sn.evacuated, 1)

            batches(act, batch)

        @block.gpsimd
        def _(pool):
            pool.sem_inc(c_low, pairs + 2)
            pool.sem_inc(q_low, 1)

            def ctx_low(b, slot):
                for j in range(pairs):
                    pool.wait_ge(c_high, pairs * b + j + 1)
                    split_ctx_low(pool, k, j, slot, c_low)

            def query_low(b):
                pool.wait_ge(q_high, 2 * b + 1)
                pool.tensor_tensor(qp[1], k.qp[:, :, bass.ds(SEQ * b, SEQ)], f32(qp[0]),
                                   ALU.subtract).then_inc(q_low, 1)
                row_low(b)

            def row_low(b):
                pool.wait_ge(q_high, 2 * b + 2)
                pool.tensor_tensor(qb[1], k.qb[:, bass.ds(SEQ * b, SEQ)], f32(qb[0]),
                                   ALU.subtract).then_inc(q_low, 1)

            row_low(0)
            pool.wait_ge(w_high, 1)
            pool.tensor_tensor(wv[CH - 1][1], k.raw[:, (CH - 1) % 3], f32(wv[CH - 1][0]),
                               ALU.subtract).then_inc(w_low, 1)

            def batch(i, t, ahead):
                b = 2 * i + t
                if ahead:
                    query_low(b + 1)
                    ctx_low(b + 1, 1 - t)
                norm_rstd(pool, sn, ln, 2 * b, 0, k.minus_half[:, :])
                if not ahead:
                    for j in range(pairs):
                        at = slice(2 * j, 2 * j + 2)
                        pool.wait_ge(x_high, j + 1)
                        pool.tensor_tensor(k.xn3[1][0][:, at, :], k.qp[:, at, 0:HALF], f32(k.xn3[0][0][:, at, :]),
                                           ALU.subtract).then_inc(x_low, 1)
                    pool.wait_ge(w_high, 2)
                    pool.tensor_tensor(k.w_first[1][:, 0], k.raw[:, 0], f32(k.w_first[0][:, 0]),
                                       ALU.subtract).then_inc(w_low, 1)
                norm_rstd(pool, sn, ln, 2 * b + 1, 0, k.minus_half[:, :])

            batches(pool, batch)

        @block.vector
        def _(dve):
            for s in x_out:
                dve.sem_inc(s, 16)
            dve.memset(f32(ones[:, :]), 1.0).then_inc(ones_set, 1)

            def batch(i, t, ahead):
                b = 2 * i + t
                dve.wait_ge(scored, b + 1)
                dve.tensor_reduce(nmax[:, :], score_bank[0:SEQ, 0:KEYS], AX, ALU.max,
                                  negate=True).then_inc(maxed, 1)
                dve.wait_ge(exped, b + 1)
                dve.reciprocal(inv[:, :], total[:, :]).then_inc(inverted, 1)
                dve.wait_ge(inverted, b + 1)
                dve.wait_ge(x_in[t], 16 * i + 16)
                for h in range(2):
                    dve.wait_ge(attended, 2 * b + h + 1)
                    cols = slice(h * 512, (h + 1) * 512)
                    dve.scalar_tensor_tensor(out=xr[:, t, cols], in0=row_banks[h][0:SEQ, :], scalar=inv[:, 0:1],
                                             in1=xr[:, t, cols], op0=ALU.mult,
                                             op1=ALU.add).then_inc(attn_added, 1)
                dve.wait_ge(attn_added, 2 * b + 2)
                norm_moments(dve, sn, ln, 2 * b, 0, xr[:, t], k.passed)
                norm_apply(dve, sn, ln, 2 * b, 0, xr[:, t])
                dve.wait_ge(consts, 48)
                lora_gates(dve, sl, lora, b, score_bank[0:SEQ], tri[:, :, :], L0_TOP, True)
                for h in range(2):
                    dve.wait_ge(sl.up, 2 * b + h + 1)
                    cols = slice(h * 512, (h + 1) * 512)
                    dve.tensor_tensor(xr[:, t, cols], row_banks[h][0:SEQ, :], xr[:, t, cols],
                                      ALU.add).then_inc(sl.added, 1)
                dve.wait_ge(sl.added, 2 * b + 2)
                norm_moments(dve, sn, ln, 2 * b + 1, 0, xr[:, t], k.passed)
                norm_apply(dve, sn, ln, 2 * b + 1, 0, xr[:, t])

            batches(dve, batch)

        @block.tensor
        def _(pe):
            def batch(i, t, ahead):
                b = 2 * i + t

                def v_piece(p, beside=None):
                    kt, h = divmod(p, 2)
                    pe.wait_ge(v_read, 6 * b + p + 1)
                    for c in range(CH):
                        if p == 0 and c == CH - 1:
                            pe.wait_ge(w_low, 1)
                        if beside and c == CH - 2:
                            beside()
                        mm = split_product(pe, v_bank[p % 2][0:KEY_TILE, :],
                                           [q[t][:, c, kt * KEY_TILE:(kt + 1) * KEY_TILE] for q in ct],
                                           [q[:, h * 512:(h + 1) * 512] for q in wv[c]], c == 0, c == CH - 1)
                        if not ahead and p == 5 and c == 0:
                            mm.then_inc(tile_used, 1)
                    mm.then_inc(v_acc, 1)

                pe.wait_ge(q_low, 2 * b + 1)
                for c in range(CH):
                    if c % 2 == 0:
                        pe.wait_ge(c_low, pairs * b + c // 2 + 3)
                    split_product(pe, score_bank[0:SEQ, 0:KEYS_EVEN], [q[:, c, :] for q in qp],
                                  [q[t][:, c, :] for q in ct], c == 0, False)
                pe.wait_ge(ones_set, 1)
                pe.wait_ge(q_low, 2 * b + 2)
                for part in range(2):
                    mm = pe.matmul(score_bank[0:SEQ, 0:KEYS_EVEN], qb[part], ones[:, :], start=False,
                                   stop=(part == 1))
                mm.then_inc(scored, 1)
                v_piece(0)
                pe.wait_ge(exped, b + 1)
                for kt in range(KEY_TILES):
                    mm = pe.transpose(turn_bank[0:KEY_TILE, kt * SEQ:(kt + 1) * SEQ],
                                      e[:, kt * KEY_TILE:(kt + 1) * KEY_TILE], k.ident[0:SEQ, 0:SEQ])
                mm.then_inc(e_turned, 1)
                v_piece(1)
                pe.wait_ge(e_staged, b + 1)
                pe.wait_ge(cn_in, 16 * b + 16)
                for h in range(2):
                    for kt in range(KEY_TILES):
                        mm = pe.matmul(row_banks[h][0:SEQ, :], et[:, kt, :],
                                       cn[0:KEY_TILE, kt, h * 512:(h + 1) * 512],
                                       start=(kt == 0), stop=(kt == KEY_TILES - 1))
                    mm.then_inc(attended, 1)
                v_piece(2)
                norm_turn(pe, sn, ln, 2 * b, 0, xn_banks, k.ident)
                v_piece(3)
                pe.wait_ge(consts, 48)
                pe.wait_ge(sn.evacuated, 4 * b + 2)
                lora_mid(pe, sl, b, score_bank[0:SEQ], xnt, aw)
                v_piece(4, lambda: lora_turn(pe, sl, lora, b, turn_bank, k.ident, k.passed))
                lora_up(pe, sl, lora, b, [r[0:SEQ, :] for r in row_banks], bw)
                v_piece(5)
                norm_turn(pe, sn, ln, 2 * b + 1, 0, xn_banks, k.ident)

            batches(pe, batch)


def query1_phase(nc, k, first):
    with ExitStack() as ctx:
        sb, pair, sem = buffers_of(nc, ctx)
        bank = k.banks[4:8]
        w = [x[:, :, :].rearrange("p s (c m) -> p s c m", c=CH) for x in k.w_first]
        rope = sb("q_rope", [P, 2, SEQ])
        straight, crossed = sb("q_straight", [P, 2, HALF]), sb("q_crossed", [P, 2, HALF])
        rotated, stored = first.q_rotated, first.q_stored

        consts = sem("d_consts")
        x_high, x_low = sem("d_x_high"), sem("d_x_low")
        w_in = [sem(f"d_w_in{i}") for i in range(2)]
        w_high, w_low = sem("d_w_high"), sem("d_w_low")
        acc = sem("d_acc")
        read = sem("d_read")
        ready = sem("d_ready")
        FIRST = ((0, 0), (1, 0), (0, 1), (1, 1))

        block = ctx.enter_context(nc.Block())

        LAST = HEADS // 2 - 1

        def half_tiles(eng, half_tile, beside=(None,) * 5):
            for unit, (t, h) in enumerate(FIRST):
                half_tile(unit, 0, t, h)
            with eng.Fori(1, LAST) as i:
                for t in range(2):
                    for h in range(2):
                        half_tile(4 * i + 2 * t + h, i, t, h)
            for n, other in enumerate(beside):
                if other:
                    other()
                if n < 4:
                    half_tile(4 * LAST + n, LAST, n // 2, n % 2)

        @block.sync
        def _(sp):
            sp.dma_start(rope[:, :, :], k.rope_q).then_inc(consts, 16)

            def store(unit, i, t, h):
                sp.wait_ge(ready, unit + 3)
                sp.dma_start(k.q_dram[2 * i + t, :, h * HALF:(h + 1) * HALF],
                             rotated[:, 2 * t + h]).then_inc(stored[2 * t + h], 16)

            def load_w(i, t):
                sp.wait_ge(w_low, 2 * i + t + 3)
                sp.dma_start(k.raw[:, t], k.wq1[2 * i + t + 2].rearrange("p c m -> p (c m)")).then_inc(w_in[t], 16)

            load_w(0, 0)
            load_w(0, 1)
            for unit, (t, h) in enumerate(FIRST):
                store(unit, 0, t, h)

            def head_pair(i, more):
                for t in range(2):
                    if more:
                        load_w(i, t)
                    for h in range(2):
                        store(4 * i + 2 * t + h, i, t, h)

            with sp.Fori(1, LAST - 1) as i:
                head_pair(i, True)
            for s in stored:
                sp.wait_ge(s, 16 + 16 * PER_GROUP // 2)
            first.load(sp)
            head_pair(LAST - 1, True)
            first.load_next(sp)
            head_pair(LAST, False)

        @block.scalar
        def _(act):
            for s in w_in:
                act.sem_inc(s, 16)
            act.sem_inc(w_high, 1)
            act.activation(k.w_first[0][:, 1], k.raw[:, 1], ACT.Copy).then_inc(w_high, 1)
            for j in range(CH // 2):
                at = slice(2 * j, 2 * j + 2)
                act.activation(k.xn3[0][1][:, at, :], k.qp[:, at, HALF:TOK], ACT.Copy).then_inc(x_high, 1)

            def weight_high(i, t, used):
                act.wait_ge(w_in[t], 16 * i + 16)
                act.wait_ge(acc, used)
                act.activation(k.w_first[0][:, t], k.raw[:, t], ACT.Copy).then_inc(w_high, 1)

            weight_high(1, 0, 7)
            weight_high(1, 1, 8)
            with act.Fori(2, HEADS // 2) as i:
                for t in range(2):
                    weight_high(i, t, 4 * i + 2 * t + 2)
            first.split_high(act)

        @block.gpsimd
        def _(pool):
            pool.sem_inc(w_low, 3)
            pool.wait_ge(w_high, 2)
            pool.tensor_tensor(k.w_first[1][:, 1], k.raw[:, 1], f32(k.w_first[0][:, 1]),
                               ALU.subtract).then_inc(w_low, 1)
            with pool.Fori(1, HEADS // 2) as i:
                for t in range(2):
                    pool.wait_ge(w_high, 2 * i + t + 1)
                    pool.tensor_tensor(k.w_first[1][:, t], k.raw[:, t], f32(k.w_first[0][:, t]),
                                       ALU.subtract).then_inc(w_low, 1)
            first.split_low(pool)

        @block.vector
        def _(dve):
            dve.sem_inc(read, 4)
            dve.sem_inc(ready, 2)
            for s in stored:
                dve.sem_inc(s, 16)
            for j in range(CH // 2):
                at = slice(2 * j, 2 * j + 2)
                dve.wait_ge(x_high, j + 1)
                dve.tensor_tensor(k.xn3[1][1][:, at, :], k.qp[:, at, HALF:TOK], f32(k.xn3[0][1][:, at, :]),
                                  ALU.subtract).then_inc(x_low, 1)
            dve.wait_ge(consts, 16)
            cos, sin = (rope[:, j, :].unsqueeze(1).broadcast_to([P, QUAD, SEQ]) for j in range(2))

            def by_batch(ap):
                return ap.rearrange("p (b t) -> p b t", b=QUAD)

            def rotated_half(unit, i, t, h):
                slot = unit % 2 if known(unit) else h
                dve.wait_ge(acc, unit + 5)
                dve.wait_ge(ready, unit + 1)
                rotate(dve, by_batch(bank[2 * t + h][:, 0:HALF]), cos, sin,
                       by_batch(straight[:, slot]), by_batch(crossed[:, slot])).then_inc(read, 1)
                dve.wait_ge(read, unit + 5)
                dve.wait_ge(stored[2 * t + h], 16 * i + 16)
                dve.tensor_tensor(rotated[:, 2 * t + h], straight[:, slot], crossed[:, slot],
                                  ALU.add).then_inc(ready, 1)

            half_tiles(dve, rotated_half, (
                lambda: first.take_mask(dve),
                lambda: first.mask_scores(dve, 0, 0, (0, 1)),
                lambda: first.mask_scores(dve, 0, 0, (2, 3)),
                lambda: first.normalise(dve, 0, 0),
                None))

        @block.tensor
        def _(pe):
            pe.sem_inc(acc, 4)

            def half_tile(unit, i, t, h):
                if t == 1 or not (known(i) and i == 0):
                    pe.wait_ge(w_low, 2 * i + t + 3)
                pe.wait_ge(read, unit + (2 if (t, h) == (0, 1) else 1))
                for c in range(CH):
                    if h == 1 and known(i) and i == 0 and c % 2 == 0:
                        pe.wait_ge(x_low, c // 2 + 1)
                    mm = split_product(pe, bank[2 * t + h][:, 0:HALF], [q[:, t, c, :] for q in w],
                                       [q[h][:, c, :] for q in k.xn3], c == 0, c == CH - 1)
                mm.then_inc(acc, 1)

            half_tiles(pe, half_tile, (
                None, lambda: first.scores(pe, 0, 0, (0, 1)), lambda: first.scores(pe, 0, 0, (2, 3)), None, None))


def known(s):
    return isinstance(s, int)


def half_of(s, u):
    return s // 2 if known(s) else (s - u % 2) // 2


class AttentionSteps:

    def __init__(self, nc, ctx, k):
        sb, pair, sem = buffers_of(nc, ctx, "right")
        self.k = k
        self.s_bank = k.banks[0:2]
        H = PER_GROUP
        self.raw_q, self.raw_k = sb("e_raw_q", [P, 2, H, SEQ]), sb("e_raw_k", [P, 2, KEYS_EVEN])
        self.raw_v = sb("e_raw_v", [KEY_TILE, 2, KEY_TILES, P])
        self.q, self.kt = pair("e_q", [P, 2, H, SEQ]), pair("e_k", [P, 2, KEYS_EVEN])
        self.v = pair("e_v", [KEY_TILE, 2, KEY_TILES, P])
        self.mask = sb("e_mask", [SEQ, BATCH, KEYS])
        self.s_buf = sb("e_scores", [SEQ, 2, H, KEYS])
        self.mx, self.nm = sb("e_max", [SEQ, 2, H]), sb("e_nmax", [SEQ, 2, H])
        self.total, self.inv = sb("e_total", [SEQ, 2, H]), sb("e_inv", [SEQ, 2, H])

        self.rows = sb("q_rotated_then_x_rows", [P, X_SLOTS, DIM])
        self.q_rotated = self.rows[:, 0:2, :].rearrange("p s d -> p (s d)")[:, 0:4 * HALF].rearrange(
            "p (n t) -> p n t", n=4)
        self.q_stored = [sem(f"e_q_stored{i}") for i in range(4)]

        self.mask_in = sem("e_mask_in")
        self.q_in, self.k_in, self.v_in = ([sem(f"e_{n}_in{i}") for i in range(2)] for n in ("q", "k", "v"))
        self.qk_high, self.qk_low = sem("e_qk_high"), sem("e_qk_low")
        self.v_high, self.v_low = sem("e_v_high"), sem("e_v_low")
        self.scored, self.masked = sem("e_scored"), sem("e_masked")
        self.negated, self.exped = sem("e_negated"), sem("e_exped")
        self.inverted, self.normed = sem("e_inverted"), sem("e_normed")
        self.turned = sem("e_turned")
        self.o_acc = sem("e_o_acc")

    def load_qk(self, sp, s, b, g):
        if not (known(s) and s < 2):
            sp.wait_ge(self.qk_low, 2 * s - 2)
        sp.dma_start(self.raw_q[:, b % 2], self.k.q_dram[bass.ds(PER_GROUP * g, PER_GROUP), :,
                                                         b * SEQ:(b + 1) * SEQ].rearrange(
            "h p t -> p h t")).then_inc(self.q_in[b % 2], 16)
        sp.dma_start(self.raw_k[:, b % 2], self.k.kt_dram[b, g]).then_inc(self.k_in[b % 2], 16)

    def load_v(self, sp, s, b, g):
        if not (known(s) and s < 2):
            sp.wait_ge(self.v_low, s - 1)
        sp.dma_start(self.raw_v[:, b % 2], self.k.v_dram[b, :, :, bass.ds(P * g, P)].rearrange(
            "c p d -> p c d")).then_inc(self.v_in[b % 2], 16)

    def qk_high_part(self, act, s, u):
        t = u % 2
        act.wait_ge(self.q_in[t], 16 * half_of(s, u) + 16)
        if not (known(s) and s < 2):
            act.wait_ge(self.scored, 4 * s - 4)
        act.activation(self.q[0][:, t], self.raw_q[:, t], ACT.Copy).then_inc(self.qk_high, 1)
        act.wait_ge(self.k_in[t], 16 * half_of(s, u) + 16)
        act.activation(self.kt[0][:, t], self.raw_k[:, t], ACT.Copy).then_inc(self.qk_high, 1)

    def v_high_part(self, act, s, u):
        t = u % 2
        act.wait_ge(self.v_in[t], 16 * half_of(s, u) + 16)
        if not (known(s) and s < 2):
            act.wait_ge(self.o_acc, s - 1)
        act.activation(self.v[0][:, t], self.raw_v[:, t], ACT.Copy).then_inc(self.v_high, 1)

    def qk_low_part(self, pool, s, u):
        t = u % 2
        for n, (raw, (high, low)) in enumerate(((self.raw_q, self.q), (self.raw_k, self.kt))):
            pool.wait_ge(self.qk_high, 2 * s + n + 1)
            pool.tensor_tensor(low[:, t], raw[:, t], f32(high[:, t]), ALU.subtract).then_inc(self.qk_low, 1)

    def v_low_part(self, pool, s, u):
        t = u % 2
        pool.wait_ge(self.v_high, s + 1)
        pool.tensor_tensor(self.v[1][:, t], self.raw_v[:, t], f32(self.v[0][:, t]),
                           ALU.subtract).then_inc(self.v_low, 1)

    def scores(self, pe, s, u, heads):
        t = u % 2
        pe.wait_ge(self.qk_low, 2 * s + 2)
        for h in heads:
            if not (known(s) and s < 1 and h < 2):
                pe.wait_ge(self.masked, 4 * s + h - 1)
            split_product(pe, self.s_bank[h % 2][0:SEQ, 0:KEYS_EVEN], [x[:, t, h, :] for x in self.q],
                          [x[:, t, :] for x in self.kt], True, True).then_inc(self.scored, 1)

    def mask_scores(self, dve, s, u, heads):
        t = u % 2
        for h in heads:
            dve.wait_ge(self.scored, 4 * s + h + 1)
            if not (known(s) and s < 2):
                dve.wait_ge(self.turned, 3 * s - 3)
            take_waits(dve, self.k.passed)
            dve.tensor_tensor_reduce(self.s_buf[:, t, h, :], self.s_bank[h % 2][0:SEQ, 0:KEYS], self.mask[:, u, :],
                                     1.0, LOWEST, ALU.add, ALU.max,
                                     self.mx[:, t, h:h + 1]).then_inc(self.masked, 1)
            dve.wait_ge(self.masked, 4 * s + h + 1)
            dve.tensor_scalar(self.nm[:, t, h:h + 1], self.mx[:, t, h:h + 1], -1.0, None,
                              ALU.mult).then_inc(self.negated, 1)

    def exps(self, act, s, u, heads):
        t = u % 2
        for h in heads:
            act.wait_ge(self.negated, 4 * s + h + 1)
            act.activation(self.s_buf[:, t, h, :], self.s_buf[:, t, h, :], ACT.Exp, bias=self.nm[:, t, h:h + 1],
                           accum_out=self.total[:, t, h:h + 1]).then_inc(self.exped, 1)

    def normalise(self, dve, s, u):
        t = u % 2
        dve.wait_ge(self.exped, 4 * s + 4)
        dve.reciprocal(self.inv[:, t, :], self.total[:, t, :]).then_inc(self.inverted, 1)
        dve.wait_ge(self.inverted, s + 1)
        for h in range(PER_GROUP):
            dve.tensor_scalar(self.s_buf[:, t, h, :], self.s_buf[:, t, h, :], self.inv[:, t, h:h + 1], None,
                              ALU.mult).then_inc(self.normed, 1)

    def load(self, sp):
        sp.dma_start(self.mask[:, :, :], self.k.mask.rearrange("b q s -> q b s")).then_inc(self.mask_in, 16)
        self.load_qk(sp, 0, 0, 0)
        self.load_qk(sp, 1, 1, 0)
        self.load_v(sp, 0, 0, 0)

    def load_next(self, sp):
        self.load_qk(sp, 2, 2, 0)
        self.load_v(sp, 1, 1, 0)

    def split_high(self, act):
        self.qk_high_part(act, 0, 0)
        self.v_high_part(act, 0, 0)
        self.qk_high_part(act, 1, 1)
        self.exps(act, 0, 0, range(PER_GROUP))

    def split_low(self, pool):
        self.qk_low_part(pool, 0, 0)
        self.v_low_part(pool, 0, 0)
        self.qk_low_part(pool, 1, 1)

    def take_mask(self, dve):
        dve.wait_ge(self.mask_in, 16)


def attention_phase(nc, k, first):
    with ExitStack() as ctx:
        sb, pair, sem = buffers_of(nc, ctx)
        bank = k.banks
        p_bank, o_bank, y_bank = bank[2:5], bank[5], bank[6:8]
        H = PER_GROUP
        STEPS = GROUPS * BATCH
        k.yt = sb("y_t", [P, CH, TOK])
        raw_wo = sb("e_raw_wo", [P, 2, H, 256])
        wo = pair("e_wo", [P, 4, H, 256])
        pt = pair("e_p_t", [KEY_TILE, KEY_TILES, H * SEQ])
        ot = pair("e_o_t", [P, 2, H, HALF])
        s_buf, v = first.s_buf, first.v
        turned, normed, o_acc, v_low = first.turned, first.normed, first.o_acc, first.v_low

        wo_in = [sem(f"e_wo_in{i}") for i in range(2)]
        wo_high, wo_low = sem("e_wo_high"), sem("e_wo_low")
        pt_high, pt_low = sem("e_pt_high"), sem("e_pt_low")
        o_high, o_low = sem("e_o_high"), sem("e_o_low")
        y_acc = sem("e_y_acc")
        y_zeroed = sem("e_y_zeroed")
        y_added = sem("e_y_added")

        block = ctx.enter_context(nc.Block())

        def steps(eng, step):
            for s in range(4):
                step(s, s, 0)
            with eng.Fori(0, GROUPS - 1) as j:
                for u in range(4, 12):
                    step(8 * j + u, u % 8, j + u // 8)
            for s in range(STEPS - 4, STEPS):
                step(s, s % 8, GROUPS - 1)

        @block.sync
        def _(sp):
            def load_wo(b, g, early):
                if not (early and b < 2):
                    sp.wait_ge(wo_low, 4 * g + b - 1)
                sp.dma_start(raw_wo[:, b % 2], k.wo1[g, :, :, b * 256:(b + 1) * 256]).then_inc(wo_in[b % 2], 16)

            def step(s, u, g):
                last = known(s) and s >= STEPS - 4
                if not (last and s + 3 >= STEPS):
                    first.load_qk(sp, s + 3, (u + 3) % 8, g + (u + 3) // 8)
                if not (last and s + 2 >= STEPS):
                    first.load_v(sp, s + 2, (u + 2) % 8, g + (u + 2) // 8)
                if u < 4:
                    load_wo(u, g, known(s))

            for q_stored in first.q_stored:
                sp.wait_ge(q_stored, 16 + 16 * HEADS // 2)
            steps(sp, step)

        @block.scalar
        def _(act):
            def step(s, u, g):
                last = known(s) and s >= STEPS - 4
                more = not (last and s + 1 >= STEPS)
                if not (last and s + 2 >= STEPS):
                    first.qk_high_part(act, s + 2, (u + 2) % 8)
                for c in range(KEY_TILES):
                    act.wait_ge(turned, 3 * s + c + 1)
                    if not (known(s) and s < 1):
                        act.wait_ge(o_acc, s)
                    act.activation(pt[0][:, c, :], p_bank[c][0:KEY_TILE, 0:HALF], ACT.Copy).then_inc(pt_high, 1)
                if more:
                    first.exps(act, s + 1, (u + 1) % 8, (0, 1))
                if more:
                    first.exps(act, s + 1, (u + 1) % 8, (2, 3))
                    first.v_high_part(act, s + 1, (u + 1) % 8)
                act.wait_ge(o_acc, s + 1)
                act.activation(ot[0][:, (u // 4) % 2, :, (u % 4) * SEQ:(u % 4 + 1) * SEQ],
                               o_bank[:, 0:HALF].rearrange("p (h t) -> p h t", h=H), ACT.Copy).then_inc(o_high, 1)
                if u < 4:
                    act.wait_ge(wo_in[u % 2], 16 * (2 * g + u // 2) + 16)
                    if not (known(s) and s < 4):
                        act.wait_ge(y_acc, 2 * s - 6)
                    act.activation(wo[0][:, u], raw_wo[:, u % 2], ACT.Copy).then_inc(wo_high, 1)

            steps(act, step)

        @block.gpsimd
        def _(pool):
            def step(s, u, g):
                last = known(s) and s >= STEPS - 4
                if not (last and s + 2 >= STEPS):
                    first.qk_low_part(pool, s + 2, (u + 2) % 8)
                if not (last and s + 1 >= STEPS):
                    first.v_low_part(pool, s + 1, (u + 1) % 8)
                if u < 4:
                    pool.wait_ge(wo_high, 4 * g + u + 1)
                    pool.tensor_tensor(wo[1][:, u], raw_wo[:, u % 2], f32(wo[0][:, u]),
                                       ALU.subtract).then_inc(wo_low, 1)
                if known(s) and s < 4:
                    pool.memset(k.yt[:, 2 * s:2 * s + 2, :], 0.0).then_inc(y_zeroed, 1)

            steps(pool, step)

        def y_tile(s, u, t):
            return 2 * (u % 4) + t, (0 if u >= 4 else HALF)

        whole = 2 + 2 * (STEPS - 4)
        rounds, normalised_rows, round_of_vectors, round_of_products = final_phase(
            nc, k, first, sb, sem, block, y_added, (whole, whole + 8))

        @block.vector
        def _(dve):
            dve.sem_inc(y_added, 2)

            def add_y(s, u, t):
                tile, at = y_tile(s, u, t)
                dve.wait_ge(y_acc, 2 * s - 8 + t + 1)
                dve.wait_ge(y_zeroed, 4)
                dve.wait_ge(y_added, 2 * s - 8 + t + 2)
                dve.tensor_tensor(k.yt[:, tile, at:at + HALF], y_bank[t][:, 0:HALF],
                                  k.yt[:, tile, at:at + HALF], ALU.add).then_inc(y_added, 1)

            def step(s, u, g):
                more = not (known(s) and s + 1 >= STEPS)
                adds = not (known(s) and s < 4)
                if more:
                    first.mask_scores(dve, s + 1, (u + 1) % 8, (0, 1))
                for c in range(KEY_TILES):
                    dve.wait_ge(pt_high, 3 * s + c + 1)
                    dve.tensor_tensor(pt[1][:, c, :], p_bank[c][0:KEY_TILE, 0:HALF], f32(pt[0][:, c, :]),
                                      ALU.subtract).then_inc(pt_low, 1)
                if adds:
                    add_y(s, u, 0)
                if more:
                    first.mask_scores(dve, s + 1, (u + 1) % 8, (2, 3))
                if adds:
                    add_y(s, u, 1)
                if more:
                    first.normalise(dve, s + 1, (u + 1) % 8)
                dve.wait_ge(o_high, s + 1)
                at = (slice(None), (u // 4) % 2, slice(None), slice((u % 4) * SEQ, (u % 4 + 1) * SEQ))
                dve.tensor_tensor(ot[1][at], o_bank[:, 0:HALF].rearrange("p (h t) -> p h t", h=H),
                                  f32(ot[0][at]), ALU.subtract).then_inc(o_low, 1)

            steps(dve, step)
            for r in rounds:
                normalised_rows(dve, r)
                if r < 4:
                    add_y(STEPS + r, r, 0)
                    add_y(STEPS + r, r, 1)
                round_of_vectors(dve, r)

        @block.tensor
        def _(pe):
            def project(s, u, t):
                quad = 0 if u >= 4 else 1
                pe.wait_ge(o_low, s - u % 4)
                if u >= 4 and t == 0:
                    pe.wait_ge(wo_low, (s - u) // 2 + u - 3)
                pe.wait_ge(y_added, 2 * s - 8 + t + 1)
                for h in range(H):
                    mm = split_product(pe, y_bank[t][:, 0:HALF],
                                       [x[:, u % 4, h, t * P:(t + 1) * P] for x in wo],
                                       [x[:, quad, h, :] for x in ot], h == 0, h == H - 1)
                mm.then_inc(y_acc, 1)

            def step(s, u, g):
                more = not (known(s) and s + 1 >= STEPS)
                adds = not (known(s) and s < 4)
                t = u % 2
                if more:
                    first.scores(pe, s + 1, (u + 1) % 8, (0, 1))
                pe.wait_ge(normed, 4 * s + 4)
                for c in range(KEY_TILES):
                    if not (known(s) and s < 1):
                        pe.wait_ge(pt_low, 3 * s - 3 + c + 1)
                    for h in range(H):
                        mm = pe.transpose(p_bank[c][0:KEY_TILE, h * SEQ:(h + 1) * SEQ],
                                          s_buf[:, t, h, c * KEY_TILE:(c + 1) * KEY_TILE],
                                          k.ident[0:SEQ, 0:SEQ])
                    mm.then_inc(turned, 1)
                if adds:
                    project(s, u, 0)
                if more:
                    first.scores(pe, s + 1, (u + 1) % 8, (2, 3))
                if adds:
                    project(s, u, 1)
                pe.wait_ge(v_low, s + 1)
                if not (known(s) and s < 1):
                    pe.wait_ge(o_low, s)
                for c in range(KEY_TILES):
                    pe.wait_ge(pt_low, 3 * s + c + 1)
                    mm = split_product(pe, o_bank[:, 0:HALF], [x[:, t, c, :] for x in v],
                                       [x[:, c, :] for x in pt], c == 0, c == KEY_TILES - 1)
                mm.then_inc(o_acc, 1)

            steps(pe, step)
            for r in rounds:
                if r < 4:
                    project(STEPS + r, r, 0)
                    project(STEPS + r, r, 1)
                round_of_products(pe, r)


def final_phase(nc, k, first, sb, sem, block, y_added, y_of_quad):
    bank = k.banks
    y_banks, xn_banks, mid_bank, turn_bank, up_banks = bank[0:2], bank[2:4], bank[4], bank[5], bank[6:8]
    width = L1_EXPERTS * RANK + L1_EXPERTS
    SLOTS = X_SLOTS
    xr, spare = first.rows[0:SEQ], first.s_buf
    ln = NormBuffers(sb, "ln4", 2)
    xnt = sb("xn4_t", [P, 2, CH, SEQ])
    lora = LoraBuffers(sb, "lora1", L1_EXPERTS)
    aw, bw = sb("a1_sb", [P, CH, width]), sb("b1_sb", [L1_EXPERTS * RANK, DIM])
    tri = sb("tri1_sb", [SEQ, L1_EXPERTS, L1_EXPERTS])

    consts = sem("f_consts")
    moved = [sem(f"f_moved{i}") for i in range(SLOTS)]
    y_turned, x_summed = sem("f_y_turned"), sem("f_x_summed")
    update_read = sem("f_update_read")
    s4, sl = NormSems(sem, "ln4"), LoraSems(sem, "lora1")
    rounds = range(BATCH + 3)

    def update(b, h):
        return spare[:, b % 2].rearrange("t h k -> t (h k)")[:, h * 512:(h + 1) * 512]

    def stage(r, n):
        return r - n if 0 <= r - n < BATCH else None

    @block.sync
    def _(sp):
        for dst, src in ((aw, k.a1), (tri, k.tri1)):
            sp.dma_start(dst[:, :, :], src).then_inc(consts, 16)
        sp.dma_start(bw[:, :], k.b1).then_inc(consts, 16)

        def load(b):
            if b >= SLOTS:
                sp.wait_ge(moved[b % SLOTS], 32 * (b // SLOTS))
            sp.dma_start(xr[:, b % SLOTS], k.x2_dram[b]).then_inc(moved[b % SLOTS], 16)

        for b in range(SLOTS):
            load(b)
        for b in range(BATCH):
            sp.wait_ge(sl.added, 2 * b + 2)
            sp.dma_start(k.out[b], xr[:, b % SLOTS]).then_inc(moved[b % SLOTS], 16)
            if b + SLOTS < BATCH:
                load(b + SLOTS)
        for i, s in enumerate(moved):
            sp.wait_ge(s, 32 * len(range(i, BATCH, SLOTS)))

    @block.scalar
    def _(act):
        for r in rounds:
            if (b := stage(r, 3)) is not None:
                act.wait_ge(sl.turned, b + 1)
                act.activation(lora.mwt[:, :], turn_bank[0:L1_EXPERTS * RANK, 0:SEQ],
                               ACT.Copy).then_inc(sl.staged, 1)
            if (b := stage(r, 1)) is not None:
                for j in range(2):
                    act.wait_ge(s4.turned, 2 * b + j + 1)
                    act.activation(xnt[:, b % 2, 4 * j:4 * j + 4, :],
                                   xn_banks[j][:, 0:HALF].rearrange("p (c t) -> p c t", c=4),
                                   ACT.Copy).then_inc(s4.evacuated, 1)
            if (b := stage(r, 3)) is not None and b < BATCH - 1:
                for h in range(2):
                    if b >= 2:
                        act.wait_ge(sl.added, 2 * b - 3 + h)
                    act.wait_ge(sl.up, 2 * b + h + 1)
                    act.activation(update(b, h), up_banks[h][0:SEQ, :], ACT.Copy).then_inc(update_read, 1)

    @block.gpsimd
    def _(pool):
        for r in rounds:
            if (b := stage(r, 0)) is not None:
                norm_rstd(pool, s4, ln, b, b % 2, k.minus_half[:, :])
            if (b := stage(r, 3)) is not None and b < BATCH - 1:
                for h in range(2):
                    x = xr[:, b % SLOTS, h * 512:(h + 1) * 512]
                    pool.wait_ge(update_read, 2 * b + h + 1)
                    pool.tensor_tensor(x, update(b, h), x, ALU.add).then_inc(sl.added, 1)

    def normalised_rows(dve, r):
        if (b := stage(r, 1)) is not None:
            norm_apply(dve, s4, ln, b, b % 2, xr[:, b % SLOTS])

    def round_of_vectors(dve, r):
        if (b := stage(r, 0)) is not None:
            x = xr[:, b % SLOTS]
            dve.wait_ge(moved[b % SLOTS], 32 * (b // SLOTS) + 16)
            for h in range(2):
                dve.wait_ge(y_turned, 2 * b + h + 1)
                cols = slice(h * 512, (h + 1) * 512)
                dve.tensor_tensor(x[:, cols], y_banks[h][0:SEQ, :], x[:, cols],
                                  ALU.add).then_inc(x_summed, 1)
            dve.wait_ge(x_summed, 2 * b + 2)
            norm_moments(dve, s4, ln, b, b % 2, x, k.passed)
        if (b := stage(r, 2)) is not None:
            if b == 0:
                dve.wait_ge(consts, 48)
            lora_gates(dve, sl, lora, b, mid_bank[0:SEQ], tri[:, :, :], L1_TOP, False)
        if (b := stage(r, 3)) == BATCH - 1:
            x = xr[:, b % SLOTS]
            dve.wait_ge(sl.added, 2 * b)
            for h in range(2):
                dve.wait_ge(sl.up, 2 * b + h + 1)
                cols = slice(h * 512, (h + 1) * 512)
                dve.tensor_tensor(x[:, cols], up_banks[h][0:SEQ, :], x[:, cols],
                                  ALU.add).then_inc(sl.added, 1)

    def round_of_products(pe, r):
        if (b := stage(r, 0)) is not None:
            pe.wait_ge(y_added, y_of_quad[b // QUAD])
            for h in range(2):
                if b:
                    pe.wait_ge(x_summed, 2 * b - 1 + h)
                for c in range(4):
                    mm = pe.transpose(y_banks[h][0:SEQ, c * P:(c + 1) * P],
                                      k.yt[:, 4 * h + c, b * SEQ:(b + 1) * SEQ], k.ident[:, :])
                mm.then_inc(y_turned, 1)
        if (b := stage(r, 3)) is not None:
            lora_turn(pe, sl, lora, b, turn_bank, k.ident, k.passed)
        if (b := stage(r, 1)) is not None:
            if b:
                pe.wait_ge(s4.evacuated, 2 * b)
            norm_turn(pe, s4, ln, b, b % 2, xn_banks, k.ident)
        if (b := stage(r, 2)) is not None:
            if b == 0:
                pe.wait_ge(consts, 48)
            pe.wait_ge(s4.evacuated, 2 * b + 2)
            if b:
                pe.wait_ge(sl.gated, 2 * b)
            lora_mid(pe, sl, b, mid_bank[0:SEQ], xnt[:, b % 2], aw)
        if (b := stage(r, 3)) is not None:
            if b == 0:
                pe.wait_ge(y_added, y_of_quad[1])
            else:
                pe.wait_ge(update_read, 2 * b)
            lora_up(pe, sl, lora, b, [x[0:SEQ, :] for x in up_banks], bw)

    return rounds, normalised_rows, round_of_vectors, round_of_products


def rope_tables(positions, scale):
    import numpy as np
    half = P // 2
    inv_freq = (1.0 / np.float32(10000.0) ** (np.arange(0, P, 2, dtype=np.float32) / np.float32(P))).astype(np.float32)
    angle = (np.arange(positions, dtype=np.float32)[None, :] * inv_freq[:, None]).astype(np.float32)
    table = np.zeros((P, 2, positions), np.float64)
    table[:half, 0] = table[half:, 0] = np.cos(angle.astype(np.float64))
    table[:half, 1] = np.sin(angle.astype(np.float64))
    table[half:, 1] = -table[:half, 1]
    return (table * scale).astype(np.float32)


def kernel(x, ctx_4096, mask_BxSxS2_ff0, L0_xattn_Wq, L0_xattn_bq, L0_xattn_Wk, L0_xattn_bk, L0_ffn_A, L0_ffn_B,
           L0_ffn_Wr, L1_xattn_wq, L1_xattn_wk, L1_xattn_wv, L1_xattn_wo, L1_ffn_route_w, L1_ffn_A, L1_ffn_Bw):
    import numpy as np
    import concourse.bacc as bacc
    from concourse.bass_utils import run_bass_kernel_spmd

    def rows(a):
        return np.ascontiguousarray(a)

    ctx = np.asarray(ctx_4096)
    ctx_t = np.zeros((BATCH, P, CH, KEYS_EVEN), ctx.dtype)
    ctx_t[..., :KEYS] = ctx.transpose(0, 2, 1).reshape(BATCH, CH, P, KEYS).transpose(0, 2, 1, 3)

    def tiles(w):
        w = np.asarray(w)
        return rows(w.reshape(CH, P, w.shape[1] // P, P).transpose(2, 1, 0, 3))

    def down(a, router):
        a, router = np.asarray(a), np.asarray(router)
        both = np.concatenate([a.reshape(-1, DIM), router], axis=0)
        return rows(both.T.reshape(CH, P, -1).transpose(1, 0, 2))

    def up(b):
        return rows(np.asarray(b).transpose(0, 2, 1).reshape(-1, DIM))

    def triangle(experts):
        t = np.tril(np.ones((experts, experts), np.float32), -1)
        return rows(np.broadcast_to(t, (SEQ, experts, experts)))

    wo = np.asarray(L1_xattn_wo).reshape(GROUPS, PER_GROUP, P, DIM).transpose(0, 2, 1, 3)
    arrays = dict(
        x=rows(x), ctx_nat=rows(ctx), ctx_t=ctx_t, mask=rows(mask_BxSxS2_ff0),
        wq0_t=tiles(np.asarray(L0_xattn_Wq).T), wk0=tiles(L0_xattn_Wk),
        bq=rows(np.asarray(L0_xattn_bq).reshape(CH, P).T), bk=rows(np.asarray(L0_xattn_bk).reshape(CH, P).T),
        a0=down(L0_ffn_A, L0_ffn_Wr), b0=up(L0_ffn_B),
        wq1=tiles(L1_xattn_wq), wk1=tiles(L1_xattn_wk),
        wv1=rows(np.asarray(L1_xattn_wv).reshape(CH, P, DIM).transpose(1, 0, 2)), wo1=rows(wo),
        a1=down(L1_ffn_A, L1_ffn_route_w), b1=up(L1_ffn_Bw),
        rope_q=rope_tables(SEQ, float(P) ** -0.5), rope_k=rope_tables(KEYS_EVEN, 1.0),
        ident_in=np.eye(P, dtype=np.float32), tri0_in=triangle(L0_EXPERTS), tri1_in=triangle(L1_EXPERTS))
    nc = bacc.Bacc("TRN2", target_bir_lowering=False, num_devices=1)
    args = {n: nc.dram_tensor(f"in_{n}", a.shape, mybir.dt.from_np(a.dtype), kind="ExternalInput").ap()
            for n, a in arrays.items()}
    out = nc.dram_tensor("out_0", (BATCH, SEQ, DIM), F32, kind="ExternalOutput").ap()
    build(nc, out=out, **args)
    r = run_bass_kernel_spmd(nc, [{f"in_{n}": a for n, a in arrays.items()}], core_ids=[0])
    return r.results[0]["out_0"]
```
